# Optimizing a Trainium2 kernel written in Bass

```python
import numpy as np
import jax
import jax.numpy as jnp

def _softmax(x, axis=-1):
    return jax.nn.softmax(x, axis=axis)

def _gelu(x):
    return jax.nn.gelu(x, approximate=True)

def _silu(x):
    return jax.nn.silu(x)

def _sigmoid(x):
    return jax.nn.sigmoid(x)

def _layernorm(x, axis=-1, eps=1e-05):
    m = jnp.mean(x, axis=axis, keepdims=True)
    v = jnp.var(x, axis=axis, keepdims=True)
    return (x - m) / jnp.sqrt(v + eps)

def _scatter_add(tgt, idx, src, axis=0):
    return tgt.at[idx].add(src)

def _segment_sum(src, seg, n):
    return jax.ops.segment_sum(src, seg, n)
kernel_name = 'mk_cond_resid_d4_seqx_r8_9d44f3'

def setup_inputs(seed: int=0):
    np.random.seed(seed)
    _w = jnp.asarray

    def _rec_inputs():
        import jax
        import jax.numpy as jnp
        _rk = jax.random.key(seed)
        x = 0.5 + 0.2887 * jax.random.normal(jax.random.fold_in(_rk, 1), (16, 128, 128), jnp.float32)
        _lenS = 128 - jax.random.randint(jax.random.fold_in(_rk, 7), (16,), 0, max(1, 128 // 4) + 1, jnp.int32)
        _lenS2 = 128 - jax.random.randint(jax.random.fold_in(_rk, 8), (16,), 0, max(1, 128 // 4) + 1, jnp.int32)
        condB_zX = jax.random.uniform(jax.random.fold_in(_rk, 11), (16,), jnp.float32, 0.0, 0.983423)
        condB_zY = jax.random.uniform(jax.random.fold_in(_rk, 12), (16,), jnp.float32, 0.0, 0.979075)
        condB_zR = jax.random.uniform(jax.random.fold_in(_rk, 13), (16,), jnp.float32, 0.0, 0.9968)
        fside_Bx8_0 = jax.random.uniform(jax.random.fold_in(_rk, 14), (16, 8), jnp.float32, 0.0, 0.556406)
        condB_sharedgateprob = jax.random.uniform(jax.random.fold_in(_rk, 15), (16,), jnp.float32, 0.0, 0.794948)
        itok_B_0_3 = jax.random.randint(jax.random.fold_in(_rk, 16), (16,), 0, 4, jnp.int32)
        fside_BxSxS_0 = 4.13588e-05 + 0.999923 * jax.random.normal(jax.random.fold_in(_rk, 17), (16, 128, 128), jnp.float32)
        itok_B_18_1004 = jax.random.randint(jax.random.fold_in(_rk, 18), (16,), 18, 1005, jnp.int32)
        return (x, condB_zX, condB_zY, condB_zR, fside_Bx8_0, condB_sharedgateprob, itok_B_0_3, fside_BxSxS_0, itok_B_18_1004)
    x, condB_zX, condB_zY, condB_zR, fside_Bx8_0, condB_sharedgateprob, itok_B_0_3, fside_BxSxS_0, itok_B_18_1004 = _rec_inputs()

    def _L0_cond_setup():
        import jax, jax.numpy as jnp
        import numpy as np
        key = jax.random.key(seed)
        k1, k2, k3, k4 = jax.random.split(key, 4)
        B, H, W = (64, 128, 128)
        return {'y': jax.random.uniform(k1, (B, H, W), dtype=jnp.float32), 'zX': jax.random.uniform(k2, (B, 1), dtype=jnp.float32), 'zY': jax.random.uniform(k3, (B, 1), dtype=jnp.float32), 'zR': jax.random.uniform(k4, (B, 1), dtype=jnp.float32), 'dx': 1, 'dy': 1}
    _L0_cond_all = _L0_cond_setup()
    _L0_cond_in = {k: v for k, v in _L0_cond_all.items() if k in ()}
    del _L0_cond_all

    def _L1_cond_setup():
        import jax, jax.numpy as jnp
        import numpy as np
        E, B, S, D, F = (8, 2, 128, 128, 512)
        key = jax.random.key(seed)
        ks = jax.random.split(key, 9)
        sc_d = 1.0 / np.sqrt(D)
        sc_f = 1.0 / np.sqrt(F)
        hidden_states = jax.random.normal(ks[0], (B, S, D), dtype=jnp.float32)
        gating_probs = jax.nn.softmax(jax.random.normal(ks[1], (B, E), dtype=jnp.float32), axis=-1)
        shared_gate_prob = jax.nn.sigmoid(jax.random.normal(ks[2], (B, 1), dtype=jnp.float32))
        Wg = jax.random.normal(ks[3], (E, D, F), dtype=jnp.float32) * sc_d
        Wu = jax.random.normal(ks[4], (E, D, F), dtype=jnp.float32) * sc_d
        Wd = jax.random.normal(ks[5], (E, F, D), dtype=jnp.float32) * sc_f
        Sg = jax.random.normal(ks[6], (D, F), dtype=jnp.float32) * sc_d
        Su = jax.random.normal(ks[7], (D, F), dtype=jnp.float32) * sc_d
        Sd = jax.random.normal(ks[8], (F, D), dtype=jnp.float32) * sc_f
        return {'hidden_states': hidden_states, 'gating_probs': gating_probs, 'shared_gate_prob': shared_gate_prob, 'Wg': Wg, 'Wu': Wu, 'Wd': Wd, 'Sg': Sg, 'Su': Su, 'Sd': Sd}
    _L1_cond_all = _L1_cond_setup()
    _L1_cond_in = {k: v for k, v in _L1_cond_all.items() if k in ('Wg', 'Wu', 'Wd', 'Sg', 'Su', 'Sd')}
    del _L1_cond_all

    def _L2_cond_setup():
        import jax, jax.numpy as jnp
        import numpy as np
        D = 128
        RANK = 16
        ALPHA = 16.0
        SCALING = ALPHA / RANK
        N_LANG = 4
        B, S = (32, 256)
        key = jax.random.key(seed)
        k1, k2, k3, k4, k5 = jax.random.split(key, 5)
        x = jax.random.normal(k1, (B, S, D), dtype=jnp.float32)
        language_ids = jax.random.randint(k2, (B,), 0, N_LANG, dtype=jnp.int32)
        lora_A = jax.random.normal(k3, (N_LANG, RANK, D), dtype=jnp.float32) * 0.02
        lora_B = jax.random.normal(k4, (N_LANG, D, RANK), dtype=jnp.float32) * 0.02
        lang_embed = jax.random.normal(k5, (N_LANG, D), dtype=jnp.float32) * 0.02
        return {'x': x, 'language_ids': language_ids, 'lora_A': lora_A, 'lora_B': lora_B, 'lang_embed': lang_embed}
    _L2_cond_all = _L2_cond_setup()
    _L2_cond_in = {k: v for k, v in _L2_cond_all.items() if k in ('lora_A', 'lora_B', 'lang_embed')}
    del _L2_cond_all

    def _L3_cond_setup():
        import jax, jax.numpy as jnp
        import numpy as np
        B, L1, L2, DIN, DOUT, H = (8, 128, 128, 128, 128, 16)
        DH = DOUT // H
        SCALE = 1.0 / np.sqrt(DH).astype(np.float32)
        key = jax.random.key(seed)
        ks = jax.random.split(key, 13)
        s = 0.02
        return {'seq1': jax.random.normal(ks[0], (B, L1, DIN), jnp.float32), 'seq2': jax.random.normal(ks[1], (B, L2, DIN), jnp.float32), 'seq_len1': jax.random.randint(ks[2], (B,), 1, L1 + 1, jnp.int32), 'Wq': jax.random.normal(ks[3], (DIN, DOUT), jnp.float32) * s, 'bq': jnp.zeros((DOUT,), jnp.float32), 'Wk': jax.random.normal(ks[4], (DIN, DOUT), jnp.float32) * s, 'bk': jnp.zeros((DOUT,), jnp.float32), 'Wv': jax.random.normal(ks[5], (DIN, DOUT), jnp.float32) * s, 'bv': jnp.zeros((DOUT,), jnp.float32), 'Wo': jax.random.normal(ks[6], (DOUT, DOUT), jnp.float32) * s, 'bo': jnp.zeros((DOUT,), jnp.float32), 'b_prev': jax.random.normal(ks[7], (1, 1, DIN), jnp.float32) * s, 'b_self': jax.random.normal(ks[8], (1, 1, DIN), jnp.float32) * s}
    _L3_cond_all = _L3_cond_setup()
    _L3_cond_in = {k: v for k, v in _L3_cond_all.items() if k in ('Wq', 'bq', 'Wk', 'bk', 'Wv', 'bv', 'Wo', 'bo', 'b_prev', 'b_self')}
    del _L3_cond_all
    return {'x': x, 'condB_zX': condB_zX, 'condB_zY': condB_zY, 'condB_zR': condB_zR, 'fside_Bx8_0': fside_Bx8_0, 'condB_sharedgateprob': condB_sharedgateprob, 'itok_B_0_3': itok_B_0_3, 'fside_BxSxS_0': fside_BxSxS_0, 'itok_B_18_1004': itok_B_18_1004, 'L1_cond_Wg': _L1_cond_in['Wg'], 'L1_cond_Wu': _L1_cond_in['Wu'], 'L1_cond_Wd': _L1_cond_in['Wd'], 'L1_cond_Sg': _L1_cond_in['Sg'], 'L1_cond_Su': _L1_cond_in['Su'], 'L1_cond_Sd': _L1_cond_in['Sd'], 'L2_cond_lora_A': _L2_cond_in['lora_A'], 'L2_cond_lora_B': _L2_cond_in['lora_B'], 'L2_cond_lang_embed': _L2_cond_in['lang_embed'], 'L3_cond_Wq': _L3_cond_in['Wq'], 'L3_cond_bq': _L3_cond_in['bq'], 'L3_cond_Wk': _L3_cond_in['Wk'], 'L3_cond_bk': _L3_cond_in['bk'], 'L3_cond_Wv': _L3_cond_in['Wv'], 'L3_cond_bv': _L3_cond_in['bv'], 'L3_cond_Wo': _L3_cond_in['Wo'], 'L3_cond_bo': _L3_cond_in['bo'], 'L3_cond_b_prev': _L3_cond_in['b_prev'], 'L3_cond_b_self': _L3_cond_in['b_self']}

def reference(x, condB_zX, condB_zY, condB_zR, fside_Bx8_0, condB_sharedgateprob, itok_B_0_3, fside_BxSxS_0, itok_B_18_1004, L1_cond_Wg, L1_cond_Wu, L1_cond_Wd, L1_cond_Sg, L1_cond_Su, L1_cond_Sd, L2_cond_lora_A, L2_cond_lora_B, L2_cond_lang_embed, L3_cond_Wq, L3_cond_bq, L3_cond_Wk, L3_cond_bk, L3_cond_Wv, L3_cond_bv, L3_cond_Wo, L3_cond_bo, L3_cond_b_prev, L3_cond_b_self):
    import jax
    import jax.numpy as jnp

    def _L0_cond_ref(y, zX, zY, zR, dx, dy):
        import jax, jax.numpy as jnp
        import numpy as np
        yp_x = jnp.pad(y, ((0, 0), (0, 0), (1, 1)), mode='reflect')
        lap_x = (yp_x[:, :, :-2] - 2.0 * y + yp_x[:, :, 2:]) / (dx * dx)
        yp_y = jnp.pad(y, ((0, 0), (1, 1), (0, 0)), mode='reflect')
        lap_y = (yp_y[:, :-2, :] - 2.0 * y + yp_y[:, 2:, :]) / (dy * dy)
        du_dt = zX[:, :, None] * lap_x + zY[:, :, None] * lap_y + zR[:, :, None] * y * (1.0 - y)
        return du_dt

    def _L1_cond_ref(hidden_states, gating_probs, shared_gate_prob, Wg, Wu, Wd, Sg, Su, Sd):
        import jax, jax.numpy as jnp
        import numpy as np
        E, B, S, D, F = (8, 2, 128, 128, 512)
        h = hidden_states
        g = jnp.einsum('bsd,edf->ebsf', h, Wg)
        u = jnp.einsum('bsd,edf->ebsf', h, Wu)
        expert_outs = jnp.einsum('ebsf,efd->ebsd', jax.nn.silu(g) * u, Wd)
        expert_output = jnp.einsum('be,ebsd->bsd', gating_probs, expert_outs)
        shared = jnp.einsum('bsf,fd->bsd', jax.nn.silu(h @ Sg) * (h @ Su), Sd)
        sg = shared_gate_prob[:, :, None]
        return (1.0 - sg) * expert_output + sg * shared

    def _L2_cond_ref(x, language_ids, lora_A, lora_B, lang_embed):
        import jax, jax.numpy as jnp
        import numpy as np
        D = 128
        RANK = 16
        ALPHA = 16.0
        SCALING = ALPHA / RANK
        N_LANG = 4
        B, S = (32, 256)
        A = lora_A[language_ids]
        Bm = lora_B[language_ids]
        emb = lang_embed[language_ids]
        t = jnp.einsum('bsd,brd->bsr', x, A)
        lora_out = jnp.einsum('bsr,bdr->bsd', t, Bm) * SCALING
        return lora_out + emb[:, None, :]

    def _L3_cond_ref(seq1, seq2, seq_len1, Wq, bq, Wk, bk, Wv, bv, Wo, bo, b_prev, b_self):
        import jax, jax.numpy as jnp
        import numpy as np
        B, L1, L2, DIN, DOUT, H = (8, 128, 128, 128, 128, 16)
        DH = DOUT // H
        SCALE = 1.0 / np.sqrt(DH).astype(np.float32)
        b, l1, _ = seq1.shape
        l2 = seq2.shape[1]
        query = seq2 + b_self
        key = jnp.concatenate([seq1 + b_prev, seq2 + b_self], 1)
        value = jnp.concatenate([seq1, seq2], 1)
        q = (query @ Wq + bq).reshape(b, l2, H, DH).transpose(0, 2, 1, 3)
        k = (key @ Wk + bk).reshape(b, l1 + l2, H, DH).transpose(0, 2, 1, 3)
        v = (value @ Wv + bv).reshape(b, l1 + l2, H, DH).transpose(0, 2, 1, 3)
        score_prev = jnp.einsum('bhqd,bhkd->bhqk', q, k[:, :, :l1]) * SCALE
        score_self = (q * k[:, :, l1:]).sum(-1, keepdims=True) * SCALE
        mask = jnp.arange(l1)[None, :] < seq_len1[:, None]
        score_prev = jnp.where(mask[:, None, None, :], score_prev, -jnp.inf)
        score = jnp.concatenate([score_prev, score_self], -1)
        weights = jax.nn.softmax(score, axis=-1)
        attn = jnp.einsum('bhqk,bhkd->bhqd', weights[..., :-1], v[:, :, :l1])
        attn = attn + weights[..., -1:] * v[:, :, l1:]
        attn = attn.transpose(0, 2, 1, 3).reshape(b, l2, H * DH)
        return attn @ Wo + bo
    x = x + _L0_cond_ref(x, condB_zX[:, None], condB_zY[:, None], condB_zR[:, None], 1, 1)
    x = x + _L1_cond_ref(x, fside_Bx8_0, condB_sharedgateprob[:, None], L1_cond_Wg, L1_cond_Wu, L1_cond_Wd, L1_cond_Sg, L1_cond_Su, L1_cond_Sd)
    x = x + _L2_cond_ref(x, itok_B_0_3, L2_cond_lora_A, L2_cond_lora_B, L2_cond_lang_embed)
    x = x + _L3_cond_ref(x, fside_BxSxS_0, itok_B_18_1004, L3_cond_Wq, L3_cond_bq, L3_cond_Wk, L3_cond_bk, L3_cond_Wv, L3_cond_bv, L3_cond_Wo, L3_cond_bo, L3_cond_b_prev, L3_cond_b_self)
    return x

_drawn_inputs = setup_inputs


def setup_inputs(seed=0):
    import zlib

    import numpy as np

    out = dict(_drawn_inputs(seed))
    spreads = {'L3_cond_bq': (0.0, 0.8),
     'L3_cond_bk': (0.0, 0.8),
     'L3_cond_bv': (0.0, 0.286),
     'L3_cond_bo': (0.0, 0.1)}
    factors = {'fside_BxSxS_0': 8.0,
     'L2_cond_lora_A': 3.181,
     'L2_cond_lora_B': 3.335,
     'L3_cond_Wq': 8.0,
     'L3_cond_Wk': 8.0,
     'L3_cond_b_prev': 8.0,
     'L3_cond_b_self': 8.0}
    for name, (base, spread) in spreads.items():
        noise = np.random.default_rng([zlib.crc32(name.encode()), seed]).standard_normal(out[name].shape)
        drawn = base * np.exp(spread * noise) if base else spread * noise
        out[name] = jnp.asarray(drawn.astype(out[name].dtype))
    for name, factor in factors.items():
        out[name] = (out[name] * factor).astype(out[name].dtype)
    return out
```

```python
from contextlib import ExitStack

import numpy as np
import concourse.bass as bass
from concourse import mybir

F32 = mybir.dt.float32
F32R = mybir.dt.float32r
I32 = mybir.dt.int32
ACT = mybir.ActivationFunctionType
ALU = mybir.AluOpType
AX_X = mybir.AxisListType.X

B, S, D = 16, 128, 128
E, F = 8, 512
NE = E + 1
FC = F // 128
SLOTS = NE * FC
TB = 4
NT = B // TB
N = TB * S
H, DH = 16, 8
SCALE = float(np.float32(1.0) / np.sqrt(DH).astype(np.float32))
LANGS, RANK = 4, 16
NEG = -1.0e30

GI, GJ = 4, 4
ROW_MASK = 3 * DH
ROW_MAX_HI, ROW_MAX_LO = ROW_MASK + 1, ROW_MASK + 2
VW = DH + 1

FIRST_AUX = []
for _f in range(NT):
    if _f == 1:
        FIRST_AUX.append(("setup", 0, 0))
    if _f:
        FIRST_AUX.append(("diffuse", _f, 0))
    FIRST_AUX += [("side", _f, 0), ("query", _f, 0)] + [("natural", _f, b) for b in range(TB)]
FIRST_AUX_SLOT = 5
N_FIRST = 1 + len(FIRST_AUX)
LATER_AUX = ["lora_a", "lora_b", "key", "value", "x_natural"]
LATER_SLOT = {3: 0, 5: 1, 9: 2, 11: 3, 13: 4}


def build(nc, a, out):
    with ExitStack() as ctx:
        def sb(name, shape, dt=F32):
            return ctx.enter_context(nc.sbuf_tensor(name, shape, dt))

        def sem(name):
            return ctx.enter_context(nc.semaphore(name))

        def dram(name, shape):
            return nc.dram_tensor(name, shape, F32, kind="Internal").ap()

        q_rows = dram("q_rows", (GI, 4, DH, GJ, B * S))
        k_rows = dram("k_rows", (GI, 4, DH, GJ, B * S))
        mask_row = dram("mask_row", (B, S))
        v_prev_d = dram("v_prev_d", (B, S, H * VW))
        v_self_d = dram("v_self_d", (B, S, D))
        x3_d = dram("x3_d", (B, S, D))

        ident = sb("ident", [128, 128])
        lap_t = sb("lap_t", [128, 128])
        z_all = sb("z_all", [128, 3, B])
        probs_b = sb("probs_b", [128, B * E])
        shared_b = sb("shared_b", [128, B])
        one_minus = sb("one_minus", [128, B])
        gates = sb("gates", [128, NE, B])
        w_raw4 = sb("w_raw4", [128, 4, D])
        w_qkv_h = sb("w_qkv_h", [128, 3, D], F32R)
        w_qkv_l = sb("w_qkv_l", [128, 3, D], F32R)
        bias_nat = sb("bias_nat", [128, 3, D])
        bo_b = sb("bo_b", [128, D])
        cols = sb("cols", [128, 4])
        lora_a_nat = sb("lora_a_nat", [64, D])
        lora_b_nat = sb("lora_b_nat", [128, LANGS, RANK])
        lora_a_t = sb("lora_a_t", [128, 64])
        lora_b_t = sb("lora_b_t", [64, D])
        embed = sb("embed", [LANGS, D])
        lang_i = sb("lang_i", [64, B], I32)
        lang_f = sb("lang_f", [64, B])
        lang_of = sb("lang_of", [64, 2])
        lang_sel = sb("lang_sel", [64, B])
        lang_one = sb("lang_one", [LANGS, B])
        len_i = sb("len_i", [B, 1], I32)
        len_f = sb("len_f", [B, 1])
        key_pos = sb("key_pos", [B, S])
        mask_sb = sb("mask_sb", [B, S])
        self_score = sb("self_score", [128, B, H])

        w_raw = [sb(f"w_raw{n}", [128, F]) for n in range(3)]
        x1 = sb("x1", [128, NT, TB, S])
        x1_hi = sb("x1_hi", [128, NT, N], F32R)
        x1_lo = sb("x1_lo", [128, NT, N], F32R)
        act_p = [sb(f"act_p{n}", [128, N]) for n in range(2)]
        act_hi = [sb(f"act_hi{n}", [128, N], F32R) for n in range(3)]
        act_lo = [sb(f"act_lo{n}", [128, N], F32R) for n in range(3)]
        xg = sb("xg", [128, TB, S])
        xg_hi = [sb(f"xg_hi{n}", [128, N], F32R) for n in range(3)]
        xg_lo = [sb(f"xg_lo{n}", [128, N], F32R) for n in range(3)]
        x_in = sb("x_in", [128, TB, D])
        side_in = sb("side_in", [128, TB, D])
        lap_zy = sb("lap_zy", [128, TB, S])
        dif_a = sb("dif_a", [128, TB, D])
        dif_b = sb("dif_b", [128, TB, D])
        in_a_hi = sb("in_a_hi", [128, N], F32R)
        in_a_lo = sb("in_a_lo", [128, N], F32R)
        in_b_hi = sb("in_b_hi", [128, N], F32R)
        in_b_lo = sb("in_b_lo", [128, N], F32R)
        rows_hi = sb("rows_hi", [128, N], F32R)
        rows_lo = sb("rows_lo", [128, N], F32R)
        stage = sb("stage", [128, 2 * 3 * D])
        nat = [stage[:, n * 3 * D:(n + 1) * 3 * D].rearrange("p (k d) -> p k d", k=3) for n in range(2)]
        qk_prod = [sb(f"qk_prod{n}", [128, D]) for n in range(2)]
        x3_t = side_in
        x3_stage = lap_zy
        low_sel = dif_a[0:64]
        one_sel = dif_b[0:LANGS]
        w_perm = stage[:, 0:2 * D].rearrange("p (k d) -> p k d", k=2)
        b_perm = stage[:, 2 * D:4 * D].rearrange("p (k d) -> p k d", k=2)
        v_stage = stage[:, 0:TB * H * VW].rearrange("p (b h w) -> p b h w", b=TB, h=H)

        phase1 = ExitStack()

        def sb1(name, shape, dt=F32):
            return phase1.enter_context(nc.sbuf_tensor(name, shape, dt))

        w_hi = sb1("w_hi", [128, NE, 3, F], F32R)
        w_lo = sb1("w_lo", [128, NE, 3, F], F32R)
        phase1.close()
        phase2 = ExitStack()

        def sb2(name, shape, dt=F32):
            return phase2.enter_context(nc.sbuf_tensor(name, shape, dt))

        qs = [sb2(f"qs{n}", [128, GJ, S], F32R) for n in range(4)]
        ks = [sb2(f"ks{n}", [128, GJ, S], F32R) for n in range(4)]
        qs_max = [sb2(f"qs_max{n}", [128, GJ, S], F32R) for n in range(2)]
        max_rows = [sb2(f"max_rows{n}", [128, GJ, S]) for n in range(2)]
        max_pad = [sb2(f"max_pad{n}", [128, GJ, S]) for n in range(2)]
        max_key = [sb2(f"max_key{n}", [128, GI, GJ]) for n in range(2)]
        max_all = [sb2(f"max_all{n}", [128, GI, GJ]) for n in range(2)]
        self_arg = [sb2(f"self_arg{n}", [128, H]) for n in range(2)]
        self_exp = [sb2(f"self_exp{n}", [128, H]) for n in range(4)]
        probs_t = [sb2(f"probs_t{n}", [128, GJ, S]) for n in range(4)]
        v_prev = [sb2(f"v_prev{n}", [128, H, VW]) for n in range(4)]
        v_self = [sb2(f"v_self{n}", [128, H, DH]) for n in range(4)]
        x3_nat = [sb2(f"x3_nat{n}", [128, D]) for n in range(4)]
        v_self_w = [sb2(f"v_self_w{n}", [128, H, DH]) for n in range(2)]
        denom = [sb2(f"denom{n}", [128, H]) for n in range(2)]
        rdenom = [sb2(f"rdenom{n}", [128, H]) for n in range(2)]
        numer = [sb2(f"numer{n}", [128, H, DH]) for n in range(2)]
        attn = [sb2(f"attn{n}", [128, H, DH]) for n in range(2)]
        attn_t = [sb2(f"attn_t{n}", [128, D]) for n in range(2)]
        ctx.enter_context(phase2)
        def bank(name):
            return nc.psum_tensor(name, [128, 512], F32)

        phase1p = ExitStack()
        g_ps = [phase1p.enter_context(bank(f"g_ps{n}")) for n in range(3)]
        u_ps = [phase1p.enter_context(bank(f"u_ps{n}")) for n in range(3)]
        acc_ps = phase1p.enter_context(bank("acc_ps"))
        aux_ps = phase1p.enter_context(bank("aux_ps"))
        phase1p.close()
        s_ps = [ctx.enter_context(bank(f"s_ps{n}")) for n in range(2)]
        st_ps = [ctx.enter_context(bank(f"st_ps{n}")) for n in range(2)]
        pv_ps = [ctx.enter_context(bank(f"pv_ps{n}")) for n in range(2)]
        out_ps = ctx.enter_context(bank("out_ps"))
        max_ps = ctx.enter_context(bank("max_ps"))

        diff_loaded = sem("diff_loaded")
        small_loaded = sem("small_loaded")
        x_loaded = sem("x_loaded")
        side_loaded = sem("side_loaded")
        w_loaded = [sem(f"w_loaded{n}") for n in range(3)]
        w_hi_done, w_lo_done = sem("w_hi_done"), sem("w_lo_done")
        gate_loaded, gates_ready = sem("gate_loaded"), sem("gates_ready")
        self_summed = sem("self_summed")
        proj_lo = sem("proj_lo")
        ones_set = sem("ones_set")
        proj_hi, proj_ready = sem("proj_hi"), sem("proj_ready")
        mask_ready = sem("mask_ready")
        mask_stored = sem("mask_stored")
        const_rows_stored = sem("const_rows_stored")
        dve_step = sem("dve_step")
        lap_ready = sem("lap_ready")
        dif_ready = sem("dif_ready")
        aux_written, aux_rounded, aux_drained = sem("aux_written"), sem("aux_rounded"), sem("aux_drained")
        prod_made = sem("prod_made")
        rows_stored = sem("rows_stored")
        self_stored = [sem(f"self_stored{n}") for n in range(2)]
        later_stored = sem("later_stored")
        xg_made, xg_rounded, xg_ready = sem("xg_made"), sem("xg_rounded"), sem("xg_ready")
        g_written, u_written = sem("g_written"), sem("u_written")
        silu_done, prod_done = sem("silu_done"), sem("prod_done")
        act_hi_done, act_lo_done = sem("act_hi_done"), sem("act_lo_done")
        down_done = sem("down_done")
        acc_written, acc_drained = sem("acc_written"), sem("acc_drained")
        x3_ready = sem("x3_ready")
        in_rounded, in_lo_ready, in_a_ready = sem("in_rounded"), sem("in_lo_ready"), sem("in_a_ready")
        one_sel_ready = sem("one_sel_ready")

        pad_zeroed = sem("pad_zeroed")
        qk_loaded = [sem(f"qk_loaded{n}") for n in range(4)]
        vx_loaded = [sem(f"vx_loaded{n}") for n in range(4)]
        s_written, max_done = sem("s_written"), sem("max_done")
        max_split = sem("max_split")
        max_turned, max_copied = sem("max_turned"), sem("max_copied")
        qs_max_ready = sem("qs_max_ready")
        st_written, exp_done = sem("st_written"), sem("exp_done")
        pv_written = sem("pv_written")
        self_exp_done = sem("self_exp_done")
        self_weighted = sem("self_weighted")
        attn_done = sem("attn_done")
        attn_turned, attn_copied = sem("attn_turned"), sem("attn_copied")
        out_written, out_ready = sem("out_written"), sem("out_ready")
        out_stored = [sem(f"out_stored{n}") for n in range(4)]
        small_step, norm_step = sem("small_step"), sem("norm_step")
        self_arg_ready = sem("self_arg_ready")
        bias_scaled = sem("bias_scaled")

        N_DIFF = 5
        N_SMALL = 17

        def vec(ap, p):
            return ap.unsqueeze(0).to_broadcast([p, ap.shape[0]])

        def part_src(w):
            e, k = divmod(w, 3)
            src = (a["L1_cond_" + "W" + "gud"[k]][e] if e < E else a["L1_cond_" + "S" + "gud"[k]])
            return src.rearrange("(c p) d -> p c d", p=128) if k == 2 else src

        def part_raw(w):
            t = w_raw[w % 3][:]
            return t.rearrange("p (c d) -> p c d", c=FC) if w % 3 == 2 else t

        def blockwise(t):
            return t.rearrange("b s d -> s b d")

        def aux_of(kind, f, b=0):
            return 0 if (kind, f) == ("diffuse", 0) else 1 + FIRST_AUX.index((kind, f, b))

        def first_at(k):
            n = k - FIRST_AUX_SLOT
            return [FIRST_AUX[n]] if 0 <= n < len(FIRST_AUX) else []

        def slot_of(kind, f):
            return FIRST_AUX_SLOT + FIRST_AUX.index((kind, f, 0))

        def rounded_of(kind, f):
            kinds = [("diffuse", 0, 0)] + FIRST_AUX
            return sum(s[0] in ("diffuse", "side", "query") for s in kinds[:aux_of(kind, f) + 1])

        N_ROUNDED = rounded_of("query", NT - 1)

        def perm(t):
            return t.rearrange("p (i j r) -> p i r j", i=GI, j=GJ)

        def as_perm(t):
            return t.rearrange("p (i r j) -> p i r j", i=GI, j=GJ)

        def loaded(b, n, dmas):
            return (b - n) * (4 * dmas) + 16 * dmas * (n // 4 + 1)

        def wait(eng, semaphore, value):
            if not isinstance(value, int) or value > 0:
                eng.wait_ge(semaphore, value)

        block = ctx.enter_context(nc.Block())

        @block.sync
        def _(sp):
            def load_part(w):
                if w >= 3:
                    sp.wait_ge(w_lo_done, w - 2)
                sp.dma_start(part_raw(w), part_src(w)).then_inc(w_loaded[w % 3], 16)

            def load_x(f):
                if f:
                    sp.wait_ge(aux_written, aux_of("diffuse", f - 1) + 1)
                sp.dma_start(x_in[:], blockwise(a["x"][TB * f:TB * f + TB])).then_inc(x_loaded, 16)

            def load_side(f):
                if f:
                    sp.wait_ge(aux_written, aux_of("side", f - 1) + 1)
                sp.dma_start(side_in[:], blockwise(a["fside_BxSxS_0"][TB * f:TB * f + TB])).then_inc(side_loaded, 16)

            def store_rows(dst, tok, slots_hi, slot_lo):
                for s in slots_hi:
                    sp.dma_start(dst[:, s, :, :, tok].rearrange("i r j n -> i (r j) n"),
                                 rows_hi[:].bitcast(F32)).then_inc(rows_stored, 16)
                sp.dma_start(dst[:, slot_lo, :, :, tok].rearrange("i r j n -> i (r j) n"),
                             rows_lo[:].bitcast(F32)).then_inc(rows_stored, 16)

            def later_stores(t, n):
                sp.wait_ge(aux_drained, n + 3)
                store_rows(k_rows, bass.ds(t * N, N), (0, 1), 2)
                sp.wait_ge(aux_drained, n + 4)
                sp.dma_start(blockwise(v_prev_d[bass.ds(t * TB, TB)]),
                             v_stage.rearrange("p b h w -> p b (h w)")).then_inc(later_stored, 16)
                sp.wait_ge(aux_drained, n + 5)
                sp.dma_start(blockwise(x3_d[bass.ds(t * TB, TB)]), x3_stage[:]).then_inc(later_stored, 16)

            load_x(0)
            for w in range(3):
                load_part(w)
            load_side(0)
            sp.dma_start(q_rows[:, 3, 0], a["ones_row"].to_broadcast([GI, GJ, B * S])).then_inc(const_rows_stored, 16)
            sp.dma_start(q_rows[:, 3, 1:].rearrange("i r j n -> i (r j) n"),
                         a["zeros_row"].to_broadcast([GI, (DH - 1) * GJ, B * S])).then_inc(const_rows_stored, 16)
            sp.dma_start(k_rows[:, 3, 1:3].rearrange("i r j n -> i (r j) n"),
                         a["ones_row"].to_broadcast([GI, 2 * GJ, B * S])).then_inc(const_rows_stored, 16)
            sp.dma_start(k_rows[:, 3, 3:].rearrange("i r j n -> i (r j) n"),
                         a["zeros_row"].to_broadcast([GI, (DH - 3) * GJ, B * S])).then_inc(const_rows_stored, 16)
            load_x(1)
            for k in range(SLOTS):
                e, c = divmod(k, FC)
                if e + 1 < NE and c < 3:
                    load_part(3 * (e + 1) + c)
                for step in first_at(k - 1):
                    kind, f, b = step
                    n = aux_of(*step)
                    if kind == "diffuse" and f + 1 < NT:
                        load_x(f + 1)
                    if kind == "query":
                        sp.wait_ge(aux_drained, n + 1)
                        store_rows(q_rows, bass.ds(f * N, N), (0, 2), 1)
                        if f + 1 < NT:
                            load_side(f + 1)
                    if kind == "natural":
                        sp.wait_ge(aux_drained, n + 1)
                        sp.dma_start(v_self_d[TB * f + b], nat[b % 2][:, 2]).then_inc(self_stored[b % 2], 16)
                if k == FIRST_AUX_SLOT:
                    sp.wait_ge(mask_ready, 1)
                    sp.dma_start(mask_row, mask_sb[:]).then_inc(mask_stored, 16)
            sp.wait_ge(mask_stored, 16)
            sp.dma_start(k_rows[:, 3, 0], mask_row.rearrange("b s -> (b s)").unsqueeze(0).unsqueeze(0)
                         .to_broadcast([GI, GJ, B * S])).then_inc(later_stored, 16)
            with sp.Fori(1, NT) as t:
                later_stores(t - 1, (t - 1) * len(LATER_AUX) + N_FIRST)
            later_stores(NT - 1, (NT - 1) * len(LATER_AUX) + N_FIRST)

            sp.wait_ge(rows_stored, 16 * 3 * 2 * NT)
            sp.wait_ge(const_rows_stored, 16 * 4)
            for stored in self_stored:
                sp.wait_ge(stored, 16 * B // 2)
            sp.wait_ge(later_stored, 16 * (1 + 2 * NT))
            sp.wait_ge(down_done, SLOTS * NT)

            def load_qk(b, n):
                tok = bass.ds(b * S, S)
                sp.dma_start(qs[n][:].bitcast(F32), q_rows[:, :, :, :, tok].rearrange("i s r j n -> (i s r) j n"))\
                    .then_inc(qk_loaded[n], 16)
                sp.dma_start(ks[n][:].bitcast(F32), k_rows[:, :, :, :, tok].rearrange("i s r j n -> (i s r) j n"))\
                    .then_inc(qk_loaded[n], 16)

            def load_vx(b, n):
                sp.dma_start(v_prev[n][:].rearrange("p h w -> p (h w)"), v_prev_d[b]).then_inc(vx_loaded[n], 16)
                sp.dma_start(v_self[n][:].rearrange("p h w -> p (h w)"), v_self_d[b]).then_inc(vx_loaded[n], 16)
                sp.dma_start(x3_nat[n][:], x3_d[b]).then_inc(vx_loaded[n], 16)

            for n in range(TB):
                load_qk(n, n)
                load_vx(n, n)

            def store_out(b, n):
                sp.wait_ge(out_ready, b + 1)
                sp.dma_start(out[b], x3_nat[n % 4][:]).then_inc(out_stored[n % 4], 16)

            with sp.Fori(0, B // TB - 1) as g:
                for n in range(TB):
                    b = g * TB + n
                    sp.wait_ge(st_written, b * GI + GI)
                    load_qk(b + TB, n)
                    store_out(b, n)
                    sp.wait_ge(out_stored[n], g * 16 + 16)
                    load_vx(b + TB, n)
            for b in range(B - TB, B):
                store_out(b, b)
            for stored in out_stored:
                sp.wait_ge(stored, 16 * B // 4)


        @block.tensor
        def _(pe):
            mm, turn = nc.tensor.matmul, nc.tensor.transpose

            def three(dst, w_h, w_l, x_h, x_l, start=True, stop=True):
                mm(dst, w_h, x_h, start=start, stop=False)
                mm(dst, w_l, x_h, start=False, stop=False)
                return mm(dst, w_h, x_l, start=False, stop=stop)

            def diffuse(f):
                pe.wait_ge(dif_ready, f + 1)
                pe.wait_ge(lap_ready, f + 1)
                for b in range(TB):
                    dst = aux_ps[:, b * S:(b + 1) * S]
                    mm(dst, dif_a[:, b], ident[:], start=True, stop=False)
                    last = mm(dst, x_in[:, b], lap_zy[:, b], start=False, stop=True)
                last.then_inc(aux_written, 1)

            def first_step(kind, f, b):
                n = aux_of(kind, f, b)
                pe.wait_ge(aux_drained, n)
                if kind == "diffuse":
                    diffuse(f)
                elif kind == "setup":
                    turn(aux_ps[:, 0:64], lora_a_nat[:], ident[0:64, 0:64])
                    turn(aux_ps[0:64, 128:256], lora_b_nat[:].rearrange("p l r -> p (l r)"), ident[:])\
                        .then_inc(aux_written, 1)
                elif kind == "side":
                    pe.wait_ge(side_loaded, 16 * (f + 1))
                    for c in range(TB):
                        last = turn(aux_ps[:, c * S:(c + 1) * S], side_in[:, c], ident[:])
                    last.then_inc(aux_written, 1)
                elif kind == "query":
                    if f == 0:
                        pe.wait_ge(proj_ready, 3)
                    three(aux_ps[:], w_qkv_h[:, 0], w_qkv_l[:, 0], in_b_hi[:], in_b_lo[:]).then_inc(aux_written, 1)
                else:
                    tok = slice(b * S, (b + 1) * S)
                    qk_h, qk_l = w_qkv_h[:, 0:2].rearrange("p k d -> p (k d)"), w_qkv_l[:, 0:2].rearrange("p k d -> p (k d)")
                    three(aux_ps[:, 0:2 * D], in_b_hi[:, tok], in_b_lo[:, tok], qk_h, qk_l)
                    three(aux_ps[:, 2 * D:3 * D], in_a_hi[:, tok], in_a_lo[:, tok], w_qkv_h[:, 2], w_qkv_l[:, 2])\
                        .then_inc(aux_written, 1)

            def later_step(m, t):
                pe.wait_ge(aux_drained, t * len(LATER_AUX) + N_FIRST + m)
                kind = LATER_AUX[m]
                if kind == "lora_a":
                    pe.wait_ge(acc_drained, t + 1)
                    last = mm(aux_ps[0:64, :], lora_a_t[:], x1[:, t].rearrange("p b s -> p (b s)"), start=True, stop=True)
                elif kind == "lora_b":
                    mm(aux_ps[:], lora_b_t[:], low_sel.rearrange("p b s -> p (b s)"), start=True, stop=False)
                    last = mm(aux_ps[:], embed[:], one_sel.rearrange("p b s -> p (b s)"), start=False, stop=True)
                elif kind == "key":
                    pe.wait_ge(in_lo_ready, t + 1)
                    last = three(aux_ps[:], w_qkv_h[:, 1], w_qkv_l[:, 1], in_b_hi[:], in_b_lo[:])
                elif kind == "value":
                    pe.wait_ge(in_a_ready, t + 1)
                    for b in range(TB):
                        tok = slice(b * S, (b + 1) * S)
                        last = three(aux_ps[:, tok], in_a_hi[:, tok], in_a_lo[:, tok], w_qkv_h[:, 2], w_qkv_l[:, 2])
                else:
                    for b in range(TB):
                        last = turn(aux_ps[:, b * S:(b + 1) * S], x3_t[:, b], ident[:])
                last.then_inc(aux_written, 1)

            def gate_product(t, k):
                e, c = divmod(k, FC)
                chunk = slice(c * 128, (c + 1) * 128)
                if isinstance(t, int) and c == 0:
                    pe.wait_ge(w_lo_done, 3 * e + 1)
                wait(pe, silu_done, t * SLOTS + k - 2)
                three(g_ps[k % 3][:], w_hi[:, e, 0, chunk], w_lo[:, e, 0, chunk], x1_hi[:, t], x1_lo[:, t])\
                    .then_inc(g_written, 1)

            def up_product(t, k):
                e, c = divmod(k, FC)
                chunk = slice(c * 128, (c + 1) * 128)
                if c == 0:
                    if isinstance(t, int):
                        pe.wait_ge(w_lo_done, 3 * e + 2)
                    pe.wait_ge(xg_ready, t * NE + e + 1)
                wait(pe, prod_done, t * SLOTS + k - 2)
                three(u_ps[k % 3][:], w_hi[:, e, 1, chunk], w_lo[:, e, 1, chunk], xg_hi[e % 3][:], xg_lo[e % 3][:])\
                    .then_inc(u_written, 1)

            def down_product(t, k):
                e, c = divmod(k, FC)
                chunk = slice(c * 128, (c + 1) * 128)
                if isinstance(t, int) and t == 0 and c == 0:
                    pe.wait_ge(w_lo_done, 3 * e + 3)
                if k == 0:
                    wait(pe, acc_drained, t)
                pe.wait_ge(act_lo_done, t * SLOTS + k + 1)
                last = three(acc_ps[:], w_hi[:, e, 2, chunk], w_lo[:, e, 2, chunk], act_hi[k % 3][:], act_lo[k % 3][:],
                             start=(k == 0), stop=(k == SLOTS - 1))
                last.then_inc(down_done, 1)

            pe.wait_ge(diff_loaded, 16 * N_DIFF)
            diffuse(0)
            pe.wait_ge(aux_drained, 1)
            for k in range(SLOTS):
                gate_product(0, k)
                up_product(0, k)
                if k == FIRST_AUX_SLOT - 1:
                    pe.wait_ge(small_loaded, 16 * N_SMALL)
                for step in first_at(k):
                    first_step(*step)
                if k >= 2:
                    down_product(0, k - 2)
            with pe.Fori(1, NT) as t:
                for k in range(SLOTS):
                    gate_product(t, k)
                    if k < 2:
                        down_product(t - 1, SLOTS - 2 + k)
                    up_product(t, k)
                    if k in LATER_SLOT:
                        later_step(LATER_SLOT[k], t - 1)
                    if k >= 2:
                        down_product(t, k - 2)
            down_product(NT - 1, SLOTS - 2)
            down_product(NT - 1, SLOTS - 1)
            for m in range(len(LATER_AUX)):
                later_step(m, NT - 1)

            def rows(i):
                return slice(32 * i, 32 * i + 32)

            def scores(b, n, i):
                if i == 0:
                    pe.wait_ge(qk_loaded[n % 4], loaded(b, n, 2))
                wait(pe, max_done, b * GI + i - 1)
                for j in range(GJ):
                    last = mm(s_ps[i % 2][:, j * S:(j + 1) * S], qs[n % 4][rows(i), j], ks[n % 4][rows(i), j],
                              start=True, stop=True)
                last.then_inc(s_written, 1)

            def turn_max(b, n):
                pe.wait_ge(max_split, b + 1)
                wait(pe, max_copied, b)
                for j in range(GJ):
                    last = turn(max_ps[:, j * S:(j + 1) * S], max_pad[n % 2][:, j], ident[:])
                last.then_inc(max_turned, 1)

            def scores_t(b, n, i):
                if i == 0:
                    pe.wait_ge(qs_max_ready, b + 1)
                wait(pe, exp_done, b * GI + i - 1)
                for j in range(GJ):
                    last = mm(st_ps[i % 2][:, j * S:(j + 1) * S], ks[n % 4][rows(i), j], qs_max[n % 2][rows(i), j],
                              start=True, stop=True)
                last.then_inc(st_written, 1)

            def weigh(b, n, i):
                if i == 0:
                    pe.wait_ge(vx_loaded[n % 4], loaded(b, n, 3))
                pe.wait_ge(exp_done, b * GI + i + 1)
                for j in range(GJ):
                    h = GJ * i + j
                    last = mm(pv_ps[n % 2][:, h * VW:(h + 1) * VW], probs_t[i][:, j], v_prev[n % 4][:, h],
                              start=True, stop=True)
                last.then_inc(pv_written, 1)

            def turn_attn(b, n):
                pe.wait_ge(attn_done, b + 1)
                wait(pe, out_ready, b)
                turn(out_ps[:, 0:D], attn[n % 2][:].rearrange("p h r -> p (h r)"), ident[:]).then_inc(attn_turned, 1)

            def project(b, n):
                pe.wait_ge(attn_copied, b + 1)
                mm(out_ps[:, D:2 * D], attn_t[n % 2][:], w_raw4[:, 3], start=True, stop=True).then_inc(out_written, 1)

            def body(b, n, first=False, s_next=True, turn_next=True):
                if turn_next:
                    turn_max(b + 1, n + 1)
                for i in range(GI):
                    if s_next:
                        scores(b + 2, n + 2, i)
                    if not first and i == 0:
                        weigh(b - 1, n - 1, GI - 1)
                    scores_t(b, n, i)
                    if i:
                        weigh(b, n, i - 1)
                    if not first and i == 2:
                        turn_attn(b - 1, n - 1)
                    if not first and i == 3:
                        project(b - 1, n - 1)

            for b in range(2):
                for i in range(GI):
                    scores(b, b, i)
            turn_max(0, 0)
            body(0, 0, first=True)
            with pe.Fori(0, B // TB - 1) as g:
                for n in range(1, TB + 1):
                    body(g * TB + n, n)
            for b in range(B - TB + 1, B):
                body(b, b % TB, s_next=b + 2 < B, turn_next=b + 1 < B)
            weigh(B - 1, B - 1, GI - 1)
            turn_attn(B - 1, B - 1)
            project(B - 1, B - 1)

        @block.scalar
        def _(act):
            activation = nc.scalar.activation

            def small(dst, src, semaphore=small_loaded):
                act.dma_start(dst, src).then_inc(semaphore, 16)

            for n, z in enumerate(("condB_zX", "condB_zY", "condB_zR")):
                small(z_all[:, n], vec(a[z], 128), diff_loaded)
            small(lap_t[:], a["lap_t"], diff_loaded)
            small(ident[:], a["ident"], diff_loaded)
            small(probs_b[:], a["fside_Bx8_0"].rearrange("b e -> (b e)").unsqueeze(0).to_broadcast([128, B * E]), gate_loaded)
            small(shared_b[:], vec(a["condB_sharedgateprob"], 128), gate_loaded)

            def split_part(w):
                act.wait_ge(w_loaded[w % 3], 16 * (w // 3 + 1))
                activation(w_hi[:, w // 3, w % 3], w_raw[w % 3][:], ACT.Identity).then_inc(w_hi_done, 1)

            def first_step(kind, f, b):
                n = aux_of(kind, f, b)
                if kind in ("natural", "setup"):
                    return
                act.wait_ge(aux_written, n + 1)
                if kind == "diffuse":
                    activation(x1_hi[:, f], aux_ps[:], ACT.Identity)
                    activation(x1[:, f].rearrange("p b s -> p (b s)"), aux_ps[:], ACT.Identity).then_inc(aux_rounded, 1)
                elif kind == "side":
                    activation(in_a_hi[:], aux_ps[:], ACT.Identity)
                    activation(in_b_hi[:], aux_ps[:], ACT.Identity, bias=cols[:, 2:3]).then_inc(aux_rounded, 1)
                else:
                    wait(act, rows_stored, 48 * f)
                    activation(rows_hi[:], aux_ps[:], ACT.Identity, bias=cols[:, 0:1]).then_inc(aux_rounded, 1)

            def later_step(m, t):
                n = t * len(LATER_AUX) + N_FIRST + m
                if LATER_AUX[m] == "lora_b":
                    act.wait_ge(aux_drained, n + 1)
                    activation(in_b_hi[:], x3_t[:].rearrange("p b s -> p (b s)"), ACT.Identity, bias=cols[:, 3:4])
                    activation(in_a_hi[:], x3_t[:].rearrange("p b s -> p (b s)"), ACT.Identity).then_inc(in_rounded, 1)
                elif LATER_AUX[m] == "key":
                    act.wait_ge(aux_written, n + 1)
                    act.wait_ge(rows_stored, t * 48 + 48 * NT)
                    activation(rows_hi[:], aux_ps[:], ACT.Identity, bias=cols[:, 1:2]).then_inc(aux_rounded, 1)

            def silu(t, k):
                wait(act, act_lo_done, t * SLOTS + k - 1)
                act.wait_ge(g_written, t * SLOTS + k + 1)
                activation(act_p[k % 2][:], g_ps[k % 3][:], ACT.Silu).then_inc(silu_done, 1)

            def round_act(t, k):
                wait(act, down_done, t * SLOTS + k - 2)
                act.wait_ge(prod_done, t * SLOTS + k + 1)
                activation(act_hi[k % 3][:], act_p[k % 2][:], ACT.Identity).then_inc(act_hi_done, 1)

            def round_xg(t, e):
                wait(act, u_written, t * SLOTS + (e - 3) * FC + FC)
                act.wait_ge(xg_made, t * NE + e + 1)
                activation(xg_hi[e % 3][:], xg[:].rearrange("p b s -> p (b s)"), ACT.Identity).then_inc(xg_rounded, 1)

            split_part(0)
            split_part(1)
            first_step("diffuse", 0, 0)
            round_xg(0, 0)
            split_part(2)

            for n, w in enumerate("qkvo"):
                small(w_raw4[:, n], a["L3_cond_W" + w])
            for n, v in enumerate(("bq", "bk", "bv")):
                small(bias_nat[:, n], vec(a["L3_cond_" + v], 128))
            small(bo_b[:], vec(a["L3_cond_bo"], 128))
            small(cols[:, 2:3], a["L3_cond_b_self"].rearrange("a b d -> d (a b)"))
            small(cols[:, 3:4], a["L3_cond_b_prev"].rearrange("a b d -> d (a b)"))
            small(lora_a_nat[:], a["L2_cond_lora_A"].rearrange("l r d -> (l r) d"))
            small(lora_b_nat[:], a["L2_cond_lora_B"].rearrange("l d r -> d l r"))
            small(embed[:], a["L2_cond_lang_embed"])
            small(lang_i[:], vec(a["itok_B_0_3"], 64))
            small(lang_of[:], a["lang_of"])
            small(len_i[:], a["itok_B_18_1004"].unsqueeze(1))
            small(key_pos[:], a["key_pos"])

            def round_projections():
                act.wait_ge(small_loaded, 16 * N_SMALL)
                activation(as_perm(w_qkv_h[:, 0]), perm(w_raw4[:, 0]), ACT.Identity, scale=SCALE).then_inc(proj_hi, 1)
                activation(as_perm(w_qkv_h[:, 1]), perm(w_raw4[:, 1]), ACT.Identity).then_inc(proj_hi, 1)
                activation(w_qkv_h[:, 2], w_raw4[:, 2], ACT.Identity).then_inc(proj_hi, 1)
                act.wait_ge(bias_scaled, 4)

            for k in range(SLOTS):
                e, c = divmod(k, FC)
                for step in first_at(k - 1):
                    first_step(*step)
                silu(0, k)
                if k:
                    round_act(0, k - 1)
                if e + 1 < NE and c < 3:
                    split_part(3 * (e + 1) + c)
                if e + 1 < NE and c == 2:
                    round_xg(0, e + 1)
                if k == 2:
                    round_projections()
            with act.Fori(1, NT) as t:
                for k in range(SLOTS):
                    e, c = divmod(k, FC)
                    if k == 0:
                        round_xg(t, 0)
                    if k - 1 in LATER_SLOT:
                        later_step(LATER_SLOT[k - 1], t - 1)
                    silu(t, k)
                    round_act(*((t, k - 1) if k else (t - 1, SLOTS - 1)))
                    if e + 1 < NE and c == 2:
                        round_xg(t, e + 1)
            round_act(NT - 1, SLOTS - 1)
            for m in range(len(LATER_AUX)):
                later_step(m, NT - 1)

            def copy_max(b, n):
                act.wait_ge(max_turned, b + 1)
                wait(act, qs_max_ready, b - 1)
                activation(max_rows[n % 2][:].rearrange("p j s -> p (j s)"), max_ps[:], ACT.Identity).then_inc(max_copied, 1)

            def exp_self(b, n):
                act.wait_ge(self_arg_ready, b + 1)
                activation(self_exp[n % 4][:], self_arg[n % 2][:], ACT.Exp).then_inc(self_exp_done, 1)

            def exp_scores(b, n, i):
                wait(act, pv_written, (b - 1) * GI + i + 1)
                act.wait_ge(st_written, b * GI + i + 1)
                activation(probs_t[i][:].rearrange("p j s -> p (j s)"), st_ps[i % 2][:], ACT.Exp).then_inc(exp_done, 1)

            def copy_attn(b, n):
                act.wait_ge(attn_turned, b + 1)
                activation(attn_t[n % 2][:], out_ps[:, 0:D], ACT.Identity).then_inc(attn_copied, 1)

            def body(b, n, first=False, turn_next=True):
                if turn_next:
                    copy_max(b + 1, n + 1)
                    exp_self(b + 1, n + 1)
                for i in range(GI):
                    exp_scores(b, n, i)
                    if not first and i == 2:
                        copy_attn(b - 1, n - 1)

            copy_max(0, 0)
            exp_self(0, 0)
            body(0, 0, first=True)
            with act.Fori(0, B // TB - 1) as g:
                for n in range(1, TB + 1):
                    body(g * TB + n, n)
            for b in range(B - TB + 1, B):
                body(b, b % TB, turn_next=b + 1 < B)
            copy_attn(B - 1, B - 1)

        @block.vector
        def _(dve):
            tt, stt, ts = nc.vector.tensor_tensor, nc.vector.scalar_tensor_tensor, nc.vector.tensor_scalar
            steps = [0]

            def chain(ins):
                steps[0] += 1
                ins.then_inc(dve_step, 1)
                dve.wait_ge(dve_step, steps[0])

            def over_s(z):
                return z.unsqueeze(2).to_broadcast([z.shape[0], TB, S])

            def diffuse_ops(f):
                x = x_in
                z = z_all[:, :, TB * f:TB * f + TB]

                def ready():
                    dve.wait_ge(x_loaded, 16 * (f + 1))
                    if f:
                        dve.wait_ge(aux_written, aux_of("diffuse", f - 1) + 1)
                    chain(tt(dif_a[:, :, 1:D - 1], x[:, :, 0:D - 2], x[:, :, 2:D], ALU.add))

                return [
                    ready,
                    lambda: chain(ts(dif_a[:, :, 0:D:D - 1], x[:, :, 1:D - 1:D - 3], 2.0, None, ALU.mult)),
                    lambda: chain(stt(dif_a[:], x[:], -2.0, dif_a[:], ALU.mult, ALU.add)),
                    lambda: chain(tt(dif_a[:], dif_a[:], over_s(z[:, 0]), ALU.mult)),
                    lambda: chain(stt(dif_b[:], x[:], 1.0, x[:], ALU.subtract, ALU.mult)),
                    lambda: chain(tt(dif_b[:], dif_b[:], over_s(z[:, 2]), ALU.mult)),
                    lambda: chain(tt(dif_a[:], dif_a[:], dif_b[:], ALU.subtract)),
                    lambda: tt(dif_a[:], dif_a[:], x[:], ALU.add).then_inc(dif_ready, 1),
                ]

            def first_step(kind, f, b):
                n = aux_of(kind, f, b)
                if kind == "natural":
                    m = TB * f + b
                    dve.wait_ge(aux_written, n + 1)
                    wait(dve, self_stored[b % 2], 16 * (m // 2))
                    wait(dve, prod_made, m - 1)
                    tt(stage[:, b % 2 * 3 * D:(b % 2 + 1) * 3 * D], aux_ps[:, 0:3 * D],
                       bias_nat[:].rearrange("p k d -> p (k d)"), ALU.add).then_inc(aux_drained, 1)
                    return
                if kind == "setup":
                    dve.wait_ge(aux_written, n + 1)
                    nc.vector.tensor_copy(lora_a_t[:], aux_ps[:, 0:64])
                    nc.vector.tensor_copy(lora_b_t[:], aux_ps[0:64, 128:256]).then_inc(aux_drained, 1)
                    return
                dve.wait_ge(aux_rounded, rounded_of(kind, f))
                if kind == "diffuse":
                    tt(x1_lo[:, f], aux_ps[:], x1_hi[:, f].bitcast(F32), ALU.subtract).then_inc(aux_drained, 1)
                elif kind == "side":
                    tt(in_a_lo[:], aux_ps[:], in_a_hi[:].bitcast(F32), ALU.subtract)
                    stt(in_b_lo[:], aux_ps[:], cols[:, 2:3], in_b_hi[:].bitcast(F32), ALU.add, ALU.subtract)\
                        .then_inc(aux_drained, 1)
                else:
                    stt(rows_lo[:], aux_ps[:], cols[:, 0:1], rows_hi[:].bitcast(F32), ALU.add, ALU.subtract)\
                        .then_inc(aux_drained, 1)

            def sum_self(f, b):
                m = TB * f + b
                dve.wait_ge(prod_made, m + 1)
                nc.vector.tensor_reduce(self_score[:, m].rearrange("p (i j) -> p i j", i=GI),
                                        qk_prod[b % 2][:].rearrange("p (i r j) -> p i j r", i=GI, j=GJ),
                                        AX_X, ALU.add).then_inc(self_summed, 1)

            def later_step(m, t):
                n = t * len(LATER_AUX) + N_FIRST + m
                kind = LATER_AUX[m]
                flat = x3_t[:].rearrange("p b s -> p (b s)")
                if kind != "key":
                    dve.wait_ge(aux_written, n + 1)
                if kind == "lora_a":
                    nc.vector.tensor_copy(one_sel, over_s(lang_one[:, bass.ds(t * TB, TB)]))
                    tt(low_sel, aux_ps[0:64].rearrange("p (b s) -> p b s", b=TB),
                       over_s(lang_sel[:, bass.ds(t * TB, TB)]), ALU.mult).then_inc(aux_drained, 1)
                elif kind == "lora_b":
                    tt(flat, x1[:, t].rearrange("p b s -> p (b s)"), aux_ps[:], ALU.add).then_inc(aux_drained, 1)
                    dve.wait_ge(in_rounded, t + 1)
                    stt(in_b_lo[:], flat, cols[:, 3:4], in_b_hi[:].bitcast(F32), ALU.add, ALU.subtract)\
                        .then_inc(in_lo_ready, 1)
                elif kind == "key":
                    dve.wait_ge(aux_rounded, t + N_ROUNDED + 1)
                    stt(rows_lo[:], aux_ps[:], cols[:, 1:2], rows_hi[:].bitcast(F32), ALU.add, ALU.subtract)\
                        .then_inc(aux_drained, 1)
                elif kind == "value":
                    dve.wait_ge(ones_set, 1)
                    dve.wait_ge(later_stored, t * 32 + 16)
                    tt(v_stage[:, :, :, 0:DH], aux_ps[:].rearrange("p (b h r) -> p b h r", b=TB, r=DH),
                       bias_nat[:, 2].rearrange("p (h r) -> p h r", r=DH).unsqueeze(1).to_broadcast([128, TB, H, DH]),
                       ALU.add).then_inc(aux_drained, 1)
                else:
                    tt(x3_stage[:], aux_ps[:].rearrange("p (b s) -> p b s", b=TB),
                       bo_b[:].unsqueeze(1).to_broadcast([128, TB, D]), ALU.add).then_inc(aux_drained, 1)

            def product(t, k):
                dve.wait_ge(u_written, t * SLOTS + k + 1)
                dve.wait_ge(silu_done, t * SLOTS + k + 1)
                tt(act_p[k % 2][:], act_p[k % 2][:], u_ps[k % 3][:], ALU.mult).then_inc(prod_done, 1)

            def split_act(t, k):
                dve.wait_ge(act_hi_done, t * SLOTS + k + 1)
                tt(act_lo[k % 3][:], act_p[k % 2][:], act_hi[k % 3][:].bitcast(F32), ALU.subtract).then_inc(act_lo_done, 1)

            def add_experts(t):
                dve.wait_ge(down_done, t * SLOTS + SLOTS)
                x = x1[:, t].rearrange("p b s -> p (b s)")
                tt(x, x, acc_ps[:], ALU.add).then_inc(acc_drained, 1)

            dve.wait_ge(diff_loaded, 16 * N_DIFF)
            for op in diffuse_ops(0):
                op()
            dve.wait_ge(gate_loaded, 32)
            chain(ts(one_minus[:], shared_b[:], -1.0, 1.0, ALU.mult, ALU.add))
            tt(gates[:, 0:E], probs_b[:].rearrange("p (b e) -> p e b", e=E),
               one_minus[:].unsqueeze(1).to_broadcast([128, E, B]), ALU.mult).then_inc(gates_ready, 1)
            nc.vector.tensor_copy(gates[:, E], shared_b[:]).then_inc(gates_ready, 1)
            first_step("diffuse", 0, 0)

            def small_work():
                dve.wait_ge(small_loaded, 16 * N_SMALL)
                nc.vector.tensor_copy(len_f[:], len_i[:])
                chain(nc.vector.tensor_copy(lang_f[:], lang_i[:]))
                ts(lang_sel[:], lang_f[:], lang_of[:, 0:1], None, ALU.is_equal)
                ts(lang_one[:], lang_f[0:LANGS], lang_of[0:LANGS, 1:2], None, ALU.is_equal)
                ts(mask_sb[:], key_pos[:], len_f[:, 0:1], NEG, ALU.is_ge, ALU.mult).then_inc(mask_ready, 1)
                dve.wait_ge(proj_hi, 3)
                nc.vector.tensor_copy(as_perm(w_perm[:, 0]), perm(w_raw4[:, 0])).then_inc(proj_lo, 1)
                nc.vector.tensor_copy(as_perm(w_perm[:, 1]), perm(w_raw4[:, 1])).then_inc(proj_lo, 1)
                nc.vector.tensor_copy(as_perm(b_perm[:, 0]), perm(bias_nat[:, 0])).then_inc(proj_lo, 1)
                nc.vector.tensor_copy(as_perm(b_perm[:, 1]), perm(bias_nat[:, 1])).then_inc(proj_lo, 1)
                dve.wait_ge(proj_lo, 4)
                stt(w_qkv_l[:, 0], w_perm[:, 0], SCALE, w_qkv_h[:, 0].bitcast(F32), ALU.mult, ALU.subtract).then_inc(proj_ready, 1)
                tt(w_qkv_l[:, 1], w_perm[:, 1], w_qkv_h[:, 1].bitcast(F32), ALU.subtract).then_inc(proj_ready, 1)
                tt(w_qkv_l[:, 2], w_raw4[:, 2], w_qkv_h[:, 2].bitcast(F32), ALU.subtract).then_inc(proj_ready, 1)
                ts(bias_nat[:, 0], b_perm[:, 0], SCALE, None, ALU.mult).then_inc(bias_scaled, 1)
                nc.vector.tensor_copy(bias_nat[:, 1], b_perm[:, 1]).then_inc(bias_scaled, 1)
                dve.wait_ge(bias_scaled, 2)
                tt(w_perm, bias_nat[:, 0:2], ident[:].unsqueeze(1).to_broadcast([128, 2, D]), ALU.mult).then_inc(bias_scaled, 1)
                dve.wait_ge(bias_scaled, 3)
                nc.vector.tensor_reduce(cols[:, 0:2], w_perm, AX_X, ALU.add).then_inc(bias_scaled, 1)

            pre = {}
            for f in range(1, NT):
                for n, op in enumerate(diffuse_ops(f)):
                    pre.setdefault(slot_of("diffuse", f) - 4 + n // 2, []).append(op)
            for k in range(SLOTS):
                for step in first_at(k - 1):
                    first_step(*step)
                for kind, f, b in first_at(k - 2):
                    if kind == "natural":
                        sum_self(f, b)
                product(0, k)
                if k:
                    split_act(0, k - 1)
                if k == 2:
                    small_work()
                for op in pre.get(k, []):
                    op()
            for stored in self_stored:
                dve.wait_ge(stored, 16 * B // 2)
            nc.vector.memset(v_stage, 1.0).then_inc(ones_set, 1)
            with dve.Fori(1, NT) as t:
                for k in range(SLOTS):
                    if k - 1 in LATER_SLOT:
                        later_step(LATER_SLOT[k - 1], t - 1)
                    product(t, k)
                    split_act(*((t, k - 1) if k else (t - 1, SLOTS - 1)))
                    if k == 1:
                        add_experts(t - 1)
            split_act(NT - 1, SLOTS - 1)
            add_experts(NT - 1)
            for m in range(len(LATER_AUX)):
                later_step(m, NT - 1)

            def max_group(b, n, i):
                dve.wait_ge(s_written, b * GI + i + 1)
                nc.vector.tensor_reduce(max_key[n % 2][:, i], s_ps[i % 2][:].rearrange("p (j s) -> p j s", j=GJ),
                                        AX_X, ALU.max).then_inc(max_done, 1)

            def split_max(b, n):
                own = self_score[:, b].rearrange("p (i j) -> p i j", i=GI)
                rows = max_pad[n % 2][:].rearrange("p j (i c) -> p i j c", i=GI)
                dve.wait_ge(max_done, b * GI + GI)
                tt(max_all[n % 2][:], max_key[n % 2][:], own, ALU.max).then_inc(small_step, 1)
                wait(dve, max_turned, b - 1)
                dve.wait_ge(small_step, b * 2 + 1)
                ts(rows[:, :, :, ROW_MAX_HI].bitcast(F32R), max_all[n % 2][:], -1.0, None, ALU.mult).then_inc(small_step, 1)
                wait(dve, self_exp_done, b - 1)
                tt(self_arg[n % 2][:].rearrange("p (i j) -> p i j", i=GI), own, max_all[n % 2][:], ALU.subtract)\
                    .then_inc(self_arg_ready, 1)
                dve.wait_ge(small_step, b * 2 + 2)
                stt(rows[:, :, :, ROW_MAX_LO], max_all[n % 2][:], -1.0, rows[:, :, :, ROW_MAX_HI],
                    ALU.mult, ALU.subtract).then_inc(max_split, 1)

            def normalise(b, n):
                pv = pv_ps[n % 2][:, 0:H * VW].rearrange("p (h w) -> p h w", w=VW)
                dve.wait_ge(pv_written, b * GI + GI)
                dve.wait_ge(self_exp_done, b + 1)
                tt(denom[n % 2][:], pv[:, :, DH], self_exp[n % 4][:], ALU.add).then_inc(norm_step, 1)
                dve.wait_ge(self_weighted, b + 1)
                tt(numer[n % 2][:], pv[:, :, 0:DH], v_self_w[n % 2][:], ALU.add).then_inc(norm_step, 1)
                dve.wait_ge(norm_step, b * 3 + 2)
                nc.vector.reciprocal(rdenom[n % 2][:], denom[n % 2][:]).then_inc(norm_step, 1)
                dve.wait_ge(norm_step, b * 3 + 3)
                tt(attn[n % 2][:], numer[n % 2][:], rdenom[n % 2][:].unsqueeze(2).to_broadcast([128, H, DH]),
                   ALU.mult).then_inc(attn_done, 1)

            def make_out(b, n):
                dve.wait_ge(out_written, b + 1)
                tt(x3_nat[n % 4][:], out_ps[:, D:2 * D], x3_nat[n % 4][:], ALU.add).then_inc(out_ready, 1)

            def body(b, n, first=False, s_next=True):
                for i in range(GI):
                    if s_next:
                        max_group(b + 2, n + 2, i)
                    if not first and i == 0:
                        normalise(b - 1, n - 1)
                if s_next:
                    split_max(b + 2, n + 2)
                if not first:
                    make_out(b - 1, n - 1)

            dve.wait_ge(pad_zeroed, 2)
            for b in range(2):
                for i in range(GI):
                    max_group(b, b, i)
                split_max(b, b)
            body(0, 0, first=True)
            with dve.Fori(0, B // TB - 1) as g:
                for n in range(1, TB + 1):
                    body(g * TB + n, n)
            for b in range(B - TB + 1, B):
                body(b, b % TB, s_next=b + 2 < B)
            normalise(B - 1, B - 1)
            make_out(B - 1, B - 1)

        @block.gpsimd
        def _(pool):
            tt = nc.gpsimd.tensor_tensor

            def over_s(z):
                return z.unsqueeze(2).to_broadcast([z.shape[0], TB, S])

            def scale_lap(f):
                if f:
                    pool.wait_ge(aux_written, aux_of("diffuse", f - 1) + 1)
                tt(lap_zy[:], lap_t[:].unsqueeze(1).to_broadcast([128, TB, S]),
                   over_s(z_all[:, 1, TB * f:TB * f + TB]), ALU.mult).then_inc(lap_ready, 1)

            def split_part(w):
                pool.wait_ge(w_hi_done, w + 1)
                tt(w_lo[:, w // 3, w % 3], w_raw[w % 3][:], w_hi[:, w // 3, w % 3].bitcast(F32), ALU.subtract)\
                    .then_inc(w_lo_done, 1)

            def gate_x(t, e):
                wait(pool, xg_ready, t * NE + e)
                tt(xg[:], x1[:, t], over_s(gates[:, e, bass.ds(t * TB, TB)]), ALU.mult).then_inc(xg_made, 1)

            def split_xg(t, e):
                pool.wait_ge(xg_rounded, t * NE + e + 1)
                tt(xg_lo[e % 3][:], xg[:].rearrange("p b s -> p (b s)"), xg_hi[e % 3][:].bitcast(F32), ALU.subtract)\
                    .then_inc(xg_ready, 1)

            def multiply_self(f, b):
                m = TB * f + b
                pool.wait_ge(aux_drained, aux_of("natural", f, b) + 1)
                wait(pool, self_summed, m - 1)
                tt(qk_prod[b % 2][:], nat[b % 2][:, 0], nat[b % 2][:, 1], ALU.mult).then_inc(prod_made, 1)

            def split_value_input(t):
                pool.wait_ge(in_rounded, t + 1)
                tt(in_a_lo[:], x3_t[:].rearrange("p b s -> p (b s)"), in_a_hi[:].bitcast(F32), ALU.subtract)\
                    .then_inc(in_a_ready, 1)

            pool.wait_ge(diff_loaded, 16 * N_DIFF)
            scale_lap(0)
            split_part(0)
            split_part(1)
            pool.wait_ge(gates_ready, 2)
            pool.wait_ge(aux_drained, 1)
            gate_x(0, 0)
            split_xg(0, 0)
            split_part(2)
            for k in range(SLOTS):
                e, c = divmod(k, FC)
                if e + 1 < NE and c == 1:
                    gate_x(0, e + 1)
                if e + 1 < NE and c < 3:
                    split_part(3 * (e + 1) + c)
                if e + 1 < NE and c == 2:
                    split_xg(0, e + 1)
                for kind, f, b in first_at(k - 1):
                    if kind == "natural":
                        multiply_self(f, b)
                for kind, f, b in first_at(k + 3):
                    if kind == "diffuse":
                        scale_lap(f)
            with pool.Fori(1, NT) as t:
                for e in range(NE):
                    gate_x(t, e)
                    split_xg(t, e)
                    if e == 1:
                        split_value_input(t - 1)
            split_value_input(NT - 1)

            def place_max(b, n):
                pool.wait_ge(qk_loaded[n % 4], loaded(b, n, 2))
                wait(pool, st_written, (b - 1) * GI)
                pool.wait_ge(max_copied, b + 1)
                tt(qs_max[n % 2][:], qs[n % 4][:].bitcast(F32), max_rows[n % 2][:], ALU.add).then_inc(qs_max_ready, 1)

            def weigh_self(b, n):
                pool.wait_ge(vx_loaded[n % 4], loaded(b, n, 3))
                if isinstance(b, int):
                    wait(pool, attn_done, b - 1)
                pool.wait_ge(self_exp_done, b + 1)
                tt(v_self_w[n % 2][:], v_self[n % 4][:], self_exp[n % 4][:].unsqueeze(2).to_broadcast([128, H, DH]),
                   ALU.mult).then_inc(self_weighted, 1)

            def body(b, n, turn_next=True):
                if turn_next:
                    place_max(b + 1, n + 1)
                weigh_self(b, n)

            pool.wait_ge(down_done, SLOTS * NT)
            for m in max_pad:
                nc.gpsimd.memset(m[:], 0.0).then_inc(pad_zeroed, 1)
            place_max(0, 0)
            body(0, 0)
            with pool.Fori(0, B // TB - 1) as g:
                for n in range(1, TB + 1):
                    body(g * TB + n, n)
            for b in range(B - TB + 1, B):
                body(b, b % TB, turn_next=b + 1 < B)


INPUTS = ["x", "condB_zX", "condB_zY", "condB_zR", "fside_Bx8_0", "condB_sharedgateprob", "itok_B_0_3",
          "fside_BxSxS_0", "itok_B_18_1004", "L1_cond_Wg", "L1_cond_Wu", "L1_cond_Wd", "L1_cond_Sg", "L1_cond_Su",
          "L1_cond_Sd", "L2_cond_lora_A", "L2_cond_lora_B", "L2_cond_lang_embed", "L3_cond_Wq", "L3_cond_bq",
          "L3_cond_Wk", "L3_cond_bk", "L3_cond_Wv", "L3_cond_bv", "L3_cond_Wo", "L3_cond_bo", "L3_cond_b_prev",
          "L3_cond_b_self"]


def shape_constants():
    lap = np.zeros((S, S), np.float32)
    for s in range(S):
        lap[s, s] = -2.0
        lap[abs(s - 1), s] += 1.0
        lap[S - 1 - abs(S - 2 - s), s] += 1.0
    lang_of = np.zeros((LANGS * RANK, 2), np.float32)
    lang_of[:, 0] = np.arange(LANGS * RANK) // RANK
    lang_of[:, 1] = np.arange(LANGS * RANK)
    return {
        "ident": np.eye(128, dtype=np.float32),
        "lap_t": lap,
        "lang_of": lang_of,
        "key_pos": np.tile(np.arange(S, dtype=np.float32), (B, 1)),
        "ones_row": np.ones((1, 1, B * S), np.float32),
        "zeros_row": np.zeros((1, 1, B * S), np.float32),
    }


def kernel(**inputs):
    import concourse.bacc as bacc
    from concourse.bass_utils import run_bass_kernel_spmd

    nc = bacc.Bacc("TRN2", target_bir_lowering=False, num_devices=1)
    arrays, args = {}, {}
    for name, value in [(n, inputs[n]) for n in INPUTS] + list(shape_constants().items()):
        value = np.ascontiguousarray(value)
        arrays[f"in_{name}"] = value
        args[name] = nc.dram_tensor(f"in_{name}", value.shape, mybir.dt.from_np(value.dtype), kind="ExternalInput").ap()
    out = nc.dram_tensor("out", (B, S, D), F32, kind="ExternalOutput").ap()
    build(nc, args, out)
    result = run_bass_kernel_spmd(nc, [arrays], core_ids=[0])
    return result.results[0]["out"]
```

```python
from contextlib import ExitStack

import numpy as np
import concourse.bass as bass
from concourse import mybir

F32 = mybir.dt.float32
F32R = mybir.dt.float32r
I32 = mybir.dt.int32
ACT = mybir.ActivationFunctionType
ALU = mybir.AluOpType
AX_X = mybir.AxisListType.X

B, S, D = 16, 128, 128
E, F = 8, 512
NE = E + 1
FC = F // 128
SLOTS = NE * FC
TB = 4
NT = B // TB
N = TB * S
H, DH = 16, 8
SCALE = float(np.float32(1.0) / np.sqrt(DH).astype(np.float32))
LANGS, RANK = 4, 16
NEG = -1.0e30

GI, GJ = 4, 4
ROW_MASK = 3 * DH * GJ
ROW_MAX = ROW_MASK + 1
Q_SLOTS, K_SLOTS = ((0, 2), 1), ((0, 1), 2)
VW = DH + 1
HALVES = 2
VROW = 32 // HALVES
V_STEP = 128 + VROW
PAIR = 2
NP = B // PAIR

FIRST_AUX = []
for _f in range(NT):
    if _f < 2:
        FIRST_AUX.append((("bias", "setup")[_f], 0, 0))
    if _f:
        FIRST_AUX.append(("diffuse", _f, 0))
    FIRST_AUX += [("side", _f, 0), ("query", _f, 0)] + [("natural", _f, b) for b in range(TB)]
FIRST_AUX_SLOT = 4
AHEAD = 3
LAST_AUX = {(0, 1): 2, (0, 3): 3, (1, 1): 4}
N_FIRST = 1 + len(FIRST_AUX)
LATER_AUX = ["lora_a", "lora_b", "key", "value", "x_natural"]
LATER_SLOT = {3: 0, 5: 1, 9: 2, 11: 3, 13: 4}
ACT_SLOT = {7: 1, 10: 2}
SPLIT_SLOT = 8


def build(nc, a, out):
    with ExitStack() as ctx:
        def sb(name, shape, dt=F32):
            return ctx.enter_context(nc.sbuf_tensor(name, shape, dt))

        def sem(name):
            return ctx.enter_context(nc.semaphore(name))

        def dram(name, shape):
            return nc.dram_tensor(name, shape, F32, kind="Internal").ap()

        q_rows = dram("q_rows", (ROW_MASK, GI, B * S))
        k_rows = dram("k_rows", (ROW_MASK + 1, GI, B * S))
        mask_row = dram("mask_row", (B, S))
        v_prev_d = dram("v_prev_d", (B, S, H * VW))
        v_self_d = dram("v_self_d", (B, S, D))
        x3_d = dram("x3_d", (B, S, D))

        squares = sb("squares", [128, 2, 128])
        ident, lap_t = squares[:, 0], squares[:, 1]
        z_all = sb("z_all", [128, 3, B])
        probs_b = sb("probs_b", [128, B * E])
        shared_b = sb("shared_b", [128, B])
        one_minus = sb("one_minus", [128, B])
        gates = sb("gates", [128, NE, B])
        w_raw4 = sb("w_raw4", [128, 4, D])
        w_qkv_h = sb("w_qkv_h", [128, 3, D], F32R)
        w_qkv_l = sb("w_qkv_l", [128, 3, D], F32R)
        bias_nat = sb("bias_nat", [128, 4, D])
        bias_kp = sb("bias_kp", [128, D])
        cols = sb("cols", [128, 4])
        z_own = sb("z_own", [128, B])
        lora_a_nat = sb("lora_a_nat", [64, D])
        lora_b_nat = sb("lora_b_nat", [128, LANGS, RANK])
        lora_a_t = sb("lora_a_t", [128, 64])
        lora_b_t = sb("lora_b_t", [64, D])
        embed = sb("embed", [LANGS, D])
        lang_i = sb("lang_i", [64, B], I32)
        lang_f = sb("lang_f", [64, B])
        lang_of = sb("lang_of", [64, 2])
        lang_sel = sb("lang_sel", [64, B])
        lang_one = sb("lang_one", [LANGS, B])
        len_i = sb("len_i", [B, 1], I32)
        len_f = sb("len_f", [B, 1])
        key_pos = sb("key_pos", [B, S])
        mask_sb = sb("mask_sb", [B, S])
        self_score = sb("self_score", [128, B, H])

        warm = sb("warm", [128, 2])
        w_raw = [sb(f"w_raw{n}", [128, F]) for n in range(3)]
        x1 = sb("x1", [128, NT, TB, S])
        x1_hi = sb("x1_hi", [128, NT, N], F32R)
        x1_lo = sb("x1_lo", [128, NT, N], F32R)
        act_p = [sb(f"act_p{n}", [128, N]) for n in range(3)]
        act_hi = [sb(f"act_hi{n}", [128, N], F32R) for n in range(3)]
        act_lo = [sb(f"act_lo{n}", [128, N], F32R) for n in range(3)]
        xg = sb("xg", [128, TB, S])
        xg_hi = [sb(f"xg_hi{n}", [128, N], F32R) for n in range(3)]
        xg_lo = [sb(f"xg_lo{n}", [128, N], F32R) for n in range(3)]
        x_in = sb("x_in", [128, TB, D])
        side_in = sb("side_in", [128, TB, D])
        lap_zy = sb("lap_zy", [128, TB, S])
        dif_a = sb("dif_a", [128, TB, D])
        dif_b = sb("dif_b", [128, TB, D])
        in_hi = sb("in_hi", [128, N], F32R)
        in_lo = sb("in_lo", [128, N], F32R)
        rows_hi = sb("rows_hi", [128, N], F32R)
        rows_lo = sb("rows_lo", [128, N], F32R)
        stage = sb("stage", [128, 2 * 3 * D])
        nat = [stage[:, n * 3 * D:(n + 1) * 3 * D].rearrange("p (k d) -> p k d", k=3) for n in range(2)]
        qk_prod = [sb(f"qk_prod{n}", [128, D]) for n in range(2)]
        b_diag = stage[:, 0:2 * D].rearrange("p (k d) -> p k d", k=2)
        b_cols = stage[:, 2 * D:4 * D].rearrange("p (k d) -> p k d", k=2)
        b_sum = stage[:, 4 * D:5 * D]
        x3_t = side_in
        x3_stage = lap_zy
        low_sel = dif_a[0:64]
        one_sel = dif_b[0:LANGS]
        v_stage = stage[:, 0:TB * H * VW].rearrange("p (b h w) -> p b h w", b=TB, h=H)

        phase1 = ExitStack()

        def sb1(name, shape, dt=F32):
            return phase1.enter_context(nc.sbuf_tensor(name, shape, dt))

        w_split = sb1("w_split", [128, NE, 2, 3, F], F32R)
        phase1.close()
        w_hi, w_lo = w_split[:, :, 0], w_split[:, :, 1]
        phase2 = ExitStack()

        def sb2(name, shape, dt=F32):
            return phase2.enter_context(nc.sbuf_tensor(name, shape, dt))

        k_blocks = [sb2(f"k_blocks{n}", [128, GI, GJ, PAIR * S], F32R) for n in range(2)]
        q_plain = [sb2(f"q_plain{n}", [128, GI, PAIR * S], F32R) for n in range(2)]
        q_blocks = [sb2(f"q_blocks{n}", [128, GI, GJ, PAIR * S], F32R) for n in range(2)]
        k_plain = [sb2(f"k_plain{n}", [128, GI, PAIR * S], F32R) for n in range(2)]
        FILLS, end = [], 0
        for tiles, constant in ((k_blocks, 0.0), (q_plain, 1.0), (q_blocks, 0.0), (k_plain, 1.0)):
            for tile in tiles:
                end += int(np.prod(tile.shape[1:]))
                FILLS.append((tile, constant, -(-end // (2 * 3 * F))))
        max_key = [sb2(f"max_key{n}", [128, GI, GJ]) for n in range(2)]
        max_all = [sb2(f"max_all{n}", [128, GI, GJ]) for n in range(2)]
        neg_max = [sb2(f"neg_max{n}", [128, 2, H]) for n in range(2)]
        max_rows = [sb2(f"max_rows{n}", [2 * H, S]) for n in range(2)]
        self_arg = [sb2(f"self_arg{n}", [128, H]) for n in range(2)]
        self_exp = [sb2(f"self_exp{n}", [128, H]) for n in range(4)]
        probs_t = [sb2(f"probs_t{n}", [128, GJ, S]) for n in range(4)]
        v_prev = [sb2(f"v_prev{n}", [128, PAIR, H, VW]) for n in range(2)]
        v_self = [sb2(f"v_self{n}", [128, PAIR, H, DH]) for n in range(2)]
        x3_nat = [sb2(f"x3_nat{n}", [128, PAIR, D]) for n in range(2)]
        v_blocks = [sb2(f"v_blocks{n}", [128, GI * V_STEP]) for n in range(2)]
        pv_own = [sb2(f"pv_own{n}", [128, HALVES, S]) for n in range(2)]
        v_self_w = [sb2(f"v_self_w{n}", [128, H, DH]) for n in range(2)]
        denom = [sb2(f"denom{n}", [128, H]) for n in range(2)]
        rdenom = [sb2(f"rdenom{n}", [128, H]) for n in range(2)]
        numer = [sb2(f"numer{n}", [128, H, DH]) for n in range(2)]
        attn = [sb2(f"attn{n}", [128, H, DH]) for n in range(2)]
        attn_t = [sb2(f"attn_t{n}", [128, D]) for n in range(2)]
        ctx.enter_context(phase2)
        def bank(name):
            return nc.psum_tensor(name, [128, 512], F32)

        phase1p = ExitStack()
        g_ps = [phase1p.enter_context(bank(f"g_ps{n}")) for n in range(3)]
        u_ps = [phase1p.enter_context(bank(f"u_ps{n}")) for n in range(3)]
        acc_ps = phase1p.enter_context(bank("acc_ps"))
        aux_ps = phase1p.enter_context(bank("aux_ps"))
        phase1p.close()
        s_ps = [ctx.enter_context(bank(f"s_ps{n}")) for n in range(2)]
        st_ps = [ctx.enter_context(bank(f"st_ps{n}")) for n in range(2)]
        pv_ps = [ctx.enter_context(bank(f"pv_ps{n}")) for n in range(2)]
        out_ps = ctx.enter_context(bank("out_ps"))
        max_ps = ctx.enter_context(bank("max_ps"))

        squares_loaded, z_loaded = sem("squares_loaded"), sem("z_loaded")
        warm_set = sem("warm_set")
        small_loaded = sem("small_loaded")
        x_loaded = sem("x_loaded")
        side_loaded = sem("side_loaded")
        w_loaded = [sem(f"w_loaded{n}") for n in range(3)]
        w_hi_done, w_lo_done = sem("w_hi_done"), sem("w_lo_done")
        gate_loaded, gates_ready = sem("gate_loaded"), sem("gates_ready")
        self_summed = sem("self_summed")
        ones_set = sem("ones_set")
        proj_hi, proj_ready = sem("proj_hi"), sem("proj_ready")
        mask_ready = sem("mask_ready")
        mask_stored = sem("mask_stored")
        dve_step = sem("dve_step")
        lap_ready = sem("lap_ready")
        dif_ready = sem("dif_ready")
        aux_written, aux_rounded, aux_drained = sem("aux_written"), sem("aux_rounded"), sem("aux_drained")
        prod_made = sem("prod_made")
        rows_stored = sem("rows_stored")
        self_stored = [sem(f"self_stored{n}") for n in range(2)]
        later_stored = sem("later_stored")
        xg_made, xg_rounded, xg_ready = sem("xg_made"), sem("xg_rounded"), sem("xg_ready")
        g_written, u_written = sem("g_written"), sem("u_written")
        silu_done, prod_done = sem("silu_done"), sem("prod_done")
        act_hi_done, act_lo_done = sem("act_hi_done"), sem("act_lo_done")
        down_done = sem("down_done")
        acc_written, acc_drained = sem("acc_written"), sem("acc_drained")
        x3_ready = sem("x3_ready")
        in_rounded, in_lo_ready = sem("in_rounded"), sem("in_lo_ready")
        cols_spread = sem("cols_spread")
        one_sel_ready = sem("one_sel_ready")

        blocks_filled, ones_placed = sem("blocks_filled"), sem("ones_placed")
        first_loaded = [sem(f"first_loaded{n}") for n in range(2)]
        second_loaded = [sem(f"second_loaded{n}") for n in range(2)]
        vx_loaded = [sem(f"vx_loaded{n}") for n in range(2)]
        max_placed = [sem(f"max_placed{n}") for n in range(2)]
        s_written, max_done = sem("s_written"), sem("max_done")
        max_split = sem("max_split")
        max_turned, max_copied = sem("max_turned"), sem("max_copied")
        st_written, exp_done = sem("st_written"), sem("exp_done")
        v_placed, v_zeroed = sem("v_placed"), sem("v_zeroed")
        pv_written = sem("pv_written")
        pv_taken = [sem(f"pv_taken{n}") for n in range(HALVES)]
        pv_turned = sem("pv_turned")
        self_exp_done = sem("self_exp_done")
        self_weighted = sem("self_weighted")
        attn_done = sem("attn_done")
        attn_turned, attn_copied = sem("attn_turned"), sem("attn_copied")
        out_written, out_ready = sem("out_written"), sem("out_ready")
        out_stored = [sem(f"out_stored{n}") for n in range(2)]
        small_step, norm_step = sem("small_step"), sem("norm_step")
        self_arg_ready = sem("self_arg_ready")
        bias_done = sem("bias_done")

        N_SMALL = 10

        def vec(ap, p):
            return ap.unsqueeze(0).to_broadcast([p, ap.shape[0]])

        def part_src(w):
            e, k = divmod(w, 3)
            src = (a["L1_cond_" + "W" + "gud"[k]][e] if e < E else a["L1_cond_" + "S" + "gud"[k]])
            return src.rearrange("(c p) d -> p c d", p=128) if k == 2 else src

        def part_raw(w):
            t = w_raw[w % 3][:]
            return t.rearrange("p (c d) -> p c d", c=FC) if w % 3 == 2 else t

        def blockwise(t):
            return t.rearrange("b s d -> s b d")

        def aux_of(kind, f, b=0):
            return 0 if (kind, f) == ("diffuse", 0) else 1 + FIRST_AUX.index((kind, f, b))

        def first_at(k):
            n = k - FIRST_AUX_SLOT
            return [FIRST_AUX[n]] if 0 <= n < len(FIRST_AUX) else []

        def slot_of(kind, f):
            return FIRST_AUX_SLOT + FIRST_AUX.index((kind, f, 0))

        def rounded_of(kind, f):
            kinds = [("diffuse", 0, 0)] + FIRST_AUX
            return sum(s[0] in ("diffuse", "side", "query") for s in kinds[:aux_of(kind, f) + 1])

        N_ROUNDED = rounded_of("query", NT - 1)
        LAST_STEP = N_FIRST + (NT - 1) * len(LATER_AUX) + 1

        def loaded(b, n, dmas):
            return (b - n) * (4 * dmas) + 16 * dmas * (n // 4 + 1)

        def placed(b, n):
            return (b - n) * 16 + 32 * (n // 2 + 1)

        def wait(eng, semaphore, value):
            if not isinstance(value, int) or value > 0:
                eng.wait_ge(semaphore, value)

        block = ctx.enter_context(nc.Block())

        @block.sync
        def _(sp):
            def load_part(w):
                if w >= 3:
                    sp.wait_ge(w_lo_done, w - 2)
                sp.dma_start(part_raw(w), part_src(w)).then_inc(w_loaded[w % 3], 16)

            def load_x(f):
                if f:
                    sp.wait_ge(aux_written, aux_of("diffuse", f - 1) + 1)
                sp.dma_start(x_in[:], blockwise(a["x"][TB * f:TB * f + TB])).then_inc(x_loaded, 16)

            def load_side(f):
                if f:
                    sp.wait_ge(aux_written, aux_of("side", f - 1) + 1)
                sp.dma_start(side_in[:], blockwise(a["fside_BxSxS_0"][TB * f:TB * f + TB])).then_inc(side_loaded, 16)

            def store_rows(dst, tok, places):
                of_place = dst[0:ROW_MASK].rearrange("(j s r) i n -> j s (r i) n", j=GJ, s=3)
                his, lo = places
                for s in his:
                    sp.dma_start(of_place[:, s, :, tok], rows_hi[:].bitcast(F32)).then_inc(rows_stored, 16)
                sp.dma_start(of_place[:, lo, :, tok], rows_lo[:].bitcast(F32)).then_inc(rows_stored, 16)

            def later_stores(t, n):
                sp.wait_ge(aux_drained, n + 3)
                store_rows(k_rows, bass.ds(t * N, N), K_SLOTS)
                sp.wait_ge(aux_drained, n + 4)
                sp.dma_start(blockwise(v_prev_d[bass.ds(t * TB, TB)]),
                             v_stage.rearrange("p b h w -> p b (h w)")).then_inc(later_stored, 16)
                sp.wait_ge(aux_drained, n + 5)
                sp.dma_start(blockwise(x3_d[bass.ds(t * TB, TB)]), x3_stage[:]).then_inc(later_stored, 16)

            load_x(0)
            sp.dma_start(squares[:], a["squares"].rearrange("k p s -> p k s")).then_inc(squares_loaded, 16)
            for w in range(3):
                load_part(w)

            def small(dst, src):
                sp.dma_start(dst, src).then_inc(small_loaded, 16)

            small(w_raw4[:], a["w_proj"].rearrange("k p d -> p k d"))
            small(bias_nat[:].rearrange("p k d -> p (k d)"), vec(a["b_proj"], 128))
            small(cols[:, 2:4], a["b_in"])
            small(lora_a_nat[:], a["L2_cond_lora_A"].rearrange("l r d -> (l r) d"))
            small(lora_b_nat[:], a["L2_cond_lora_B"].rearrange("l d r -> d l r"))
            small(embed[:], a["L2_cond_lang_embed"])
            small(lang_i[:], vec(a["itok_B_0_3"], 64))
            small(lang_of[:], a["lang_of"])
            small(len_i[:], a["itok_B_18_1004"].unsqueeze(1))
            small(key_pos[:], a["key_pos"])
            load_side(0)
            for w in range(3, 3 + AHEAD):
                load_part(w)
            load_x(1)
            for k in range(SLOTS):
                e, c = divmod(k + AHEAD, FC)
                if e + 1 < NE and c < 3:
                    load_part(3 * (e + 1) + c)
                for step in first_at(k - 1):
                    kind, f, b = step
                    n = aux_of(*step)
                    if kind == "diffuse" and f + 1 < NT:
                        load_x(f + 1)
                    if kind == "query":
                        sp.wait_ge(aux_drained, n + 1)
                        store_rows(q_rows, bass.ds(f * N, N), Q_SLOTS)
                        if f + 1 < NT:
                            load_side(f + 1)
                    if kind == "natural":
                        sp.wait_ge(aux_drained, n + 1)
                        sp.dma_start(v_self_d[TB * f + b], nat[b % 2][:, 2]).then_inc(self_stored[b % 2], 16)
                if k == FIRST_AUX_SLOT:
                    sp.wait_ge(mask_ready, 1)
                    sp.dma_start(mask_row, mask_sb[:]).then_inc(mask_stored, 16)
            sp.wait_ge(mask_stored, 16)
            sp.dma_start(k_rows[ROW_MASK:], mask_row.rearrange("b s -> (b s)").unsqueeze(0).unsqueeze(0)
                         .to_broadcast([1, GI, B * S])).then_inc(later_stored, 16)
            with sp.Fori(1, NT) as t:
                later_stores(t - 1, (t - 1) * len(LATER_AUX) + N_FIRST)

            def load_blocks(dst, src, tok, semaphore):
                for j in range(GJ):
                    r = slice(3 * DH * j, 3 * DH * (j + 1))
                    sp.dma_start(dst[r, :, j].bitcast(F32), src[r, :, tok]).then_inc(semaphore, 16)

            def load_first(p, m):
                tok = bass.ds(p * PAIR * S, PAIR * S)
                load_blocks(k_blocks[m % 2], k_rows, tok, first_loaded[m % 2])
                sp.dma_start(k_blocks[m % 2][ROW_MASK:ROW_MASK + 1].rearrange("p i j n -> p (i j) n").bitcast(F32),
                             mask_row.rearrange("b s -> (b s)").unsqueeze(0).unsqueeze(0)[:, :, tok]
                             .to_broadcast([1, H, PAIR * S])).then_inc(first_loaded[m % 2], 16)
                sp.dma_start(q_plain[m % 2][0:ROW_MASK].bitcast(F32), q_rows[:, :, tok]).then_inc(first_loaded[m % 2], 16)

            def load_second(p, m):
                tok = bass.ds(p * PAIR * S, PAIR * S)
                load_blocks(q_blocks[m % 2], q_rows, tok, second_loaded[m % 2])
                sp.dma_start(k_plain[m % 2][0:ROW_MASK + 1].bitcast(F32), k_rows[:, :, tok])\
                    .then_inc(second_loaded[m % 2], 16)

            def load_vx(p, m):
                pair = bass.ds(p * PAIR, PAIR)
                sp.dma_start(v_prev[m % 2][:].rearrange("p b h w -> p b (h w)"), blockwise(v_prev_d[pair]))\
                    .then_inc(vx_loaded[m % 2], 16)
                sp.dma_start(v_self[m % 2][:].rearrange("p b h w -> p b (h w)"), blockwise(v_self_d[pair]))\
                    .then_inc(vx_loaded[m % 2], 16)
                sp.dma_start(x3_nat[m % 2][:], blockwise(x3_d[pair])).then_inc(vx_loaded[m % 2], 16)

            def store_out(p, m):
                sp.wait_ge(out_ready, p * PAIR + PAIR)
                sp.dma_start(blockwise(out[bass.ds(p * PAIR, PAIR)]), x3_nat[m % 2][:]).then_inc(out_stored[m % 2], 16)

            def step(p, m, first=True, second=True):
                if first:
                    sp.wait_ge(s_written, (p * PAIR + 2 * PAIR) * GI)
                    load_first(p + 3, m + 1)
                if second:
                    sp.wait_ge(st_written, (p * PAIR + PAIR) * GI)
                    load_second(p + 2, m)
                store_out(p, m)
                if second:
                    sp.wait_ge(out_stored[m % 2], (p - m) * 8 + 16)
                    load_vx(p + 2, m)

            sp.wait_ge(rows_stored, 16 * 3 * (2 * NT - 1))
            sp.wait_ge(later_stored, 16 * (1 + 2 * (NT - 1)))
            sp.wait_ge(blocks_filled, 4)
            for m in range(2):
                load_first(m, m)
            sp.wait_ge(blocks_filled, 8)
            for m in range(2):
                sp.dma_start(q_blocks[m][ROW_MASK:ROW_MASK + 1].rearrange("p i j n -> p (i j) n").bitcast(F32),
                             k_plain[m][127:128, 0:1].bitcast(F32).to_broadcast([1, H, PAIR * S])).then_inc(ones_placed, 16)
                load_second(m, m)
            for stored in self_stored:
                sp.wait_ge(stored, 16 * B // 2)
            sp.wait_ge(down_done, SLOTS * NT)
            for m in range(2):
                load_vx(m, m)
            sp.wait_ge(s_written, PAIR * GI)
            load_first(2, 0)
            later_stores(NT - 1, (NT - 1) * len(LATER_AUX) + N_FIRST)
            sp.wait_ge(rows_stored, 16 * 3 * 2 * NT)
            sp.wait_ge(later_stored, 16 * (1 + 2 * NT))
            with sp.Fori(0, NP // 2 - 2) as g:
                for m in range(2):
                    step(g * 2 + m, m)
            for p in range(NP - 4, NP):
                step(p, p % 2, first=p + 3 < NP, second=p + 2 < NP)
            for stored in out_stored:
                sp.wait_ge(stored, 16 * NP // 2)

        @block.tensor
        def _(pe):
            mm, turn = nc.tensor.matmul, nc.tensor.transpose

            def three(dst, w_h, w_l, x_h, x_l, start=True, stop=True):
                mm(dst, w_h, x_h, start=start, stop=False)
                mm(dst, w_h, x_l, start=False, stop=False)
                return mm(dst, w_l, x_h, start=False, stop=stop)

            def diffuse(f):
                pe.wait_ge(dif_ready, f + 1)
                pe.wait_ge(lap_ready, f + 1)
                for b in range(TB):
                    dst = aux_ps[:, b * S:(b + 1) * S]
                    mm(dst, dif_a[:, b], ident, start=True, stop=False)
                    last = mm(dst, x_in[:, b], lap_zy[:, b], start=False, stop=True)
                last.then_inc(aux_written, 1)

            def first_step(kind, f, b):
                n = aux_of(kind, f, b)
                pe.wait_ge(aux_drained, n)
                if kind == "diffuse":
                    diffuse(f)
                elif kind == "bias":
                    pe.wait_ge(cols_spread, 1)
                    mm(aux_ps[:, 0:2 * D], b_cols[:, 0], w_raw4[:, 0:2].rearrange("p k d -> p (k d)"), start=True, stop=True)
                    mm(aux_ps[:, 2 * D:3 * D], b_cols[:, 1], w_raw4[:, 1], start=True, stop=True).then_inc(aux_written, 1)
                elif kind == "setup":
                    turn(aux_ps[:, 0:64], lora_a_nat[:], squares[0:64, 0, 0:64])
                    turn(aux_ps[0:64, 128:256], lora_b_nat[:].rearrange("p l r -> p (l r)"), ident)\
                        .then_inc(aux_written, 1)
                elif kind == "side":
                    pe.wait_ge(side_loaded, 16 * (f + 1))
                    for c in range(TB):
                        last = turn(aux_ps[:, c * S:(c + 1) * S], side_in[:, c], ident)
                    last.then_inc(aux_written, 1)
                elif kind == "query":
                    if f == 0:
                        pe.wait_ge(proj_ready, 2)
                    three(aux_ps[:], w_qkv_h[:, 0], w_qkv_l[:, 0], in_hi[:], in_lo[:]).then_inc(aux_written, 1)
                else:
                    tok = slice(b * S, (b + 1) * S)
                    three(aux_ps[:, 0:3 * D], in_hi[:, tok], in_lo[:, tok], w_qkv_h[:].rearrange("p k d -> p (k d)"),
                          w_qkv_l[:].rearrange("p k d -> p (k d)")).then_inc(aux_written, 1)

            def later_step(m, t):
                pe.wait_ge(aux_drained, t * len(LATER_AUX) + N_FIRST + m)
                kind = LATER_AUX[m]
                if kind == "lora_a":
                    pe.wait_ge(acc_drained, t + 1)
                    last = mm(aux_ps[0:64, :], lora_a_t[:], x1[:, t].rearrange("p b s -> p (b s)"), start=True, stop=True)
                elif kind == "lora_b":
                    mm(aux_ps[:], lora_b_t[:], low_sel.rearrange("p b s -> p (b s)"), start=True, stop=False)
                    last = mm(aux_ps[:], embed[:], one_sel.rearrange("p b s -> p (b s)"), start=False, stop=True)
                elif kind == "key":
                    pe.wait_ge(in_lo_ready, t + 1)
                    last = three(aux_ps[:], w_qkv_h[:, 1], w_qkv_l[:, 1], in_hi[:], in_lo[:])
                elif kind == "value":
                    for b in range(TB):
                        tok = slice(b * S, (b + 1) * S)
                        last = three(aux_ps[:, tok], in_hi[:, tok], in_lo[:, tok], w_qkv_h[:, 2], w_qkv_l[:, 2])
                else:
                    for b in range(TB):
                        last = turn(aux_ps[:, b * S:(b + 1) * S], x3_t[:, b], ident)
                last.then_inc(aux_written, 1)

            def gate_product(t, k):
                e, c = divmod(k, FC)
                chunk = slice(c * 128, (c + 1) * 128)
                if isinstance(t, int) and c == 0:
                    pe.wait_ge(w_lo_done, 3 * e + 1)
                wait(pe, silu_done, t * SLOTS + k - 2)
                three(g_ps[k % 3][:], w_hi[:, e, 0, chunk], w_lo[:, e, 0, chunk], x1_hi[:, t], x1_lo[:, t])\
                    .then_inc(g_written, 1)

            def up_product(t, k):
                e, c = divmod(k, FC)
                chunk = slice(c * 128, (c + 1) * 128)
                if c == 0:
                    if isinstance(t, int):
                        pe.wait_ge(w_lo_done, 3 * e + 2)
                    pe.wait_ge(xg_ready, t * NE + e + 1)
                wait(pe, prod_done, t * SLOTS + k - 2)
                three(u_ps[k % 3][:], w_hi[:, e, 1, chunk], w_lo[:, e, 1, chunk], xg_hi[e % 3][:], xg_lo[e % 3][:])\
                    .then_inc(u_written, 1)

            def down_product(t, k):
                e, c = divmod(k, FC)
                chunk = slice(c * 128, (c + 1) * 128)
                if isinstance(t, int) and t == 0 and c == 0:
                    pe.wait_ge(w_lo_done, 3 * e + 3)
                if k == 0:
                    wait(pe, acc_drained, t)
                pe.wait_ge(act_lo_done, t * SLOTS + k + 1)
                last = three(acc_ps[:], w_hi[:, e, 2, chunk], w_lo[:, e, 2, chunk], act_hi[k % 3][:], act_lo[k % 3][:],
                             start=(k == 0), stop=(k == SLOTS - 1))
                last.then_inc(down_done, 1)

            pe.wait_ge(squares_loaded, 16)
            diffuse(0)
            pe.wait_ge(aux_drained, 1)
            for k in range(3):
                gate_product(0, k)
            for k in range(SLOTS):
                if k >= 3:
                    gate_product(0, k)
                up_product(0, k)
                if k == FIRST_AUX_SLOT - 1:
                    pe.wait_ge(small_loaded, 16 * N_SMALL)
                for step in first_at(k):
                    first_step(*step)
                if k >= 2:
                    down_product(0, k - 2)
            with pe.Fori(1, NT) as t:
                for k in range(SLOTS):
                    gate_product(t, k)
                    if k < 2:
                        down_product(t - 1, SLOTS - 2 + k)
                    up_product(t, k)
                    if k in LATER_SLOT:
                        later_step(LATER_SLOT[k], t - 1)
                    if k >= 2:
                        down_product(t, k - 2)
            def half(n):
                return slice(n % 2 * S, (n % 2 + 1) * S)

            def scores(b, n, i):
                if i == 0:
                    pe.wait_ge(first_loaded[n // 2 % 2], loaded(b, n, 6))
                wait(pe, max_done, b * GI + i - 1)
                mm(s_ps[i % 2][:], q_plain[n // 2 % 2][0:ROW_MASK + 1, i, half(n)],
                   k_blocks[n // 2 % 2][0:ROW_MASK + 1, i, :, half(n)], start=True, stop=True).then_inc(s_written, 1)

            def turn_max(b, n):
                pe.wait_ge(max_split, b + 1)
                wait(pe, max_copied, b)
                turn(max_ps[0:2 * H, 0:S], neg_max[n % 2][:].rearrange("p c h -> p (c h)"), ident)\
                    .then_inc(max_turned, 1)

            def scores_t(b, n, i):
                if i == 0:
                    pe.wait_ge(second_loaded[n // 2 % 2], loaded(b, n, 5))
                    pe.wait_ge(max_placed[n % 2], placed(b, n))
                wait(pe, exp_done, b * GI + i - 1)
                mm(st_ps[i % 2][:], k_plain[n // 2 % 2][0:ROW_MAX + 2, i, half(n)],
                   q_blocks[n // 2 % 2][0:ROW_MAX + 2, i, :, half(n)], start=True, stop=True).then_inc(st_written, 1)

            def weigh(b, n, i):
                if i == 0:
                    pe.wait_ge(v_placed, b * 2 + 2)
                if i % 2 == 0:
                    wait(pe, pv_taken[i // 2], b)
                pe.wait_ge(exp_done, b * GI + i + 1)
                window = V_STEP * i - VROW * (i % 2)
                mm(pv_ps[i // 2][:], v_blocks[n % 2][:, window:window + 128], probs_t[i][:].rearrange("p j s -> p (j s)"),
                   start=(i % 2 == 0), stop=(i % 2 == 1)).then_inc(pv_written, 1)

            def turn_pv(b, n):
                for taken in pv_taken:
                    pe.wait_ge(taken, b + 1)
                wait(pe, out_ready, b)
                for half in range(HALVES):
                    last = turn(out_ps[:, half * D:(half + 1) * D], pv_own[n % 2][:, half], ident)
                last.then_inc(pv_turned, 1)

            def turn_attn(b, n):
                pe.wait_ge(attn_done, b + 1)
                turn(out_ps[:, 2 * D:3 * D], attn[n % 2][:].rearrange("p h r -> p (h r)"), ident).then_inc(attn_turned, 1)

            def project(b, n):
                pe.wait_ge(attn_copied, b + 1)
                mm(out_ps[:, 3 * D:4 * D], attn_t[n % 2][:], w_raw4[:, 3], start=True, stop=True).then_inc(out_written, 1)

            def body(b, n, first=False, s_next=True, turn_next=True):
                if turn_next:
                    turn_max(b + 1, n + 1)
                for i in range(GI):
                    if s_next:
                        scores(b + 2, n + 2, i)
                    if not first and i == 0:
                        weigh(b - 1, n - 1, GI - 1)
                    scores_t(b, n, i)
                    if i:
                        weigh(b, n, i - 1)
                    if not first and i == 1:
                        turn_pv(b - 1, n - 1)
                    if not first and i == 2:
                        turn_attn(b - 1, n - 1)
                    if not first and i == 3:
                        project(b - 1, n - 1)
                    if isinstance(b, int) and (b, i) in LAST_AUX:
                        pe.wait_ge(max_copied, b + 2)
                        later_step(LAST_AUX[b, i], NT - 1)

            for i in range(2):
                pe.wait_ge(silu_done, SLOTS * NT - 2 + i)
                scores(0, 0, i)
                down_product(NT - 1, SLOTS - 2 + i)
            for i in range(2, GI):
                scores(0, 0, i)
            later_step(0, NT - 1)
            for i in range(2):
                scores(1, 1, i)
            pe.wait_ge(aux_drained, LAST_STEP)
            turn_max(0, 0)
            pe.wait_ge(max_copied, 1)
            later_step(1, NT - 1)
            for i in range(2, GI):
                scores(1, 1, i)
            pe.wait_ge(aux_drained, LAST_STEP + 1)
            pe.wait_ge(ones_placed, 32)
            body(0, 0, first=True)
            pe.wait_ge(aux_drained, LAST_STEP + 3)
            body(1, 1)
            pe.wait_ge(aux_drained, LAST_STEP + 4)
            with pe.Fori(0, B // TB - 1) as g:
                for n in range(2, TB + 2):
                    body(g * TB + n, n)
            for b in range(B - 2, B):
                body(b, b % TB, s_next=b + 2 < B, turn_next=b + 1 < B)
            weigh(B - 1, B - 1, GI - 1)
            turn_pv(B - 1, B - 1)
            turn_attn(B - 1, B - 1)
            project(B - 1, B - 1)

        @block.scalar
        def _(act):
            activation = nc.scalar.activation

            def small(dst, src, semaphore):
                act.dma_start(dst, src).then_inc(semaphore, 16)

            small(z_all[:].rearrange("p k b -> p (k b)"), vec(a["z"], 128), z_loaded)
            small(probs_b[:], a["fside_Bx8_0"].rearrange("b e -> (b e)").unsqueeze(0).to_broadcast([128, B * E]), gate_loaded)
            small(shared_b[:], vec(a["condB_sharedgateprob"], 128), gate_loaded)

            act.wait_ge(warm_set, 1)
            activation(warm[:, 1:2], warm[:, 0:1], ACT.Silu)

            def split_part(w):
                act.wait_ge(w_loaded[w % 3], 16 * (w // 3 + 1))
                activation(w_hi[:, w // 3, w % 3], w_raw[w % 3][:], ACT.Identity).then_inc(w_hi_done, 1)

            def first_step(kind, f, b):
                n = aux_of(kind, f, b)
                if kind in ("natural", "setup", "bias"):
                    return
                act.wait_ge(aux_written, n + 1)
                if kind == "diffuse":
                    activation(x1_hi[:, f], aux_ps[:], ACT.Identity)
                    activation(x1[:, f].rearrange("p b s -> p (b s)"), aux_ps[:], ACT.Identity).then_inc(aux_rounded, 1)
                elif kind == "side":
                    activation(in_hi[:], aux_ps[:], ACT.Identity).then_inc(aux_rounded, 1)
                else:
                    wait(act, rows_stored, 48 * f)
                    activation(rows_hi[:], aux_ps[:], ACT.Identity, bias=cols[:, 0:1]).then_inc(aux_rounded, 1)

            def later_step(m, t):
                n = t * len(LATER_AUX) + N_FIRST + m
                if LATER_AUX[m] == "lora_b":
                    act.wait_ge(aux_drained, n + 1)
                    activation(in_hi[:], x3_t[:].rearrange("p b s -> p (b s)"), ACT.Identity).then_inc(in_rounded, 1)
                elif LATER_AUX[m] == "key":
                    act.wait_ge(aux_written, n + 1)
                    act.wait_ge(rows_stored, t * 48 + 48 * NT)
                    activation(rows_hi[:], aux_ps[:], ACT.Identity, bias=cols[:, 1:2]).then_inc(aux_rounded, 1)

            def silu(t, k):
                wait(act, act_lo_done, t * SLOTS + k - 2)
                act.wait_ge(g_written, t * SLOTS + k + 1)
                activation(act_p[k % 3][:], g_ps[k % 3][:], ACT.Silu).then_inc(silu_done, 1)

            def round_act(t, k):
                wait(act, down_done, t * SLOTS + k - 2)
                act.wait_ge(prod_done, t * SLOTS + k + 1)
                activation(act_hi[k % 3][:], act_p[k % 3][:], ACT.Identity).then_inc(act_hi_done, 1)

            def round_xg(t, e):
                wait(act, u_written, t * SLOTS + (e - 3) * FC + FC)
                act.wait_ge(xg_made, t * NE + e + 1)
                activation(xg_hi[e % 3][:], xg[:].rearrange("p b s -> p (b s)"), ACT.Identity).then_inc(xg_rounded, 1)

            split_part(0)
            split_part(1)
            first_step("diffuse", 0, 0)
            round_xg(0, 0)
            split_part(2)

            def round_projections():
                act.wait_ge(small_loaded, 16 * N_SMALL)
                activation(w_qkv_h[:, 0], w_raw4[:, 0], ACT.Identity, scale=SCALE).then_inc(proj_hi, 1)
                activation(w_qkv_h[:, 1:3], w_raw4[:, 1:3], ACT.Identity).then_inc(proj_hi, 1)

            for k in range(SLOTS):
                e, c = divmod(k, FC)
                for step in first_at(k - 1):
                    first_step(*step)
                silu(0, k)
                if k:
                    round_act(0, k - 1)
                if e + 1 < NE and c < 3:
                    split_part(3 * (e + 1) + c)
                if e + 1 < NE and c == 2:
                    round_xg(0, e + 1)
                if k == 2:
                    round_projections()
            with act.Fori(1, NT) as t:
                for k in range(SLOTS):
                    e, c = divmod(k, FC)
                    if k == 0:
                        round_xg(t, 0)
                    if k in ACT_SLOT:
                        later_step(ACT_SLOT[k], t - 1)
                    silu(t, k)
                    round_act(*((t, k - 1) if k else (t - 1, SLOTS - 1)))
                    if e + 1 < NE and c == 2:
                        round_xg(t, e + 1)
            round_act(NT - 1, SLOTS - 1)

            def copy_max(b, n):
                act.wait_ge(max_turned, b + 1)
                if n >= 2:
                    act.wait_ge(max_placed[n % 2], placed(b - 2, n - 2))
                activation(max_rows[n % 2][:], max_ps[0:2 * H, 0:S], ACT.Identity).then_inc(max_copied, 1)

            def exp_self(b, n):
                act.wait_ge(self_arg_ready, b + 1)
                activation(self_exp[n % 4][:], self_arg[n % 2][:], ACT.Exp).then_inc(self_exp_done, 1)

            def exp_scores(b, n, i):
                wait(act, pv_written, (b - 1) * GI + i + 1)
                act.wait_ge(st_written, b * GI + i + 1)
                activation(probs_t[i][:].rearrange("p j s -> p (j s)"), st_ps[i % 2][:], ACT.Exp).then_inc(exp_done, 1)

            def take_first(b, n):
                act.wait_ge(pv_written, b * GI + 2)
                wait(act, pv_turned, b - 1)
                for j in range(GJ):
                    rows = slice(32 * j, 32 * j + 32)
                    last = activation(pv_own[n % 2][rows, 0], pv_ps[0][rows, j * S:(j + 1) * S], ACT.Identity)
                last.then_inc(pv_taken[0], 1)

            def copy_attn(b, n):
                act.wait_ge(attn_turned, b + 1)
                activation(attn_t[n % 2][:], out_ps[:, 2 * D:3 * D], ACT.Identity).then_inc(attn_copied, 1)

            def body(b, n, first=False, turn_next=True):
                if turn_next:
                    copy_max(b + 1, n + 1)
                    exp_self(b + 1, n + 1)
                for i in range(GI):
                    exp_scores(b, n, i)
                    if isinstance(b, int) and (b, i) in LAST_AUX:
                        later_step(LAST_AUX[b, i], NT - 1)
                    if i == 2:
                        take_first(b, n)
                    if not first and i == 3:
                        copy_attn(b - 1, n - 1)

            copy_max(0, 0)
            exp_self(0, 0)
            later_step(1, NT - 1)
            body(0, 0, first=True)
            body(1, 1)
            with act.Fori(0, B // TB - 1) as g:
                for n in range(2, TB + 2):
                    body(g * TB + n, n)
            for b in range(B - 2, B):
                body(b, b % TB, turn_next=b + 1 < B)
            copy_attn(B - 1, B - 1)

        @block.vector
        def _(dve):
            tt, stt, ts = nc.vector.tensor_tensor, nc.vector.scalar_tensor_tensor, nc.vector.tensor_scalar
            steps = [0]

            def chain(ins):
                steps[0] += 1
                ins.then_inc(dve_step, 1)
                dve.wait_ge(dve_step, steps[0])

            def over_s(z):
                return z.unsqueeze(2).to_broadcast([z.shape[0], TB, S])

            def diffuse_ops(f):
                x = x_in
                z = z_all[:, :, TB * f:TB * f + TB]

                def ready():
                    dve.wait_ge(x_loaded, 16 * (f + 1))
                    if f:
                        dve.wait_ge(aux_written, aux_of("diffuse", f - 1) + 1)
                    chain(tt(dif_a[:, :, 1:D - 1], x[:, :, 0:D - 2], x[:, :, 2:D], ALU.add))

                def scale():
                    if f == 0:
                        dve.wait_ge(z_loaded, 16)
                    chain(tt(dif_a[:], dif_a[:], over_s(z[:, 0]), ALU.mult))

                return [
                    ready,
                    lambda: chain(ts(dif_a[:, :, 0:D:D - 1], x[:, :, 1:D - 1:D - 3], 2.0, None, ALU.mult)),
                    lambda: chain(stt(dif_a[:], x[:], -2.0, dif_a[:], ALU.mult, ALU.add)),
                    lambda: chain(stt(dif_b[:], x[:], 1.0, x[:], ALU.subtract, ALU.mult)),
                    scale,
                    lambda: chain(tt(dif_b[:], dif_b[:], over_s(z[:, 2]), ALU.mult)),
                    lambda: chain(tt(dif_a[:], dif_a[:], dif_b[:], ALU.subtract)),
                    lambda: tt(dif_a[:], dif_a[:], x[:], ALU.add).then_inc(dif_ready, 1),
                ]

            def first_step(kind, f, b):
                n = aux_of(kind, f, b)
                if kind == "natural":
                    m = TB * f + b
                    dve.wait_ge(aux_written, n + 1)
                    wait(dve, self_stored[b % 2], 16 * (m // 2))
                    wait(dve, prod_made, m - 1)
                    tt(stage[:, b % 2 * 3 * D:(b % 2 + 1) * 3 * D], aux_ps[:, 0:3 * D],
                       bias_nat[:, 0:3].rearrange("p k d -> p (k d)"), ALU.add).then_inc(aux_drained, 1)
                    return
                if kind == "bias":
                    dve.wait_ge(aux_written, n + 1)
                    tt(b_sum, aux_ps[:, 0:D], bias_nat[:, 0], ALU.add).then_inc(bias_done, 1)
                    tt(bias_kp[:], aux_ps[:, 2 * D:3 * D], bias_nat[:, 1], ALU.add).then_inc(bias_done, 1)
                    dve.wait_ge(bias_done, 2)
                    ts(bias_nat[:, 0], b_sum, SCALE, None, ALU.mult).then_inc(bias_done, 1)
                    tt(bias_nat[:, 1], aux_ps[:, D:2 * D], bias_nat[:, 1], ALU.add).then_inc(bias_done, 1)
                    dve.wait_ge(bias_done, 4)
                    tt(b_diag[:, 0], bias_nat[:, 0], ident, ALU.mult).then_inc(bias_done, 1)
                    tt(b_diag[:, 1], bias_kp[:], ident, ALU.mult).then_inc(bias_done, 1)
                    dve.wait_ge(bias_done, 6)
                    nc.vector.tensor_reduce(cols[:, 0:2], b_diag, AX_X, ALU.add).then_inc(aux_drained, 1)
                    return
                if kind == "setup":
                    dve.wait_ge(aux_written, n + 1)
                    nc.vector.tensor_copy(lora_a_t[:], aux_ps[:, 0:64])
                    nc.vector.tensor_copy(lora_b_t[:], aux_ps[0:64, 128:256]).then_inc(aux_drained, 1)
                    return
                dve.wait_ge(aux_rounded, rounded_of(kind, f))
                if kind == "diffuse":
                    tt(x1_lo[:, f], aux_ps[:], x1_hi[:, f].bitcast(F32), ALU.subtract).then_inc(aux_drained, 1)
                elif kind == "side":
                    tt(in_lo[:], aux_ps[:], in_hi[:].bitcast(F32), ALU.subtract).then_inc(aux_drained, 1)
                else:
                    stt(rows_lo[:], aux_ps[:], cols[:, 0:1], rows_hi[:].bitcast(F32), ALU.add, ALU.subtract)\
                        .then_inc(aux_drained, 1)

            def sum_self(f, b):
                m = TB * f + b
                dve.wait_ge(prod_made, m + 1)
                nc.vector.tensor_reduce(self_score[:, m].rearrange("p (i j) -> p i j", i=GI),
                                        qk_prod[b % 2][:].rearrange("p (j r i) -> p i j r", i=GI, j=GJ),
                                        AX_X, ALU.add).then_inc(self_summed, 1)

            def later_step(m, t):
                n = t * len(LATER_AUX) + N_FIRST + m
                kind = LATER_AUX[m]
                flat = x3_t[:].rearrange("p b s -> p (b s)")
                if kind != "key":
                    dve.wait_ge(aux_written, n + 1)
                if kind == "lora_a":
                    nc.vector.tensor_copy(one_sel, over_s(lang_one[:, bass.ds(t * TB, TB)]))
                    tt(low_sel, aux_ps[0:64].rearrange("p (b s) -> p b s", b=TB),
                       over_s(lang_sel[:, bass.ds(t * TB, TB)]), ALU.mult).then_inc(aux_drained, 1)
                elif kind == "lora_b":
                    tt(flat, x1[:, t].rearrange("p b s -> p (b s)"), aux_ps[:], ALU.add).then_inc(aux_drained, 1)
                elif kind == "key":
                    dve.wait_ge(aux_rounded, t + N_ROUNDED + 1)
                    stt(rows_lo[:], aux_ps[:], cols[:, 1:2], rows_hi[:].bitcast(F32), ALU.add, ALU.subtract)\
                        .then_inc(aux_drained, 1)
                elif kind == "value":
                    dve.wait_ge(ones_set, 1)
                    dve.wait_ge(later_stored, t * 32 + 16)
                    tt(v_stage[:, :, :, 0:DH], aux_ps[:].rearrange("p (b h r) -> p b h r", b=TB, r=DH),
                       bias_nat[:, 2].rearrange("p (h r) -> p h r", r=DH).unsqueeze(1).to_broadcast([128, TB, H, DH]),
                       ALU.add).then_inc(aux_drained, 1)
                else:
                    tt(x3_stage[:], aux_ps[:].rearrange("p (b s) -> p b s", b=TB),
                       bias_nat[:, 3].unsqueeze(1).to_broadcast([128, TB, D]), ALU.add).then_inc(aux_drained, 1)

            def split_input(t):
                dve.wait_ge(in_rounded, t + 1)
                tt(in_lo[:], x3_t[:].rearrange("p b s -> p (b s)"), in_hi[:].bitcast(F32), ALU.subtract).then_inc(in_lo_ready, 1)

            def product(t, k):
                dve.wait_ge(u_written, t * SLOTS + k + 1)
                dve.wait_ge(silu_done, t * SLOTS + k + 1)
                tt(act_p[k % 3][:], act_p[k % 3][:], u_ps[k % 3][:], ALU.mult).then_inc(prod_done, 1)

            def split_act(t, k):
                dve.wait_ge(act_hi_done, t * SLOTS + k + 1)
                tt(act_lo[k % 3][:], act_p[k % 3][:], act_hi[k % 3][:].bitcast(F32), ALU.subtract).then_inc(act_lo_done, 1)

            def add_experts(t):
                dve.wait_ge(down_done, t * SLOTS + SLOTS)
                x = x1[:, t].rearrange("p b s -> p (b s)")
                tt(x, x, acc_ps[:], ALU.add).then_inc(acc_drained, 1)

            nc.vector.memset(warm[:], 0.0).then_inc(warm_set, 1)
            for op in diffuse_ops(0):
                op()
            dve.wait_ge(gate_loaded, 32)
            chain(ts(one_minus[:], shared_b[:], -1.0, 1.0, ALU.mult, ALU.add))
            tt(gates[:, 0:E], probs_b[:].rearrange("p (b e) -> p e b", e=E),
               one_minus[:].unsqueeze(1).to_broadcast([128, E, B]), ALU.mult).then_inc(gates_ready, 1)
            nc.vector.tensor_copy(gates[:, E], shared_b[:]).then_inc(gates_ready, 1)
            first_step("diffuse", 0, 0)
            flat = xg[:].rearrange("p b s -> p (b s)")
            dve.wait_ge(gates_ready, 2)
            tt(xg[:], x1[:, 0], over_s(gates[:, 0, 0:TB]), ALU.mult).then_inc(xg_made, 1)
            dve.wait_ge(xg_rounded, 1)
            tt(xg_lo[0][:], flat, xg_hi[0][:].bitcast(F32), ALU.subtract).then_inc(xg_ready, 1)

            def small_work():
                dve.wait_ge(small_loaded, 16 * N_SMALL)
                nc.vector.tensor_copy(len_f[:], len_i[:])
                chain(nc.vector.tensor_copy(lang_f[:], lang_i[:]))
                ts(lang_sel[:], lang_f[:], lang_of[:, 0:1], None, ALU.is_equal)
                ts(lang_one[:], lang_f[0:LANGS], lang_of[0:LANGS, 1:2], None, ALU.is_equal)
                ts(mask_sb[:], key_pos[:], len_f[:, 0:1], NEG, ALU.is_ge, ALU.mult).then_inc(mask_ready, 1)
                dve.wait_ge(proj_hi, 2)
                nc.vector.tensor_copy(b_cols, cols[:, 2:4].unsqueeze(2).to_broadcast([128, 2, D])).then_inc(cols_spread, 1)
                stt(w_qkv_l[:, 0], w_raw4[:, 0], SCALE, w_qkv_h[:, 0].bitcast(F32), ALU.mult, ALU.subtract).then_inc(proj_ready, 1)
                tt(w_qkv_l[:, 1:3], w_raw4[:, 1:3], w_qkv_h[:, 1:3].bitcast(F32), ALU.subtract).then_inc(proj_ready, 1)

            pre = {}
            for f in range(1, NT):
                for n, op in enumerate(diffuse_ops(f)):
                    pre.setdefault(slot_of("diffuse", f) - 4 + n // 2, []).append(op)
            for k in range(SLOTS):
                for step in first_at(k - 1):
                    first_step(*step)
                for kind, f, b in first_at(k - 2):
                    if kind == "natural":
                        sum_self(f, b)
                product(0, k)
                if k:
                    split_act(0, k - 1)
                if k == 2:
                    small_work()
                for op in pre.get(k, []):
                    op()
            for stored in self_stored:
                dve.wait_ge(stored, 16 * B // 2)
            nc.vector.memset(v_stage, 1.0).then_inc(ones_set, 1)
            with dve.Fori(1, NT) as t:
                for k in range(SLOTS):
                    if k - 1 in LATER_SLOT:
                        later_step(LATER_SLOT[k - 1], t - 1)
                    if k == SPLIT_SLOT:
                        split_input(t - 1)
                    product(t, k)
                    split_act(*((t, k - 1) if k else (t - 1, SLOTS - 1)))
                    if k == 1:
                        add_experts(t - 1)
            split_act(NT - 1, SLOTS - 1)
            def max_group(b, n, i):
                dve.wait_ge(s_written, b * GI + i + 1)
                nc.vector.tensor_reduce(max_key[n % 2][:, i], s_ps[i % 2][:].rearrange("p (j s) -> p j s", j=GJ),
                                        AX_X, ALU.max).then_inc(max_done, 1)

            def split_max(b, n):
                own = self_score[:, b].rearrange("p (i j) -> p i j", i=GI)
                part = neg_max[n % 2][:].rearrange("p c (i j) -> p c i j", i=GI)
                dve.wait_ge(max_done, b * GI + GI)
                tt(max_all[n % 2][:], max_key[n % 2][:], own, ALU.max).then_inc(small_step, 1)
                wait(dve, max_turned, b - 1)
                dve.wait_ge(small_step, b * 2 + 1)
                ts(part[:, 0].bitcast(F32R), max_all[n % 2][:], -1.0, None, ALU.mult).then_inc(small_step, 1)
                wait(dve, self_exp_done, b - 1)
                tt(self_arg[n % 2][:].rearrange("p (I j c) -> p I c j", I=HALVES, j=GJ),
                   self_score[:, b].rearrange("p (I c j) -> p I c j", I=HALVES, j=GJ),
                   max_all[n % 2][:].rearrange("p (I c) j -> p I c j", I=HALVES), ALU.subtract).then_inc(self_arg_ready, 1)
                dve.wait_ge(small_step, b * 2 + 2)
                stt(part[:, 1], max_all[n % 2][:], -1.0, part[:, 0], ALU.mult, ALU.subtract).then_inc(max_split, 1)

            def take_second(b, n):
                dve.wait_ge(pv_written, b * GI + GI)
                for j in range(GJ):
                    rows = slice(32 * j, 32 * j + 32)
                    last = nc.vector.tensor_copy(pv_own[n % 2][rows, 1], pv_ps[1][rows, j * S:(j + 1) * S])
                last.then_inc(pv_taken[1], 1)

            def normalise(b, n):
                pv = out_ps[:, 0:H * VROW].rearrange("p (h w) -> p h w", w=VROW)
                dve.wait_ge(pv_turned, b + 1)
                dve.wait_ge(self_exp_done, b + 1)
                tt(denom[n % 2][:], pv[:, :, DH], self_exp[n % 4][:], ALU.add).then_inc(norm_step, 1)
                dve.wait_ge(self_weighted, b + 1)
                tt(numer[n % 2][:], pv[:, :, 0:DH], v_self_w[n % 2][:], ALU.add).then_inc(norm_step, 1)
                dve.wait_ge(norm_step, b * 3 + 2)
                nc.vector.reciprocal(rdenom[n % 2][:], denom[n % 2][:]).then_inc(norm_step, 1)
                dve.wait_ge(norm_step, b * 3 + 3)
                tt(attn[n % 2][:], numer[n % 2][:], rdenom[n % 2][:].unsqueeze(2).to_broadcast([128, H, DH]),
                   ALU.mult).then_inc(attn_done, 1)

            def make_out(b, n):
                dve.wait_ge(out_written, b + 1)
                x = x3_nat[n // 2 % 2][:, n % 2]
                tt(x, out_ps[:, 3 * D:4 * D], x, ALU.add).then_inc(out_ready, 1)

            def body(b, n, first=False, s_next=True):
                for i in range(GI):
                    if s_next:
                        max_group(b + 2, n + 2, i)
                    if not first and i == 0:
                        take_second(b - 1, n - 1)
                    if not first and i == 1:
                        normalise(b - 1, n - 1)
                    if isinstance(b, int) and (b, i) in LAST_AUX:
                        later_step(LAST_AUX[b, i], NT - 1)
                if s_next:
                    split_max(b + 2, n + 2)
                if not first:
                    make_out(b - 1, n - 1)

            max_group(0, 0, 0)
            add_experts(NT - 1)
            for i in range(1, GI):
                max_group(0, 0, i)
            split_max(0, 0)
            later_step(0, NT - 1)
            for i in range(2):
                max_group(1, 1, i)
            later_step(1, NT - 1)
            split_input(NT - 1)
            for i in range(2, GI):
                max_group(1, 1, i)
            split_max(1, 1)
            body(0, 0, first=True)
            body(1, 1)
            with dve.Fori(0, B // TB - 1) as g:
                for n in range(2, TB + 2):
                    body(g * TB + n, n)
            for b in range(B - 2, B):
                body(b, b % TB, s_next=b + 2 < B)
            take_second(B - 1, B - 1)
            normalise(B - 1, B - 1)
            make_out(B - 1, B - 1)

        @block.gpsimd
        def _(pool):
            tt = nc.gpsimd.tensor_tensor

            def over_s(z):
                return z.unsqueeze(2).to_broadcast([z.shape[0], TB, S])

            def scale_lap(f):
                if f:
                    pool.wait_ge(aux_written, aux_of("diffuse", f - 1) + 1)
                tt(lap_zy[:], lap_t.unsqueeze(1).to_broadcast([128, TB, S]),
                   over_s(z_all[:, 1, TB * f:TB * f + TB]), ALU.mult).then_inc(lap_ready, 1)

            def split_part(w):
                pool.wait_ge(w_hi_done, w + 1)
                tt(w_lo[:, w // 3, w % 3], w_raw[w % 3][:], w_hi[:, w // 3, w % 3].bitcast(F32), ALU.subtract)\
                    .then_inc(w_lo_done, 1)

            def gate_x(t, e):
                wait(pool, xg_ready, t * NE + e)
                tt(xg[:], x1[:, t], over_s(gates[:, e, bass.ds(t * TB, TB)]), ALU.mult).then_inc(xg_made, 1)

            def split_xg(t, e):
                pool.wait_ge(xg_rounded, t * NE + e + 1)
                tt(xg_lo[e % 3][:], xg[:].rearrange("p b s -> p (b s)"), xg_hi[e % 3][:].bitcast(F32), ALU.subtract)\
                    .then_inc(xg_ready, 1)

            def multiply_self(f, b):
                m = TB * f + b
                pool.wait_ge(aux_drained, aux_of("natural", f, b) + 1)
                wait(pool, self_summed, m - 1)
                tt(qk_prod[b % 2][:], nat[b % 2][:, 0], nat[b % 2][:, 1], ALU.mult).then_inc(prod_made, 1)

            pool.wait_ge(squares_loaded, 16)
            pool.wait_ge(z_loaded, 16)
            scale_lap(0)
            split_part(0)
            split_part(1)
            pool.wait_ge(gates_ready, 2)
            split_part(2)
            pool.wait_ge(aux_drained, 1)
            for k in range(SLOTS):
                e, c = divmod(k, FC)
                if e + 1 < NE and c == 1:
                    gate_x(0, e + 1)
                if e + 1 < NE and c < 3:
                    split_part(3 * (e + 1) + c)
                if e + 1 < NE and c == 2:
                    split_xg(0, e + 1)
                for kind, f, b in first_at(k - 1):
                    if kind == "natural":
                        multiply_self(f, b)
                for kind, f, b in first_at(k + 3):
                    if kind == "diffuse":
                        scale_lap(f)
            with pool.Fori(1, NT - 1) as t:
                for e in range(NE):
                    gate_x(t, e)
                    split_xg(t, e)
            for e in range(NE):
                gate_x(NT - 1, e)
                split_xg(NT - 1, e)
                for tile, constant, experts in FILLS:
                    if e == min(experts + 2, NE - 1):
                        pool.wait_ge(down_done, SLOTS * (NT - 1) + experts * FC)
                        nc.gpsimd.memset(tile[:].bitcast(F32), constant).then_inc(blocks_filled, 1)

            def place_max(b, n):
                for c in range(2):
                    pool.dma_start(q_blocks[n // 2 % 2][ROW_MAX + c:ROW_MAX + c + 1, :, :, n % 2 * S:(n % 2 + 1) * S]
                                   .rearrange("p i j s -> p (i j) s").bitcast(F32),
                                   max_rows[n % 2][c * H:(c + 1) * H]).then_inc(max_placed[n % 2], 16)

            def place_values(b, n):
                for half in range(HALVES):
                    to = v_blocks[n % 2][:, 2 * half * V_STEP:2 * (half + 1) * V_STEP].rearrange("p (c x) -> p c x", c=HALVES)
                    nc.gpsimd.tensor_copy(to[:, :, 0:128].rearrange("p c (j y) -> p j c y", j=GJ)[:, :, :, 0:VW],
                                          v_prev[n // 2 % 2][:, n % 2, half * H // 2:(half + 1) * H // 2]
                                          .rearrange("p (j c) w -> p j c w", j=GJ)).then_inc(v_placed, 1)

            def weigh_self(b, n, place_next):
                pool.wait_ge(vx_loaded[n // 2 % 2], loaded(b, n, 3))
                wait(pool, attn_done, b - 1)
                wait(pool, pv_written, (b - 1) * GI)
                pool.wait_ge(self_exp_done, b + 1)
                if place_next:
                    pool.wait_ge(max_copied, b + 2)
                tt(v_self_w[n % 2][:], v_self[n // 2 % 2][:, n % 2], self_exp[n % 4][:].unsqueeze(2).to_broadcast([128, H, DH]),
                   ALU.mult).then_inc(self_weighted, 1)

            def body(b, n, turn_next=True):
                weigh_self(b, n, turn_next)
                place_values(b, n)
                if turn_next:
                    place_max(b + 1, n + 1)

            pool.wait_ge(down_done, SLOTS * NT)
            for v in v_blocks:
                nc.gpsimd.memset(v[:], 0.0).then_inc(v_zeroed, 1)
            pool.wait_ge(v_zeroed, 2)
            pool.wait_ge(max_copied, 1)
            place_max(0, 0)
            body(0, 0)
            body(1, 1)
            with pool.Fori(0, B // TB - 1) as g:
                for n in range(2, TB + 2):
                    body(g * TB + n, n)
            for b in range(B - 2, B):
                body(b, b % TB, turn_next=b + 1 < B)


def flat_inputs(inputs):
    stacked = {
        "z": ("condB_zX", "condB_zY", "condB_zR"),
        "w_proj": ("L3_cond_Wq", "L3_cond_Wk", "L3_cond_Wv", "L3_cond_Wo"),
        "b_proj": ("L3_cond_bq", "L3_cond_bk", "L3_cond_bv", "L3_cond_bo"),
        "b_in": ("L3_cond_b_self", "L3_cond_b_prev"),
    }
    arrays = {name: laid_out(name, np.asarray(value)) for name, value in inputs.items()}
    for name, parts in stacked.items():
        arrays[name] = np.stack([arrays.pop(part) for part in parts])
    for name in ("z", "b_proj"):
        arrays[name] = arrays[name].reshape(-1)
    arrays["b_in"] = arrays["b_in"].reshape(2, D).T
    return arrays


def shape_constants():
    lap = np.zeros((S, S), np.float32)
    for s in range(S):
        lap[s, s] = -2.0
        lap[abs(s - 1), s] += 1.0
        lap[S - 1 - abs(S - 2 - s), s] += 1.0
    lang_of = np.zeros((LANGS * RANK, 2), np.float32)
    lang_of[:, 0] = np.arange(LANGS * RANK) // RANK
    lang_of[:, 1] = np.arange(LANGS * RANK)
    return {
        "squares": np.stack([np.eye(128, dtype=np.float32), lap]),
        "lang_of": lang_of,
        "key_pos": np.tile(np.arange(S, dtype=np.float32), (B, 1)),
    }


def laid_out(name, value):
    rows = value.shape[:-1]
    if name in ("L3_cond_Wq", "L3_cond_Wk", "L3_cond_bq", "L3_cond_bk"):
        return np.moveaxis(value.reshape(*rows, GI, GJ, DH), -3, -1).reshape(value.shape)
    if name in ("L3_cond_Wv", "L3_cond_bv"):
        return value.reshape(*rows, HALVES, GI // HALVES, GJ, DH).swapaxes(-3, -2).reshape(value.shape)
    if name == "L3_cond_Wo":
        return value.reshape(HALVES, GI // HALVES, GJ, DH, D).swapaxes(1, 2).reshape(value.shape)
    return value


def kernel(**inputs):
    import concourse.bacc as bacc
    from concourse.bass_utils import run_bass_kernel_spmd

    nc = bacc.Bacc("TRN2", target_bir_lowering=False, num_devices=1)
    arrays, args = {}, {}
    for name, value in {**flat_inputs(inputs), **shape_constants()}.items():
        value = np.ascontiguousarray(value)
        arrays[f"in_{name}"] = value
        args[name] = nc.dram_tensor(f"in_{name}", value.shape, mybir.dt.from_np(value.dtype), kind="ExternalInput").ap()
    out = nc.dram_tensor("out", (B, S, D), F32, kind="ExternalOutput").ap()
    build(nc, args, out)
    result = run_bass_kernel_spmd(nc, [arrays], core_ids=[0])
    return result.results[0]["out"]
```

```python
from contextlib import ExitStack

import numpy as np
import concourse.bass as bass
from concourse import mybir

F32 = mybir.dt.float32
F32R = mybir.dt.float32r
I32 = mybir.dt.int32
ACT = mybir.ActivationFunctionType
ALU = mybir.AluOpType
AX_X = mybir.AxisListType.X

B, S, D = 16, 128, 128
E, F = 8, 512
NE = E + 1
FC = F // 128
SLOTS = NE * FC
TB = 4
NT = B // TB
N = TB * S
H, DH = 16, 8
SCALE = float(np.float32(1.0) / np.sqrt(DH).astype(np.float32))
LANGS, RANK = 4, 16
LORA_ROWS = LANGS * RANK
NEG = -1.0e30

GI, GJ = 4, 4
ROW_MASK = 3 * DH * GJ
ROW_MAX = ROW_MASK + 1
Q_SLOTS, K_SLOTS = ((0, 2), 1), ((0, 1), 2)
VW = DH + 1
HALVES = 2
VROW = 32 // HALVES
V_STEP = 128 + VROW
PAIR = 2
NP = B // PAIR

FIRST_AUX = []
for _f in range(NT):
    if _f < 2:
        FIRST_AUX.append((("bias", "setup")[_f], 0, 0))
    if _f:
        FIRST_AUX.append(("diffuse", _f, 0))
    FIRST_AUX += [("side", _f, 0), ("query", _f, 0)] + [("natural", _f, b) for b in range(TB)]
FIRST_AUX_SLOT = 4
WARM_PRODUCTS = 4
MIX_AHEAD, SQUARE_AHEAD = 6, 4
AHEAD = 3
LAST_AUX = {(0, 1): 0, (0, 2): 1, (1, 1): 2, (1, 2): 3, (1, 3): 4}
LAST_SPLIT = (0, 3)
EARLY_SCORES = {22 + 4 * b + i: (b, i) for b in range(2) for i in range(4)}
EARLY_TURN = 31
N_FIRST = 1 + len(FIRST_AUX)
LATER_AUX = ["lora_a", "lora_b", "key", "value", "x_natural"]
LATER_SLOT = {3: 0, 5: 1, 9: 2, 11: 3, 13: 4}
ACT_SLOT = {7: 1, 10: 2}
LAST_ROUND = SLOTS - 2
SPLIT_SLOT = 8


def build(nc, a, out):
    with ExitStack() as ctx:
        def sb(name, shape, dt=F32):
            return ctx.enter_context(nc.sbuf_tensor(name, shape, dt))

        def sem(name):
            return ctx.enter_context(nc.semaphore(name))

        def dram(name, shape):
            return nc.dram_tensor(name, shape, F32, kind="Internal").ap()

        q_rows = dram("q_rows", (ROW_MASK, GI, B * S))
        k_rows = dram("k_rows", (ROW_MASK + 1, GI, B * S))
        mask_row = dram("mask_row", (B, S))
        v_d = dram("v_d", (B, S, H * VW + D))
        v_prev_d, v_self_d = v_d[:, :, 0:H * VW], v_d[:, :, H * VW:]
        x3_d = dram("x3_d", (B, S, D))

        squares = sb("squares", [128, 2, 128])
        ident, lap_t = squares[:, 0], squares[:, 1]
        z_all = sb("z_all", [128, 3, B])
        probs_b = sb("probs_b", [128, B * E])
        shared_b = sb("shared_b", [128, B])
        one_minus = sb("one_minus", [128, B])
        gates = sb("gates", [128, NE, B])
        w_raw4 = sb("w_raw4", [128, 4, D])
        w_qkv_h = sb("w_qkv_h", [128, 3, D], F32R)
        w_qkv_l = sb("w_qkv_l", [128, 3, D], F32R)
        bias_nat = sb("bias_nat", [128, 4, D])
        bias_kp = sb("bias_kp", [128, D])
        cols = sb("cols", [128, 4])
        z_own = sb("z_own", [128, B])
        lora_a_nat = sb("lora_a_nat", [64, D])
        lora_b_nat = sb("lora_b_nat", [128, LANGS, RANK])
        lora_a_t = sb("lora_a_t", [128, 64])
        lora_b_t = sb("lora_b_t", [LORA_ROWS + LANGS, D])
        lang_i = sb("lang_i", [LORA_ROWS + LANGS, B], I32)
        lang_f = sb("lang_f", [LORA_ROWS + LANGS, B])
        lang_of = sb("lang_of", [LORA_ROWS + LANGS, 1])
        lang_sel = sb("lang_sel", [LORA_ROWS + LANGS, B])
        len_i = sb("len_i", [B, 1], I32)
        len_f = sb("len_f", [B, 1])
        key_pos = sb("key_pos", [B, S])
        mask_sb = sb("mask_sb", [B, S])
        self_score = sb("self_score", [128, B, H])

        warm = sb("warm", [128, 2])
        w_raw = [sb(f"w_raw{n}", [128, F]) for n in range(3)]
        x1 = sb("x1", [128, NT, TB, S])
        x1_hi = sb("x1_hi", [128, NT, N], F32R)
        x1_lo = sb("x1_lo", [128, NT, N], F32R)
        act_p = [sb(f"act_p{n}", [128, N]) for n in range(3)]
        act_hi = [sb(f"act_hi{n}", [128, N], F32R) for n in range(3)]
        act_lo = [sb(f"act_lo{n}", [128, N], F32R) for n in range(3)]
        xg = sb("xg", [128, TB, S])
        xg_hi = [sb(f"xg_hi{n}", [128, N], F32R) for n in range(3)]
        xg_lo = [sb(f"xg_lo{n}", [128, N], F32R) for n in range(3)]
        x_in = sb("x_in", [128, TB, D])
        side_in = sb("side_in", [128, TB, D])
        mix = sb("mix", [128, TB, S])
        mix_own = sb("mix_own", [128, TB, S])
        dif_a = sb("dif_a", [128, TB, D])
        dif_b = sb("dif_b", [128, TB, D])
        in_hi = sb("in_hi", [128, N], F32R)
        in_lo = sb("in_lo", [128, N], F32R)
        rows_hi = sb("rows_hi", [128, N], F32R)
        rows_lo = sb("rows_lo", [128, N], F32R)
        stage = sb("stage", [128, 2 * 3 * D])
        nat = [stage[:, n * 3 * D:(n + 1) * 3 * D].rearrange("p (k d) -> p k d", k=3) for n in range(2)]
        qk_prod = [sb(f"qk_prod{n}", [128, D]) for n in range(2)]
        b_diag = stage[:, 0:2 * D].rearrange("p (k d) -> p k d", k=2)
        b_cols = stage[:, 2 * D:4 * D].rearrange("p (k d) -> p k d", k=2)
        b_sum = stage[:, 4 * D:5 * D]
        x3_t = side_in
        x3_stage = mix
        low_sel = dif_a[0:LORA_ROWS + LANGS]
        v_stage = stage[:, 0:TB * H * VW].rearrange("p (b h w) -> p b h w", b=TB, h=H)

        phase1 = ExitStack()

        def sb1(name, shape, dt=F32):
            return phase1.enter_context(nc.sbuf_tensor(name, shape, dt))

        w_split = sb1("w_split", [128, NE, 2, 3, F], F32R)
        phase1.close()
        w_hi, w_lo = w_split[:, :, 0], w_split[:, :, 1]
        phase2 = ExitStack()

        def sb2(name, shape, dt=F32):
            return phase2.enter_context(nc.sbuf_tensor(name, shape, dt))

        max_key = [sb2(f"max_key{n}", [128, GI, GJ]) for n in range(2)]
        max_all = [sb2(f"max_all{n}", [128, GI, GJ]) for n in range(2)]
        neg_max = [sb2(f"neg_max{n}", [128, 2, H]) for n in range(2)]
        max_rows = [sb2(f"max_rows{n}", [2 * H, S]) for n in range(2)]
        self_arg = [sb2(f"self_arg{n}", [128, H]) for n in range(2)]
        self_exp = [sb2(f"self_exp{n}", [128, H]) for n in range(4)]
        SMALLS = 2 * (GI * GJ + GI * GJ + 2 * H + S + H) + 4 * H
        k_blocks, q_plain, q_blocks, k_plain = [], [], [], []
        for blocks, plain, names in ((k_blocks, q_plain, ("k_blocks", "q_plain")), (q_blocks, k_plain, ("q_blocks", "k_plain"))):
            for n in range(2):
                blocks.append(sb2(f"{names[0]}{n}", [128, GI, GJ, PAIR * S], F32R))
                plain.append(sb2(f"{names[1]}{n}", [128, GI, PAIR * S], F32R))
        FILLS, end = [], SMALLS
        for blocks, plain in ((k_blocks, q_plain), (q_blocks, k_plain)):
            for n in range(2):
                for tile, constant in ((blocks[n], 0.0), (plain[n], 1.0)):
                    end += int(np.prod(tile.shape[1:]))
                    FILLS.append((tile, constant, -(-end // (2 * 3 * F))))
        probs_t = [sb2(f"probs_t{n}", [128, GJ, S]) for n in range(4)]
        v_both = [sb2(f"v_both{n}", [128, PAIR, H * VW + D]) for n in range(2)]
        v_prev = [v[:, :, 0:H * VW].rearrange("p b (h w) -> p b h w", w=VW) for v in v_both]
        v_self = [v[:, :, H * VW:].rearrange("p b (h r) -> p b h r", r=DH) for v in v_both]
        x3_nat = [sb2(f"x3_nat{n}", [128, PAIR, D]) for n in range(2)]
        v_blocks = [sb2(f"v_blocks{n}", [128, GI * V_STEP]) for n in range(2)]
        pv_own = [sb2(f"pv_own{n}", [128, HALVES, S]) for n in range(2)]
        v_self_w = [sb2(f"v_self_w{n}", [128, H, DH]) for n in range(2)]
        denom = [sb2(f"denom{n}", [128, H]) for n in range(2)]
        rdenom = [sb2(f"rdenom{n}", [128, H]) for n in range(2)]
        numer = [sb2(f"numer{n}", [128, H, DH]) for n in range(2)]
        attn = [sb2(f"attn{n}", [128, H, DH]) for n in range(2)]
        attn_t = [sb2(f"attn_t{n}", [128, D]) for n in range(2)]
        ctx.enter_context(phase2)
        def bank(name):
            return nc.psum_tensor(name, [128, 512], F32)

        phase1p = ExitStack()
        g_ps = [phase1p.enter_context(bank(f"g_ps{n}")) for n in range(3)]
        u_ps = [phase1p.enter_context(bank(f"u_ps{n}")) for n in range(3)]
        acc_ps = phase1p.enter_context(bank("acc_ps"))
        aux_ps = phase1p.enter_context(bank("aux_ps"))
        phase1p.close()
        s_ps = [ctx.enter_context(bank(f"s_ps{n}")) for n in range(2)]
        st_ps = [ctx.enter_context(bank(f"st_ps{n}")) for n in range(2)]
        pv_ps = [ctx.enter_context(bank(f"pv_ps{n}")) for n in range(2)]
        out_ps = ctx.enter_context(bank("out_ps"))
        max_ps = ctx.enter_context(bank("max_ps"))

        squares_loaded, z_loaded = sem("squares_loaded"), sem("z_loaded")
        warm_set = sem("warm_set")
        first_split = sem("first_split")
        z_ready, squared, mix_step = sem("z_ready"), sem("squared"), sem("mix_step")
        small_loaded = sem("small_loaded")
        x_loaded = sem("x_loaded")
        side_loaded = sem("side_loaded")
        w_loaded = [sem(f"w_loaded{n}") for n in range(3)]
        w_hi_done, w_lo_done = sem("w_hi_done"), sem("w_lo_done")
        gate_loaded, gates_ready = sem("gate_loaded"), sem("gates_ready")
        self_summed = sem("self_summed")
        ones_set = sem("ones_set")
        proj_hi, proj_ready = sem("proj_hi"), sem("proj_ready")
        mask_ready = sem("mask_ready")
        mask_stored = sem("mask_stored")
        dif_step, z_step, gate_step, small_cast = sem("dif_step"), sem("z_step"), sem("gate_step"), sem("small_cast")
        mix_ready = sem("mix_ready")
        dif_ready = sem("dif_ready")
        aux_written, aux_rounded, aux_drained = sem("aux_written"), sem("aux_rounded"), sem("aux_drained")
        prod_made = sem("prod_made")
        rows_stored = sem("rows_stored")
        self_stored = [sem(f"self_stored{n}") for n in range(2)]
        later_stored = sem("later_stored")
        xg_made, xg_rounded, xg_ready = sem("xg_made"), sem("xg_rounded"), sem("xg_ready")
        g_written, u_written = sem("g_written"), sem("u_written")
        silu_done, prod_done = sem("silu_done"), sem("prod_done")
        act_hi_done, act_lo_done = sem("act_hi_done"), sem("act_lo_done")
        down_done = sem("down_done")
        acc_written, acc_drained = sem("acc_written"), sem("acc_drained")
        x3_ready = sem("x3_ready")
        in_rounded, in_lo_ready = sem("in_rounded"), sem("in_lo_ready")
        cols_spread = sem("cols_spread")

        blocks_filled, ones_placed = sem("blocks_filled"), sem("ones_placed")
        first_loaded = [sem(f"first_loaded{n}") for n in range(2)]
        second_loaded = [sem(f"second_loaded{n}") for n in range(2)]
        v_loaded = [sem(f"v_loaded{n}") for n in range(2)]
        x3_loaded = [sem(f"x3_loaded{n}") for n in range(2)]
        max_placed = [sem(f"max_placed{n}") for n in range(2)]
        s_written, max_done = sem("s_written"), sem("max_done")
        max_split = sem("max_split")
        max_turned, max_copied = sem("max_turned"), sem("max_copied")
        st_written, exp_done = sem("st_written"), sem("exp_done")
        v_placed, v_zeroed = sem("v_placed"), sem("v_zeroed")
        pv_written = sem("pv_written")
        pv_taken = [sem(f"pv_taken{n}") for n in range(HALVES)]
        pv_turned = sem("pv_turned")
        self_exp_done = sem("self_exp_done")
        self_weighted = sem("self_weighted")
        attn_done = sem("attn_done")
        attn_turned, attn_copied = sem("attn_turned"), sem("attn_copied")
        out_written, out_ready = sem("out_written"), sem("out_ready")
        out_stored = [sem(f"out_stored{n}") for n in range(2)]
        small_step, norm_step = sem("small_step"), sem("norm_step")
        self_arg_ready = sem("self_arg_ready")
        bias_done = sem("bias_done")

        N_SMALL = 10

        def vec(ap, p):
            return ap.unsqueeze(0).to_broadcast([p, ap.shape[0]])

        def part_src(w):
            e, k = divmod(w, 3)
            src = (a["L1_cond_" + "W" + "gud"[k]][e] if e < E else a["L1_cond_" + "S" + "gud"[k]])
            return src.rearrange("(c p) d -> p c d", p=128) if k == 2 else src

        def part_raw(w):
            t = w_raw[w % 3][:]
            return t.rearrange("p (c d) -> p c d", c=FC) if w % 3 == 2 else t

        def blockwise(t):
            return t.rearrange("b s d -> s b d")

        def aux_of(kind, f, b=0):
            return 0 if (kind, f) == ("diffuse", 0) else 1 + FIRST_AUX.index((kind, f, b))

        def first_at(k):
            n = k - FIRST_AUX_SLOT
            return [FIRST_AUX[n]] if 0 <= n < len(FIRST_AUX) else []

        def slot_of(kind, f):
            return FIRST_AUX_SLOT + FIRST_AUX.index((kind, f, 0))

        def rounded_of(kind, f):
            kinds = [("diffuse", 0, 0)] + FIRST_AUX
            return sum(s[0] in ("diffuse", "side", "query") for s in kinds[:aux_of(kind, f) + 1])

        N_ROUNDED = rounded_of("query", NT - 1)
        LAST_STEP = N_FIRST + (NT - 1) * len(LATER_AUX) + 1

        def loaded(b, n, dmas):
            return (b - n) * (4 * dmas) + 16 * dmas * (n // 4 + 1)

        def placed(b, n):
            return (b - n) * 16 + 32 * (n // 2 + 1)

        def wait(eng, semaphore, value):
            if not isinstance(value, int) or value > 0:
                eng.wait_ge(semaphore, value)

        block = ctx.enter_context(nc.Block())

        @block.sync
        def _(sp):
            def load_part(w):
                if w >= 3:
                    sp.wait_ge(w_lo_done, w - 2)
                sp.dma_start(part_raw(w), part_src(w)).then_inc(w_loaded[w % 3], 16)

            def load_x(f):
                if f:
                    sp.wait_ge(aux_written, aux_of("diffuse", f - 1) + 1)
                sp.dma_start(x_in[:], blockwise(a["x"][TB * f:TB * f + TB])).then_inc(x_loaded, 16)

            def load_side(f):
                if f:
                    sp.wait_ge(aux_written, aux_of("side", f - 1) + 1)
                sp.dma_start(side_in[:], blockwise(a["fside_BxSxS_0"][TB * f:TB * f + TB])).then_inc(side_loaded, 16)

            def store_rows(dst, tok, places):
                of_place = dst[0:ROW_MASK].rearrange("(j s r) i n -> j s (r i) n", j=GJ, s=3)
                his, lo = places
                for s in his:
                    sp.dma_start(of_place[:, s, :, tok], rows_hi[:].bitcast(F32)).then_inc(rows_stored, 16)
                sp.dma_start(of_place[:, lo, :, tok], rows_lo[:].bitcast(F32)).then_inc(rows_stored, 16)

            def later_stores(t, n):
                sp.wait_ge(aux_drained, n + 3)
                store_rows(k_rows, bass.ds(t * N, N), K_SLOTS)
                sp.wait_ge(aux_drained, n + 4)
                sp.dma_start(blockwise(v_prev_d[bass.ds(t * TB, TB)]),
                             v_stage.rearrange("p b h w -> p b (h w)")).then_inc(later_stored, 16)
                sp.wait_ge(aux_drained, n + 5)
                sp.dma_start(blockwise(x3_d[bass.ds(t * TB, TB)]), x3_stage[:]).then_inc(later_stored, 16)

            load_x(0)
            sp.dma_start(squares[:], a["squares"].rearrange("k p s -> p k s")).then_inc(squares_loaded, 16)
            for w in range(3):
                load_part(w)

            def small(dst, src):
                sp.dma_start(dst, src).then_inc(small_loaded, 16)

            small(w_raw4[:], a["w_proj"].rearrange("k p d -> p k d"))
            small(bias_nat[:].rearrange("p k d -> p (k d)"), vec(a["b_proj"], 128))
            small(cols[:, 2:4], a["b_in"])
            small(lora_a_nat[:], a["L2_cond_lora_A"].rearrange("l r d -> (l r) d"))
            small(lora_b_nat[:], a["L2_cond_lora_B"].rearrange("l d r -> d l r"))
            small(lora_b_t[LORA_ROWS:], a["L2_cond_lang_embed"])
            small(lang_i[:], vec(a["itok_B_0_3"], LORA_ROWS + LANGS))
            small(lang_of[:], a["lang_of"])
            small(len_i[:], a["itok_B_18_1004"].unsqueeze(1))
            small(key_pos[:], a["key_pos"])
            load_side(0)
            for w in range(3, 3 + AHEAD):
                load_part(w)
            load_x(1)
            for k in range(SLOTS):
                e, c = divmod(k + AHEAD, FC)
                if e + 1 < NE and c < 3:
                    load_part(3 * (e + 1) + c)
                for step in first_at(k - 1):
                    kind, f, b = step
                    n = aux_of(*step)
                    if kind == "diffuse" and f + 1 < NT:
                        load_x(f + 1)
                    if kind == "query":
                        sp.wait_ge(aux_drained, n + 1)
                        store_rows(q_rows, bass.ds(f * N, N), Q_SLOTS)
                        if f + 1 < NT:
                            load_side(f + 1)
                    if kind == "natural":
                        sp.wait_ge(aux_drained, n + 1)
                        sp.dma_start(v_self_d[TB * f + b], nat[b % 2][:, 2]).then_inc(self_stored[b % 2], 16)
                if k == FIRST_AUX_SLOT:
                    sp.wait_ge(mask_ready, 1)
                    sp.dma_start(mask_row, mask_sb[:]).then_inc(mask_stored, 16)
            sp.wait_ge(mask_stored, 16)
            sp.dma_start(k_rows[ROW_MASK:], mask_row.rearrange("b s -> (b s)").unsqueeze(0).unsqueeze(0)
                         .to_broadcast([1, GI, B * S])).then_inc(later_stored, 16)
            with sp.Fori(1, NT) as t:
                later_stores(t - 1, (t - 1) * len(LATER_AUX) + N_FIRST)

            def load_blocks(dst, src, tok, semaphore):
                for j in range(GJ):
                    r = slice(3 * DH * j, 3 * DH * (j + 1))
                    sp.dma_start(dst[r, :, j].bitcast(F32), src[r, :, tok]).then_inc(semaphore, 16)

            def load_first(p, m):
                tok = bass.ds(p * PAIR * S, PAIR * S)
                load_blocks(k_blocks[m % 2], k_rows, tok, first_loaded[m % 2])
                sp.dma_start(k_blocks[m % 2][ROW_MASK:ROW_MASK + 1].rearrange("p i j n -> p (i j) n").bitcast(F32),
                             mask_row.rearrange("b s -> (b s)").unsqueeze(0).unsqueeze(0)[:, :, tok]
                             .to_broadcast([1, H, PAIR * S])).then_inc(first_loaded[m % 2], 16)
                sp.dma_start(q_plain[m % 2][0:ROW_MASK].bitcast(F32), q_rows[:, :, tok]).then_inc(first_loaded[m % 2], 16)

            def load_second(p, m):
                tok = bass.ds(p * PAIR * S, PAIR * S)
                load_blocks(q_blocks[m % 2], q_rows, tok, second_loaded[m % 2])
                sp.dma_start(k_plain[m % 2][0:ROW_MASK + 1].bitcast(F32), k_rows[:, :, tok])\
                    .then_inc(second_loaded[m % 2], 16)

            def load_v(p, m):
                sp.dma_start(v_both[m % 2][:], blockwise(v_d[bass.ds(p * PAIR, PAIR)])).then_inc(v_loaded[m % 2], 16)

            def load_x3(p, m):
                sp.dma_start(x3_nat[m % 2][:], blockwise(x3_d[bass.ds(p * PAIR, PAIR)])).then_inc(x3_loaded[m % 2], 16)

            def store_out(p, m):
                sp.wait_ge(out_ready, p * PAIR + PAIR)
                sp.dma_start(blockwise(out[bass.ds(p * PAIR, PAIR)]), x3_nat[m % 2][:]).then_inc(out_stored[m % 2], 16)

            def step(p, m, out=True, first=True, second=True, x3=True):
                if out:
                    store_out(p, m)
                if second:
                    if not out:
                        sp.wait_ge(v_placed, 2 * PAIR)
                    sp.wait_ge(self_weighted, p * PAIR + 2 * PAIR)
                    load_v(p + 3, m + 1)
                if first:
                    sp.wait_ge(s_written, (p * PAIR + 3 * PAIR) * GI)
                    load_first(p + 4, m)
                if second:
                    sp.wait_ge(st_written, (p * PAIR + 2 * PAIR) * GI)
                    load_second(p + 3, m + 1)
                if x3:
                    sp.wait_ge(out_stored[m % 2], (p - m) * 8 + 16)
                    load_x3(p + 2, m)

            sp.wait_ge(rows_stored, 16 * 3 * (2 * NT - 1))
            sp.wait_ge(later_stored, 16 * (1 + 2 * (NT - 1)))
            for m in range(2):
                sp.wait_ge(blocks_filled, 2 * (m + 1))
                load_first(m, m)
            for m in range(2):
                sp.wait_ge(blocks_filled, 2 * (m + 3))
                sp.dma_start(q_blocks[m][ROW_MASK:ROW_MASK + 1].rearrange("p i j n -> p (i j) n").bitcast(F32),
                             k_plain[m][127:128, 0:1].bitcast(F32).to_broadcast([1, H, PAIR * S])).then_inc(ones_placed, 16)
                load_second(m, m)
            for stored in self_stored:
                sp.wait_ge(stored, 16 * B // 2)
            sp.wait_ge(down_done, SLOTS * NT)
            for m in range(2):
                load_v(m, m)
                load_x3(m, m)
            sp.wait_ge(s_written, PAIR * GI)
            load_first(2, 0)
            later_stores(NT - 1, (NT - 1) * len(LATER_AUX) + N_FIRST)
            sp.wait_ge(rows_stored, 16 * 3 * 2 * NT)
            sp.wait_ge(later_stored, 16 * (1 + 2 * NT))
            step(-1, 1, out=False, x3=False)
            with sp.Fori(0, NP // 2 - 2) as g:
                for m in range(2):
                    step(g * 2 + m, m)
            for p in range(NP - 4, NP):
                step(p, p % 2, first=p + 4 < NP, second=p + 3 < NP, x3=p + 2 < NP)
            for stored in out_stored:
                sp.wait_ge(stored, 16 * NP // 2)

        @block.tensor
        def _(pe):
            mm, turn = nc.tensor.matmul, nc.tensor.transpose

            def three(dst, w_h, w_l, x_h, x_l, start=True, stop=True):
                mm(dst, w_h, x_h, start=start, stop=False)
                mm(dst, w_h, x_l, start=False, stop=False)
                return mm(dst, w_l, x_h, start=False, stop=stop)

            def diffuse(f):
                pe.wait_ge(dif_ready, f + 1)
                pe.wait_ge(mix_ready, f + 1)
                for b in range(TB):
                    dst = aux_ps[:, b * S:(b + 1) * S]
                    mm(dst, dif_a[:, b], ident, start=True, stop=False)
                    last = mm(dst, x_in[:, b], mix[:, b], start=False, stop=True)
                last.then_inc(aux_written, 1)

            def first_step(kind, f, b):
                n = aux_of(kind, f, b)
                pe.wait_ge(aux_drained, n)
                if kind == "diffuse":
                    diffuse(f)
                elif kind == "bias":
                    pe.wait_ge(cols_spread, 1)
                    mm(aux_ps[:, 0:2 * D], b_cols[:, 0], w_raw4[:, 0:2].rearrange("p k d -> p (k d)"), start=True, stop=True)
                    mm(aux_ps[:, 2 * D:3 * D], b_cols[:, 1], w_raw4[:, 1], start=True, stop=True).then_inc(aux_written, 1)
                elif kind == "setup":
                    turn(aux_ps[:, 0:64], lora_a_nat[:], squares[0:64, 0, 0:64])
                    turn(aux_ps[0:64, 128:256], lora_b_nat[:].rearrange("p l r -> p (l r)"), ident)\
                        .then_inc(aux_written, 1)
                elif kind == "side":
                    pe.wait_ge(side_loaded, 16 * (f + 1))
                    for c in range(TB):
                        last = turn(aux_ps[:, c * S:(c + 1) * S], side_in[:, c], ident)
                    last.then_inc(aux_written, 1)
                elif kind == "query":
                    if f == 0:
                        pe.wait_ge(proj_ready, 2)
                    three(aux_ps[:], w_qkv_h[:, 0], w_qkv_l[:, 0], in_hi[:], in_lo[:]).then_inc(aux_written, 1)
                else:
                    tok = slice(b * S, (b + 1) * S)
                    three(aux_ps[:, 0:3 * D], in_hi[:, tok], in_lo[:, tok], w_qkv_h[:].rearrange("p k d -> p (k d)"),
                          w_qkv_l[:].rearrange("p k d -> p (k d)")).then_inc(aux_written, 1)

            def later_step(m, t):
                pe.wait_ge(aux_drained, t * len(LATER_AUX) + N_FIRST + m)
                kind = LATER_AUX[m]
                if kind == "lora_a":
                    pe.wait_ge(acc_drained, t + 1)
                    last = mm(aux_ps[0:64, :], lora_a_t[:], x1[:, t].rearrange("p b s -> p (b s)"), start=True, stop=True)
                elif kind == "lora_b":
                    last = mm(aux_ps[:], lora_b_t[:], low_sel.rearrange("p b s -> p (b s)"), start=True, stop=True)
                elif kind == "key":
                    pe.wait_ge(in_lo_ready, t + 1)
                    last = three(aux_ps[:], w_qkv_h[:, 1], w_qkv_l[:, 1], in_hi[:], in_lo[:])
                elif kind == "value":
                    for b in range(TB):
                        tok = slice(b * S, (b + 1) * S)
                        last = three(aux_ps[:, tok], in_hi[:, tok], in_lo[:, tok], w_qkv_h[:, 2], w_qkv_l[:, 2])
                else:
                    for b in range(TB):
                        last = turn(aux_ps[:, b * S:(b + 1) * S], x3_t[:, b], ident)
                last.then_inc(aux_written, 1)

            def half(n):
                return slice(n % 2 * S, (n % 2 + 1) * S)

            def scores(b, n, i, bank=None):
                if i == 0:
                    pe.wait_ge(first_loaded[n // 2 % 2], loaded(b, n, 6))
                wait(pe, max_done, b * GI + i - (1 if bank is None else 0))
                mm((s_ps[i % 2] if bank is None else bank)[:], q_plain[n // 2 % 2][0:ROW_MASK + 1, i, half(n)],
                   k_blocks[n // 2 % 2][0:ROW_MASK + 1, i, :, half(n)], start=True, stop=True).then_inc(s_written, 1)

            def turn_max(b, n):
                pe.wait_ge(max_split, b + 1)
                wait(pe, max_copied, b)
                turn(max_ps[0:2 * H, 0:S], neg_max[n % 2][:].rearrange("p c h -> p (c h)"), ident)\
                    .then_inc(max_turned, 1)

            def gate_product(t, k):
                e, c = divmod(k, FC)
                chunk = slice(c * 128, (c + 1) * 128)
                if isinstance(t, int) and c == 0:
                    pe.wait_ge(w_lo_done, 3 * e + 1)
                wait(pe, silu_done, t * SLOTS + k - 2)
                three(g_ps[k % 3][:], w_hi[:, e, 0, chunk], w_lo[:, e, 0, chunk], x1_hi[:, t], x1_lo[:, t])\
                    .then_inc(g_written, 1)

            def up_product(t, k):
                e, c = divmod(k, FC)
                chunk = slice(c * 128, (c + 1) * 128)
                if c == 0:
                    if isinstance(t, int):
                        pe.wait_ge(w_lo_done, 3 * e + 2)
                    pe.wait_ge(xg_ready, t * NE + e + 1)
                wait(pe, prod_done, t * SLOTS + k - 2)
                three(u_ps[k % 3][:], w_hi[:, e, 1, chunk], w_lo[:, e, 1, chunk], xg_hi[e % 3][:], xg_lo[e % 3][:])\
                    .then_inc(u_written, 1)

            def down_product(t, k):
                e, c = divmod(k, FC)
                chunk = slice(c * 128, (c + 1) * 128)
                if isinstance(t, int) and t == 0 and c == 0:
                    pe.wait_ge(w_lo_done, 3 * e + 3)
                if k == 0:
                    wait(pe, acc_drained, t)
                pe.wait_ge(act_lo_done, t * SLOTS + k + 1)
                last = three(acc_ps[:], w_hi[:, e, 2, chunk], w_lo[:, e, 2, chunk], act_hi[k % 3][:], act_lo[k % 3][:],
                             start=(k == 0), stop=(k == SLOTS - 1))
                last.then_inc(down_done, 1)

            pe.wait_ge(warm_set, 2)
            for _ in range(WARM_PRODUCTS):
                mm(g_ps[0][:], act_p[0][:, 0:128], act_p[0][:], start=True, stop=True)
            pe.wait_ge(squares_loaded, 16)
            diffuse(0)
            pe.wait_ge(first_split, 1)
            for k in range(3):
                gate_product(0, k)
            for k in range(SLOTS):
                if k >= 3:
                    gate_product(0, k)
                up_product(0, k)
                if k >= 2:
                    down_product(0, k - 2)
                if k == FIRST_AUX_SLOT - 1:
                    pe.wait_ge(small_loaded, 16 * N_SMALL)
                for step in first_at(k):
                    first_step(*step)
            def slot(t, k):
                gate_product(t, k)
                up_product(t, k)
                if k in LATER_SLOT:
                    later_step(LATER_SLOT[k], t - 1)
                down_product(*((t, k - 2) if k >= 2 else (t - 1, SLOTS - 2 + k)))

            with pe.Fori(1, NT - 1) as t:
                for k in range(SLOTS):
                    slot(t, k)
            for k in range(SLOTS):
                slot(NT - 1, k)
                if k in EARLY_SCORES:
                    b, i = EARLY_SCORES[k]
                    pe.wait_ge(aux_drained, LAST_STEP - 1)
                    scores(b, b, i, bank=max_ps)
                if k == EARLY_TURN:
                    pe.wait_ge(max_done, 2 * GI)
                    turn_max(0, 0)
            for k in range(2):
                down_product(NT - 1, SLOTS - 2 + k)

            def scores_t(b, n, i):
                if i == 0:
                    pe.wait_ge(second_loaded[n // 2 % 2], loaded(b, n, 5))
                    pe.wait_ge(max_placed[n % 2], placed(b, n))
                wait(pe, exp_done, b * GI + i - 1)
                mm(st_ps[i % 2][:], k_plain[n // 2 % 2][0:ROW_MAX + 2, i, half(n)],
                   q_blocks[n // 2 % 2][0:ROW_MAX + 2, i, :, half(n)], start=True, stop=True).then_inc(st_written, 1)

            def weigh(b, n, i):
                if i == 0:
                    pe.wait_ge(v_placed, b * 2 + 2)
                if i % 2 == 0:
                    wait(pe, pv_taken[i // 2], b)
                pe.wait_ge(exp_done, b * GI + i + 1)
                window = V_STEP * i - VROW * (i % 2)
                mm(pv_ps[i // 2][:], v_blocks[n % 2][:, window:window + 128], probs_t[i][:].rearrange("p j s -> p (j s)"),
                   start=(i % 2 == 0), stop=(i % 2 == 1)).then_inc(pv_written, 1)

            def turn_pv(b, n):
                for taken in pv_taken:
                    pe.wait_ge(taken, b + 1)
                wait(pe, out_ready, b)
                for half in range(HALVES):
                    last = turn(out_ps[:, half * D:(half + 1) * D], pv_own[n % 2][:, half], ident)
                last.then_inc(pv_turned, 1)

            def turn_attn(b, n):
                pe.wait_ge(attn_done, b + 1)
                turn(out_ps[:, 2 * D:3 * D], attn[n % 2][:].rearrange("p h r -> p (h r)"), ident).then_inc(attn_turned, 1)

            def project(b, n):
                pe.wait_ge(attn_copied, b + 1)
                mm(out_ps[:, 3 * D:4 * D], attn_t[n % 2][:], w_raw4[:, 3], start=True, stop=True).then_inc(out_written, 1)

            def body(b, n, first=False, s_next=True, turn_next=True):
                for i in range(GI):
                    if s_next:
                        scores(b + 2, n + 2, i)
                    if not first and i < 2:
                        weigh(b - 1, n - 1, i + 2)
                    if n >= 2 and i == 0:
                        project(b - 2, n - 2)
                    scores_t(b, n, i)
                    if turn_next and i == 0:
                        turn_max(b + 1, n + 1)
                    if i >= 2:
                        weigh(b, n, i - 2)
                    if not first and i == 2:
                        turn_pv(b - 1, n - 1)
                    if not first and i == 3:
                        turn_attn(b - 1, n - 1)
                    if isinstance(b, int) and (b, i) in LAST_AUX:
                        pe.wait_ge(max_copied, b + 2)
                        later_step(LAST_AUX[b, i], NT - 1)

            pe.wait_ge(max_copied, 1)
            pe.wait_ge(ones_placed, 32)
            body(0, 0, first=True)
            pe.wait_ge(aux_drained, LAST_STEP + 1)
            body(1, 1)
            pe.wait_ge(aux_drained, LAST_STEP + 4)
            with pe.Fori(0, B // TB - 1) as g:
                for n in range(2, TB + 2):
                    body(g * TB + n, n)
            for b in range(B - 2, B):
                body(b, b % TB, s_next=b + 2 < B, turn_next=b + 1 < B)
            for i in range(2, GI):
                weigh(B - 1, B - 1, i)
            project(B - 2, B - 2)
            turn_pv(B - 1, B - 1)
            turn_attn(B - 1, B - 1)
            project(B - 1, B - 1)

        @block.scalar
        def _(act):
            activation = nc.scalar.activation

            def small(dst, src, semaphore):
                act.dma_start(dst, src).then_inc(semaphore, 16)

            small(z_all[:].rearrange("p k b -> p (k b)"), vec(a["z"], 128), z_loaded)
            small(probs_b[:], a["fside_Bx8_0"].rearrange("b e -> (b e)").unsqueeze(0).to_broadcast([128, B * E]), gate_loaded)
            small(shared_b[:], vec(a["condB_sharedgateprob"], 128), gate_loaded)

            act.wait_ge(warm_set, 1)
            activation(warm[:, 1:2], warm[:, 0:1], ACT.Silu)

            def split_part(w):
                act.wait_ge(w_loaded[w % 3], 16 * (w // 3 + 1))
                activation(w_hi[:, w // 3, w % 3], w_raw[w % 3][:], ACT.Identity).then_inc(w_hi_done, 1)

            def first_step(kind, f, b):
                n = aux_of(kind, f, b)
                if kind in ("natural", "setup", "bias"):
                    return
                act.wait_ge(aux_written, n + 1)
                if kind == "diffuse":
                    activation(x1_hi[:, f], aux_ps[:], ACT.Identity)
                    activation(x1[:, f].rearrange("p b s -> p (b s)"), aux_ps[:], ACT.Identity).then_inc(aux_rounded, 1)
                elif kind == "side":
                    activation(in_hi[:], aux_ps[:], ACT.Identity).then_inc(aux_rounded, 1)
                else:
                    wait(act, rows_stored, 48 * f)
                    activation(rows_hi[:], aux_ps[:], ACT.Identity, bias=cols[:, 0:1]).then_inc(aux_rounded, 1)

            def later_step(m, t):
                n = t * len(LATER_AUX) + N_FIRST + m
                if LATER_AUX[m] == "lora_b":
                    act.wait_ge(aux_drained, n + 1)
                    activation(in_hi[:], x3_t[:].rearrange("p b s -> p (b s)"), ACT.Identity).then_inc(in_rounded, 1)
                elif LATER_AUX[m] == "key":
                    act.wait_ge(aux_written, n + 1)
                    act.wait_ge(rows_stored, t * 48 + 48 * NT)
                    activation(rows_hi[:], aux_ps[:], ACT.Identity, bias=cols[:, 1:2]).then_inc(aux_rounded, 1)

            def silu(t, k):
                wait(act, act_lo_done, t * SLOTS + k - 2)
                act.wait_ge(g_written, t * SLOTS + k + 1)
                activation(act_p[k % 3][:], g_ps[k % 3][:], ACT.Silu).then_inc(silu_done, 1)

            def round_act(t, k):
                wait(act, down_done, t * SLOTS + k - 2)
                act.wait_ge(prod_done, t * SLOTS + k + 1)
                activation(act_hi[k % 3][:], act_p[k % 3][:], ACT.Identity).then_inc(act_hi_done, 1)

            def round_xg(t, e):
                wait(act, u_written, t * SLOTS + (e - 3) * FC + FC)
                act.wait_ge(xg_made, t * NE + e + 1)
                activation(xg_hi[e % 3][:], xg[:].rearrange("p b s -> p (b s)"), ACT.Identity).then_inc(xg_rounded, 1)

            def square(f):
                act.wait_ge(x_loaded, 16 * (f + 1))
                if f:
                    act.wait_ge(dif_ready, f)
                activation(dif_b[:], x_in[:], ACT.Square).then_inc(squared, 1)

            square(0)
            split_part(0)
            split_part(1)
            act.wait_ge(aux_written, 1)
            activation(x1_hi[:, 0], aux_ps[:], ACT.Identity).then_inc(aux_rounded, 1)
            round_xg(0, 0)
            activation(x1[:, 0].rearrange("p b s -> p (b s)"), aux_ps[:], ACT.Identity).then_inc(aux_drained, 1)
            split_part(2)

            def round_projections():
                act.wait_ge(small_loaded, 16 * N_SMALL)
                activation(w_qkv_h[:, 0], w_raw4[:, 0], ACT.Identity, scale=SCALE).then_inc(proj_hi, 1)
                activation(w_qkv_h[:, 1:3], w_raw4[:, 1:3], ACT.Identity).then_inc(proj_hi, 1)

            for k in range(LAST_ROUND):
                e, c = divmod(k, FC)
                for step in first_at(k - 1):
                    first_step(*step)
                silu(0, k)
                if k:
                    round_act(0, k - 1)
                if e + 1 < NE and c == 2:
                    round_xg(0, e + 1)
                if e + 1 < NE and c < 3:
                    split_part(3 * (e + 1) + c)
                if k == 2:
                    round_projections()
                for kind, f, b in first_at(k + SQUARE_AHEAD):
                    if kind == "diffuse":
                        square(f)
            def copy_max(b, n):
                act.wait_ge(max_turned, b + 1)
                if n >= 2:
                    act.wait_ge(max_placed[n % 2], placed(b - 2, n - 2))
                activation(max_rows[n % 2][:], max_ps[0:2 * H, 0:S], ACT.Identity).then_inc(max_copied, 1)

            def last_slots(t, rounds_next=True):
                for k in range(LAST_ROUND, SLOTS):
                    silu(t, k)
                    round_act(t, k - 1)
                    if k == LAST_ROUND and rounds_next:
                        round_xg(t + 1, 0)
                    if k == LAST_ROUND and not rounds_next:
                        copy_max(0, 0)

            with act.Fori(1, NT) as t:
                last_slots(t - 1)
                for k in range(LAST_ROUND):
                    e, c = divmod(k, FC)
                    if k in ACT_SLOT:
                        later_step(ACT_SLOT[k], t - 1)
                    silu(t, k)
                    round_act(*((t, k - 1) if k else (t - 1, SLOTS - 1)))
                    if e + 1 < NE and c == 2:
                        round_xg(t, e + 1)
            last_slots(NT - 1, rounds_next=False)
            round_act(NT - 1, SLOTS - 1)

            def exp_self(b, n):
                act.wait_ge(self_arg_ready, b + 1)
                activation(self_exp[n % 4][:], self_arg[n % 2][:], ACT.Exp).then_inc(self_exp_done, 1)

            def exp_scores(b, n, i):
                wait(act, pv_written, (b - 1) * GI + i + 1)
                act.wait_ge(st_written, b * GI + i + 1)
                activation(probs_t[i][:].rearrange("p j s -> p (j s)"), st_ps[i % 2][:], ACT.Exp).then_inc(exp_done, 1)

            def place_values(b, n):
                act.wait_ge(v_loaded[n // 2 % 2], loaded(b, n, 1))
                wait(act, pv_written, (b - 1) * GI)
                for half in range(HALVES):
                    to = v_blocks[n % 2][:, 2 * half * V_STEP:2 * (half + 1) * V_STEP].rearrange("p (c x) -> p c x", c=HALVES)
                    activation(to[:, :, 0:128].rearrange("p c (j y) -> p j c y", j=GJ)[:, :, :, 0:VW],
                               v_prev[n // 2 % 2][:, n % 2, half * H // 2:(half + 1) * H // 2]
                               .rearrange("p (j c) w -> p j c w", j=GJ), ACT.Identity).then_inc(v_placed, 1)

            def take_first(b, n):
                act.wait_ge(pv_written, b * GI + 2)
                for j in range(GJ):
                    rows = slice(32 * j, 32 * j + 32)
                    last = activation(pv_own[n % 2][rows, 0], pv_ps[0][rows, j * S:(j + 1) * S], ACT.Identity)
                last.then_inc(pv_taken[0], 1)

            def copy_attn(b, n):
                act.wait_ge(attn_turned, b + 1)
                activation(attn_t[n % 2][:], out_ps[:, 2 * D:3 * D], ACT.Identity).then_inc(attn_copied, 1)

            def body(b, n, first=False, turn_next=True):
                for i in range(GI):
                    exp_scores(b, n, i)
                    if turn_next and i == 0:
                        copy_max(b + 1, n + 1)
                        exp_self(b + 1, n + 1)
                    if not first and i == 0:
                        take_first(b - 1, n - 1)
                    if first and i == 0:
                        act.wait_ge(v_zeroed, 2)
                        place_values(0, 0)
                    if turn_next and i == 1:
                        place_values(b + 1, n + 1)
                    if isinstance(b, int) and (b, i) in LAST_AUX:
                        later_step(LAST_AUX[b, i], NT - 1)
                    if not first and i == 3:
                        copy_attn(b - 1, n - 1)

            exp_self(0, 0)
            body(0, 0, first=True)
            body(1, 1)
            with act.Fori(0, B // TB - 1) as g:
                for n in range(2, TB + 2):
                    body(g * TB + n, n)
            for b in range(B - 2, B):
                body(b, b % TB, turn_next=b + 1 < B)
            take_first(B - 1, B - 1)
            copy_attn(B - 1, B - 1)

        @block.vector
        def _(dve):
            tt, stt, ts = nc.vector.tensor_tensor, nc.vector.scalar_tensor_tensor, nc.vector.tensor_scalar

            def over_s(z):
                return z.unsqueeze(2).to_broadcast([z.shape[0], TB, S])

            def diffuse_part(f, part):
                x = x_in
                z = z_all[:, :, TB * f:TB * f + TB]
                if part == 0:
                    dve.wait_ge(x_loaded, 16 * (f + 1))
                    if f:
                        dve.wait_ge(aux_written, aux_of("diffuse", f - 1) + 1)
                    tt(dif_a[:, :, 1:D - 1], x[:, :, 0:D - 2], x[:, :, 2:D], ALU.add).then_inc(dif_step, 1)
                    ts(dif_a[:, :, 0:D:D - 1], x[:, :, 1:D - 1:D - 3], 2.0, None, ALU.mult).then_inc(dif_step, 1)
                elif part == 1:
                    dve.wait_ge(dif_step, 4 * f + 2)
                    tt(dif_a[:], dif_a[:], over_s(z[:, 0]), ALU.mult).then_inc(dif_step, 1)
                elif part == 2:
                    dve.wait_ge(squared, f + 1)
                    tt(dif_b[:], dif_b[:], over_s(z[:, 2]), ALU.mult).then_inc(dif_step, 1)
                else:
                    dve.wait_ge(dif_step, 4 * f + 4)
                    tt(dif_a[:], dif_a[:], dif_b[:], ALU.subtract).then_inc(dif_ready, 1)

            def first_step(kind, f, b):
                n = aux_of(kind, f, b)
                if kind == "natural":
                    m = TB * f + b
                    dve.wait_ge(aux_written, n + 1)
                    wait(dve, self_stored[b % 2], 16 * (m // 2))
                    wait(dve, prod_made, m - 1)
                    tt(stage[:, b % 2 * 3 * D:(b % 2 + 1) * 3 * D], aux_ps[:, 0:3 * D],
                       bias_nat[:, 0:3].rearrange("p k d -> p (k d)"), ALU.add).then_inc(aux_drained, 1)
                    return
                if kind == "bias":
                    dve.wait_ge(aux_written, n + 1)
                    tt(b_sum, aux_ps[:, 0:D], bias_nat[:, 0], ALU.add).then_inc(bias_done, 1)
                    tt(bias_kp[:], aux_ps[:, 2 * D:3 * D], bias_nat[:, 1], ALU.add).then_inc(bias_done, 1)
                    dve.wait_ge(bias_done, 2)
                    ts(bias_nat[:, 0], b_sum, SCALE, None, ALU.mult).then_inc(bias_done, 1)
                    tt(bias_nat[:, 1], aux_ps[:, D:2 * D], bias_nat[:, 1], ALU.add).then_inc(bias_done, 1)
                    dve.wait_ge(bias_done, 4)
                    tt(b_diag[:, 0], bias_nat[:, 0], ident, ALU.mult).then_inc(bias_done, 1)
                    tt(b_diag[:, 1], bias_kp[:], ident, ALU.mult).then_inc(bias_done, 1)
                    dve.wait_ge(bias_done, 6)
                    nc.vector.tensor_reduce(cols[:, 0:2], b_diag, AX_X, ALU.add).then_inc(aux_drained, 1)
                    return
                if kind == "setup":
                    dve.wait_ge(aux_written, n + 1)
                    nc.vector.tensor_copy(lora_a_t[:], aux_ps[:, 0:64])
                    nc.vector.tensor_copy(lora_b_t[0:LORA_ROWS], aux_ps[0:64, 128:256]).then_inc(aux_drained, 1)
                    return
                dve.wait_ge(aux_rounded, rounded_of(kind, f))
                if kind == "diffuse":
                    tt(x1_lo[:, f], aux_ps[:], x1_hi[:, f].bitcast(F32), ALU.subtract).then_inc(aux_drained, 1)
                elif kind == "side":
                    tt(in_lo[:], aux_ps[:], in_hi[:].bitcast(F32), ALU.subtract).then_inc(aux_drained, 1)
                else:
                    stt(rows_lo[:], aux_ps[:], cols[:, 0:1], rows_hi[:].bitcast(F32), ALU.add, ALU.subtract)\
                        .then_inc(aux_drained, 1)

            def sum_self(f, b):
                m = TB * f + b
                dve.wait_ge(prod_made, m + 1)
                nc.vector.tensor_reduce(self_score[:, m].rearrange("p (i j) -> p i j", i=GI),
                                        qk_prod[b % 2][:].rearrange("p (j r i) -> p i j r", i=GI, j=GJ),
                                        AX_X, ALU.add).then_inc(self_summed, 1)

            def later_step(m, t):
                n = t * len(LATER_AUX) + N_FIRST + m
                kind = LATER_AUX[m]
                flat = x3_t[:].rearrange("p b s -> p (b s)")
                if kind != "key":
                    dve.wait_ge(aux_written, n + 1)
                if kind == "lora_a":
                    nc.vector.tensor_copy(low_sel[LORA_ROWS:], over_s(lang_sel[LORA_ROWS:, bass.ds(t * TB, TB)]))
                    tt(low_sel[0:LORA_ROWS], aux_ps[0:LORA_ROWS].rearrange("p (b s) -> p b s", b=TB),
                       over_s(lang_sel[0:LORA_ROWS, bass.ds(t * TB, TB)]), ALU.mult).then_inc(aux_drained, 1)
                elif kind == "lora_b":
                    tt(flat, x1[:, t].rearrange("p b s -> p (b s)"), aux_ps[:], ALU.add).then_inc(aux_drained, 1)
                elif kind == "key":
                    dve.wait_ge(aux_rounded, t + N_ROUNDED + 1)
                    stt(rows_lo[:], aux_ps[:], cols[:, 1:2], rows_hi[:].bitcast(F32), ALU.add, ALU.subtract)\
                        .then_inc(aux_drained, 1)
                elif kind == "value":
                    dve.wait_ge(ones_set, 1)
                    dve.wait_ge(later_stored, t * 32 + 16)
                    tt(v_stage[:, :, :, 0:DH], aux_ps[:].rearrange("p (b h r) -> p b h r", b=TB, r=DH),
                       bias_nat[:, 2].rearrange("p (h r) -> p h r", r=DH).unsqueeze(1).to_broadcast([128, TB, H, DH]),
                       ALU.add).then_inc(aux_drained, 1)
                else:
                    tt(x3_stage[:], aux_ps[:].rearrange("p (b s) -> p b s", b=TB),
                       bias_nat[:, 3].unsqueeze(1).to_broadcast([128, TB, D]), ALU.add).then_inc(aux_drained, 1)

            def split_input(t):
                dve.wait_ge(in_rounded, t + 1)
                tt(in_lo[:], x3_t[:].rearrange("p b s -> p (b s)"), in_hi[:].bitcast(F32), ALU.subtract).then_inc(in_lo_ready, 1)

            def product(t, k):
                dve.wait_ge(u_written, t * SLOTS + k + 1)
                dve.wait_ge(silu_done, t * SLOTS + k + 1)
                tt(act_p[k % 3][:], act_p[k % 3][:], u_ps[k % 3][:], ALU.mult).then_inc(prod_done, 1)

            def split_act(t, k):
                dve.wait_ge(act_hi_done, t * SLOTS + k + 1)
                tt(act_lo[k % 3][:], act_p[k % 3][:], act_hi[k % 3][:].bitcast(F32), ALU.subtract).then_inc(act_lo_done, 1)

            def add_experts(t):
                dve.wait_ge(down_done, t * SLOTS + SLOTS)
                x = x1[:, t].rearrange("p b s -> p (b s)")
                tt(x, x, acc_ps[:], ALU.add).then_inc(acc_drained, 1)

            nc.vector.memset(warm[:], 0.0).then_inc(warm_set, 1)
            nc.vector.memset(act_p[0][:], 0.0).then_inc(warm_set, 1)
            dve.wait_ge(z_loaded, 16)
            ts(z_own[:], z_all[:, 0], -2.0, 1.0, ALU.mult, ALU.add).then_inc(z_step, 1)
            diffuse_part(0, 0)
            dve.wait_ge(z_step, 1)
            tt(z_own[:], z_own[:], z_all[:, 2], ALU.add).then_inc(z_ready, 1)
            for part in range(1, 4):
                diffuse_part(0, part)
            dve.wait_ge(gate_loaded, 32)
            ts(one_minus[:], shared_b[:], -1.0, 1.0, ALU.mult, ALU.add).then_inc(gate_step, 1)
            dve.wait_ge(gate_step, 1)
            tt(gates[:, 0:E], probs_b[:].rearrange("p (b e) -> p e b", e=E),
               one_minus[:].unsqueeze(1).to_broadcast([128, E, B]), ALU.mult).then_inc(gates_ready, 1)
            nc.vector.tensor_copy(gates[:, E], shared_b[:]).then_inc(gates_ready, 1)
            dve.wait_ge(aux_rounded, 1)
            tt(x1_lo[:, 0], aux_ps[:], x1_hi[:, 0].bitcast(F32), ALU.subtract).then_inc(first_split, 1)
            flat = xg[:].rearrange("p b s -> p (b s)")
            dve.wait_ge(gates_ready, 2)
            tt(xg[:], aux_ps[:].rearrange("p (b s) -> p b s", b=TB), over_s(gates[:, 0, 0:TB]), ALU.mult).then_inc(xg_made, 1)
            dve.wait_ge(xg_rounded, 1)
            tt(xg_lo[0][:], flat, xg_hi[0][:].bitcast(F32), ALU.subtract).then_inc(xg_ready, 1)

            def small_work():
                dve.wait_ge(small_loaded, 16 * N_SMALL)
                nc.vector.tensor_copy(len_f[:], len_i[:])
                nc.vector.tensor_copy(lang_f[:], lang_i[:]).then_inc(small_cast, 1)
                dve.wait_ge(small_cast, 1)
                ts(lang_sel[:], lang_f[:], lang_of[:, 0:1], None, ALU.is_equal)
                ts(mask_sb[:], key_pos[:], len_f[:, 0:1], NEG, ALU.is_ge, ALU.mult).then_inc(mask_ready, 1)
                dve.wait_ge(proj_hi, 2)
                nc.vector.tensor_copy(b_cols, cols[:, 2:4].unsqueeze(2).to_broadcast([128, 2, D])).then_inc(cols_spread, 1)
                stt(w_qkv_l[:, 0], w_raw4[:, 0], SCALE, w_qkv_h[:, 0].bitcast(F32), ALU.mult, ALU.subtract).then_inc(proj_ready, 1)
                tt(w_qkv_l[:, 1:3], w_raw4[:, 1:3], w_qkv_h[:, 1:3].bitcast(F32), ALU.subtract).then_inc(proj_ready, 1)

            for k in range(SLOTS):
                for step in first_at(k - 1):
                    first_step(*step)
                for kind, f, b in first_at(k - 2):
                    if kind == "natural":
                        sum_self(f, b)
                product(0, k)
                if k:
                    split_act(0, k - 1)
                if k == 2:
                    small_work()
                for part in range(4):
                    for kind, f, b in first_at(k + 4 - part):
                        if kind == "diffuse":
                            diffuse_part(f, part)
            for stored in self_stored:
                dve.wait_ge(stored, 16 * B // 2)
            nc.vector.memset(v_stage, 1.0).then_inc(ones_set, 1)
            def max_group(b, n, i, bank=None):
                dve.wait_ge(s_written, b * GI + i + 1)
                nc.vector.tensor_reduce(max_key[n % 2][:, i], (s_ps[i % 2] if bank is None else bank)[:].rearrange("p (j s) -> p j s", j=GJ),
                                        AX_X, ALU.max).then_inc(max_done, 1)

            def split_max(b, n):
                own = self_score[:, b].rearrange("p (i j) -> p i j", i=GI)
                part = neg_max[n % 2][:].rearrange("p c (i j) -> p c i j", i=GI)
                dve.wait_ge(max_done, b * GI + GI)
                tt(max_all[n % 2][:], max_key[n % 2][:], own, ALU.max).then_inc(small_step, 1)
                wait(dve, max_turned, b - 1)
                dve.wait_ge(small_step, b * 2 + 1)
                ts(part[:, 0].bitcast(F32R), max_all[n % 2][:], -1.0, None, ALU.mult).then_inc(small_step, 1)
                wait(dve, self_exp_done, b - 1)
                tt(self_arg[n % 2][:].rearrange("p (I j c) -> p I c j", I=HALVES, j=GJ),
                   self_score[:, b].rearrange("p (I c j) -> p I c j", I=HALVES, j=GJ),
                   max_all[n % 2][:].rearrange("p (I c) j -> p I c j", I=HALVES), ALU.subtract).then_inc(self_arg_ready, 1)
                dve.wait_ge(small_step, b * 2 + 2)
                stt(part[:, 1], max_all[n % 2][:], -1.0, part[:, 0], ALU.mult, ALU.subtract).then_inc(max_split, 1)

            def slot(t, k):
                if k - 1 in LATER_SLOT:
                    later_step(LATER_SLOT[k - 1], t - 1)
                if k == SPLIT_SLOT:
                    split_input(t - 1)
                product(t, k)
                split_act(*((t, k - 1) if k else (t - 1, SLOTS - 1)))
                if k == 1:
                    add_experts(t - 1)

            with dve.Fori(1, NT - 1) as t:
                for k in range(SLOTS):
                    slot(t, k)
            for k in range(SLOTS):
                slot(NT - 1, k)
                if k in EARLY_SCORES:
                    b, i = EARLY_SCORES[k]
                    max_group(b, b, i, bank=max_ps)
                    if i == GI - 1:
                        split_max(b, b)
            split_act(NT - 1, SLOTS - 1)
            add_experts(NT - 1)

            def take_second(b, n):
                dve.wait_ge(pv_written, b * GI + GI)
                for j in range(GJ):
                    rows = slice(32 * j, 32 * j + 32)
                    last = nc.vector.tensor_copy(pv_own[n % 2][rows, 1], pv_ps[1][rows, j * S:(j + 1) * S])
                last.then_inc(pv_taken[1], 1)

            def normalise(b, n):
                pv = out_ps[:, 0:H * VROW].rearrange("p (h w) -> p h w", w=VROW)
                dve.wait_ge(pv_turned, b + 1)
                dve.wait_ge(self_exp_done, b + 1)
                tt(denom[n % 2][:], pv[:, :, DH], self_exp[n % 4][:], ALU.add).then_inc(norm_step, 1)
                dve.wait_ge(self_weighted, b + 1)
                tt(numer[n % 2][:], pv[:, :, 0:DH], v_self_w[n % 2][:], ALU.add).then_inc(norm_step, 1)
                dve.wait_ge(norm_step, b * 3 + 2)
                nc.vector.reciprocal(rdenom[n % 2][:], denom[n % 2][:]).then_inc(norm_step, 1)
                dve.wait_ge(norm_step, b * 3 + 3)
                tt(attn[n % 2][:], numer[n % 2][:], rdenom[n % 2][:].unsqueeze(2).to_broadcast([128, H, DH]),
                   ALU.mult).then_inc(attn_done, 1)

            def make_out(b, n):
                dve.wait_ge(x3_loaded[n // 2 % 2], loaded(b, n, 1))
                dve.wait_ge(out_written, b + 1)
                x = x3_nat[n // 2 % 2][:, n % 2]
                tt(x, out_ps[:, 3 * D:4 * D], x, ALU.add).then_inc(out_ready, 1)

            def body(b, n, first=False, s_next=True):
                for i in range(GI):
                    if s_next:
                        max_group(b + 2, n + 2, i)
                    if n >= 2 and i == 0:
                        make_out(b - 2, n - 2)
                    if not first and i == 1:
                        take_second(b - 1, n - 1)
                    if not first and i == 2:
                        normalise(b - 1, n - 1)
                    if isinstance(b, int) and (b, i) in LAST_AUX:
                        later_step(LAST_AUX[b, i], NT - 1)
                    if isinstance(b, int) and (b, i) == LAST_SPLIT:
                        split_input(NT - 1)
                if s_next:
                    split_max(b + 2, n + 2)

            body(0, 0, first=True)
            body(1, 1)
            with dve.Fori(0, B // TB - 1) as g:
                for n in range(2, TB + 2):
                    body(g * TB + n, n)
            for b in range(B - 2, B):
                body(b, b % TB, s_next=b + 2 < B)
            take_second(B - 1, B - 1)
            make_out(B - 2, B - 2)
            normalise(B - 1, B - 1)
            make_out(B - 1, B - 1)

        @block.gpsimd
        def _(pool):
            tt = nc.gpsimd.tensor_tensor

            def over_s(z):
                return z.unsqueeze(2).to_broadcast([z.shape[0], TB, S])

            def make_mix(f, part):
                z = z_all[:, 1, TB * f:TB * f + TB]
                if part == 0:
                    if f:
                        pool.wait_ge(aux_written, aux_of("diffuse", f - 1) + 1)
                    tt(mix[:], lap_t.unsqueeze(1).to_broadcast([128, TB, S]), over_s(z), ALU.mult).then_inc(mix_step, 1)
                elif part == 1:
                    pool.wait_ge(z_ready, 1)
                    tt(mix_own[:], ident.unsqueeze(1).to_broadcast([128, TB, S]), over_s(z_own[:, TB * f:TB * f + TB]),
                       ALU.mult).then_inc(mix_step, 1)
                else:
                    pool.wait_ge(mix_step, 2 * f + 2)
                    tt(mix[:], mix[:], mix_own[:], ALU.add).then_inc(mix_ready, 1)

            def split_part(w):
                pool.wait_ge(w_hi_done, w + 1)
                tt(w_lo[:, w // 3, w % 3], w_raw[w % 3][:], w_hi[:, w // 3, w % 3].bitcast(F32), ALU.subtract)\
                    .then_inc(w_lo_done, 1)

            def gate_x(t, e):
                wait(pool, xg_ready, t * NE + e)
                tt(xg[:], x1[:, t], over_s(gates[:, e, bass.ds(t * TB, TB)]), ALU.mult).then_inc(xg_made, 1)

            def split_xg(t, e):
                pool.wait_ge(xg_rounded, t * NE + e + 1)
                tt(xg_lo[e % 3][:], xg[:].rearrange("p b s -> p (b s)"), xg_hi[e % 3][:].bitcast(F32), ALU.subtract)\
                    .then_inc(xg_ready, 1)

            def multiply_self(f, b):
                m = TB * f + b
                pool.wait_ge(aux_drained, aux_of("natural", f, b) + 1)
                wait(pool, self_summed, m - 1)
                tt(qk_prod[b % 2][:], nat[b % 2][:, 0], nat[b % 2][:, 1], ALU.mult).then_inc(prod_made, 1)

            pool.wait_ge(squares_loaded, 16)
            pool.wait_ge(z_loaded, 16)
            for part in range(3):
                make_mix(0, part)
            split_part(0)
            split_part(1)
            pool.wait_ge(gates_ready, 2)
            split_part(2)
            pool.wait_ge(aux_drained, 1)
            for k in range(SLOTS):
                e, c = divmod(k, FC)
                if e + 1 < NE and c == 1:
                    gate_x(0, e + 1)
                if e + 1 < NE and c == 2:
                    split_xg(0, e + 1)
                if e + 1 < NE and c < 3:
                    split_part(3 * (e + 1) + c)
                for kind, f, b in first_at(k - 1):
                    if kind == "natural":
                        multiply_self(f, b)
                for part in range(3):
                    for kind, f, b in first_at(k + MIX_AHEAD - part):
                        if kind == "diffuse":
                            make_mix(f, part)
            with pool.Fori(1, NT - 1) as t:
                for e in range(NE):
                    gate_x(t, e)
                    split_xg(t, e)
            for e in range(NE):
                gate_x(NT - 1, e)
                split_xg(NT - 1, e)
                for tile, constant, experts in FILLS:
                    if e == min(experts + 2, NE - 1):
                        pool.wait_ge(down_done, SLOTS * (NT - 1) + experts * FC)
                        nc.gpsimd.memset(tile[:].bitcast(F32), constant).then_inc(blocks_filled, 1)

            def place_max(b, n):
                for c in range(2):
                    pool.dma_start(q_blocks[n // 2 % 2][ROW_MAX + c:ROW_MAX + c + 1, :, :, n % 2 * S:(n % 2 + 1) * S]
                                   .rearrange("p i j s -> p (i j) s").bitcast(F32),
                                   max_rows[n % 2][c * H:(c + 1) * H]).then_inc(max_placed[n % 2], 16)

            def weigh_self(b, n, place_next):
                pool.wait_ge(v_loaded[n // 2 % 2], loaded(b, n, 1))
                wait(pool, attn_done, b - 1)
                pool.wait_ge(self_exp_done, b + 1)
                if place_next:
                    pool.wait_ge(max_copied, b + 2)
                tt(v_self_w[n % 2][:], v_self[n // 2 % 2][:, n % 2], self_exp[n % 4][:].unsqueeze(2).to_broadcast([128, H, DH]),
                   ALU.mult).then_inc(self_weighted, 1)

            def body(b, n, turn_next=True):
                weigh_self(b, n, turn_next)
                if turn_next:
                    place_max(b + 1, n + 1)

            pool.wait_ge(max_copied, 1)
            place_max(0, 0)
            pool.wait_ge(down_done, SLOTS * NT)
            for v in v_blocks:
                nc.gpsimd.memset(v[:], 0.0).then_inc(v_zeroed, 1)
            body(0, 0)
            body(1, 1)
            with pool.Fori(0, B // TB - 1) as g:
                for n in range(2, TB + 2):
                    body(g * TB + n, n)
            for b in range(B - 2, B):
                body(b, b % TB, turn_next=b + 1 < B)


def flat_inputs(inputs):
    stacked = {
        "z": ("condB_zX", "condB_zY", "condB_zR"),
        "w_proj": ("L3_cond_Wq", "L3_cond_Wk", "L3_cond_Wv", "L3_cond_Wo"),
        "b_proj": ("L3_cond_bq", "L3_cond_bk", "L3_cond_bv", "L3_cond_bo"),
        "b_in": ("L3_cond_b_self", "L3_cond_b_prev"),
    }
    arrays = {name: laid_out(name, np.asarray(value)) for name, value in inputs.items()}
    for name, parts in stacked.items():
        arrays[name] = np.stack([arrays.pop(part) for part in parts])
    for name in ("z", "b_proj"):
        arrays[name] = arrays[name].reshape(-1)
    arrays["b_in"] = arrays["b_in"].reshape(2, D).T
    return arrays


def shape_constants():
    lap = np.zeros((S, S), np.float32)
    for s in range(S):
        lap[s, s] = -2.0
        lap[abs(s - 1), s] += 1.0
        lap[S - 1 - abs(S - 2 - s), s] += 1.0
    lang_of = np.concatenate([np.arange(LORA_ROWS) // RANK, np.arange(LANGS)]).astype(np.float32)[:, None]
    return {
        "squares": np.stack([np.eye(128, dtype=np.float32), lap]),
        "lang_of": lang_of,
        "key_pos": np.tile(np.arange(S, dtype=np.float32), (B, 1)),
    }


def laid_out(name, value):
    rows = value.shape[:-1]
    if name in ("L3_cond_Wq", "L3_cond_Wk", "L3_cond_bq", "L3_cond_bk"):
        return np.moveaxis(value.reshape(*rows, GI, GJ, DH), -3, -1).reshape(value.shape)
    if name in ("L3_cond_Wv", "L3_cond_bv"):
        return value.reshape(*rows, HALVES, GI // HALVES, GJ, DH).swapaxes(-3, -2).reshape(value.shape)
    if name == "L3_cond_Wo":
        return value.reshape(HALVES, GI // HALVES, GJ, DH, D).swapaxes(1, 2).reshape(value.shape)
    return value


def kernel(**inputs):
    import concourse.bacc as bacc
    from concourse.bass_utils import run_bass_kernel_spmd

    nc = bacc.Bacc("TRN2", target_bir_lowering=False, num_devices=1)
    arrays, args = {}, {}
    for name, value in {**flat_inputs(inputs), **shape_constants()}.items():
        value = np.ascontiguousarray(value)
        arrays[f"in_{name}"] = value
        args[name] = nc.dram_tensor(f"in_{name}", value.shape, mybir.dt.from_np(value.dtype), kind="ExternalInput").ap()
    out = nc.dram_tensor("out", (B, S, D), F32, kind="ExternalOutput").ap()
    build(nc, args, out)
    result = run_bass_kernel_spmd(nc, [arrays], core_ids=[0])
    return result.results[0]["out"]
```
